# Optimizing a Trainium2 kernel written in Bass

```python
import numpy as np
import jax
import jax.numpy as jnp

def _softmax(x, axis=-1):
    return jax.nn.softmax(x, axis=axis)

def _gelu(x):
    return jax.nn.gelu(x, approximate=True)

def _silu(x):
    return jax.nn.silu(x)

def _sigmoid(x):
    return jax.nn.sigmoid(x)

def _layernorm(x, axis=-1, eps=1e-05):
    m = jnp.mean(x, axis=axis, keepdims=True)
    v = jnp.var(x, axis=axis, keepdims=True)
    return (x - m) / jnp.sqrt(v + eps)

def _scatter_add(tgt, idx, src, axis=0):
    return tgt.at[idx].add(src)

def _segment_sum(src, seg, n):
    return jax.ops.segment_sum(src, seg, n)
kernel_name = 'mk_perceiver_d1_seqx_r2_88c904'

def setup_inputs(seed: int=0):
    np.random.seed(seed)
    _w = jnp.asarray

    def _rec_inputs():
        import jax
        import jax.numpy as jnp
        _rk = jax.random.key(seed)
        x = -0.0002928 + 1 * jax.random.normal(jax.random.fold_in(_rk, 1), (32, 32, 512), jnp.float32)
        _lenS = 32 - jax.random.randint(jax.random.fold_in(_rk, 7), (32,), 0, max(1, 32 // 4) + 1, jnp.int32)
        _lenS2 = 257 - jax.random.randint(jax.random.fold_in(_rk, 8), (32,), 0, max(1, 257 // 4) + 1, jnp.int32)
        _ctx_1024P = jax.random.normal(jax.random.fold_in(_rk, 11), (32, 16, 512), jnp.float32)
        _ctx_1024c = jax.random.dirichlet(jax.random.fold_in(_rk, 511), 0.3 * jnp.ones((16,), jnp.float32), (32, 257))
        _ctx_1024t = jnp.einsum('bsk,bkd->bsd', _ctx_1024c, _ctx_1024P)
        _ctx_1024t = _ctx_1024t * jax.lax.rsqrt(jnp.mean(jnp.square(_ctx_1024t)) + 1e-12) * 0.953939
        ctx_1024 = -1.39393e-06 + 0.999914 * (_ctx_1024t + 0.3 * jax.random.normal(jax.random.fold_in(_rk, 611), (32, 257, 512), jnp.float32))
        _validS = jnp.arange(32)[None, :] < _lenS[:, None]
        _validS2 = jnp.arange(257)[None, :] < _lenS2[:, None]
        _causal = jnp.tril(jnp.ones((32, 32), dtype=bool))
        mask_Bx1xS2_ik0 = jnp.where(jnp.broadcast_to(_validS2[:, None, :], (32, 1, 257)), 0, 1).astype(jnp.int32)
        return (x, ctx_1024, mask_Bx1xS2_ik0)
    x, ctx_1024, mask_Bx1xS2_ik0 = _rec_inputs()

    def _L0_xattn_setup():
        import jax, jax.numpy as jnp
        import numpy as np
        B, SQ, SK = (2, 1024, 1024)
        DQ = DK = DV = DM = 512
        H = 16
        DHEAD = DM // H
        key = jax.random.key(seed)
        ks = jax.random.split(key, 12)
        s = 0.02
        return {'Q': jax.random.normal(ks[0], (B, SQ, DQ), jnp.float32), 'K': jax.random.normal(ks[1], (B, SK, DK), jnp.float32), 'V': jax.random.normal(ks[2], (B, SK, DV), jnp.float32), 'mask': jax.random.randint(ks[3], (B, 1, SK), 0, 2, jnp.int32), 'Wq': jax.random.normal(ks[4], (DM, DQ), jnp.float32) * s, 'bq': jnp.zeros((DM,), jnp.float32), 'Wk': jax.random.normal(ks[5], (DM, DK), jnp.float32) * s, 'bk': jnp.zeros((DM,), jnp.float32), 'Wv': jax.random.normal(ks[6], (DM, DV), jnp.float32) * s, 'bv': jnp.zeros((DM,), jnp.float32), 'Wo': jax.random.normal(ks[7], (DQ, DM), jnp.float32) * s, 'bo': jnp.zeros((DQ,), jnp.float32)}
    _L0_xattn_all = _L0_xattn_setup()
    _L0_xattn_in = {k: v for k, v in _L0_xattn_all.items() if k in ('Wq', 'bq', 'Wk', 'bk', 'Wv', 'bv', 'Wo', 'bo')}
    del _L0_xattn_all

    def _L0_attn_setup():
        import jax, jax.numpy as jnp
        import numpy as np
        D = 512
        B, S = (4, 1024)
        key = jax.random.key(seed)
        ks = jax.random.split(key, 4)
        scale = 1.0 / np.sqrt(D)
        return {'x': jax.random.normal(ks[0], (B, S, D), dtype=jnp.float32), 'Wq': jax.random.normal(ks[1], (D, D), dtype=jnp.float32) * scale, 'bq': jnp.zeros((D,), jnp.float32), 'Wk': jax.random.normal(ks[2], (D, D), dtype=jnp.float32) * scale, 'bk': jnp.zeros((D,), jnp.float32), 'Wv': jax.random.normal(ks[3], (D, D), dtype=jnp.float32) * scale, 'bv': jnp.zeros((D,), jnp.float32)}
    _L0_attn_all = _L0_attn_setup()
    _L0_attn_in = {k: v for k, v in _L0_attn_all.items() if k in ('Wq', 'bq', 'Wk', 'bk', 'Wv', 'bv')}
    del _L0_attn_all

    def _L0_ffn_setup():
        import jax, jax.numpy as jnp
        import numpy as np
        NUM_HEADS = 16
        TOP_K = 2
        key = jax.random.key(seed)
        ks = jax.random.split(key, 5)
        B, S, D, E = (4, 1024, 512, 8)
        scale = 0.02
        return {'x': jax.random.normal(ks[0], (B, S, D), dtype=jnp.float32), 'W_qkv': jax.random.normal(ks[1], (D, 3 * D), dtype=jnp.float32) * scale, 'b_qkv': jnp.zeros((3 * D,), dtype=jnp.float32), 'W_gate': jax.random.normal(ks[2], (D, E), dtype=jnp.float32) * scale, 'b_gate': jnp.zeros((E,), dtype=jnp.float32), 'W_experts': jax.random.normal(ks[3], (E, D, D), dtype=jnp.float32) * scale, 'b_experts': jnp.zeros((E, D), dtype=jnp.float32)}
    _L0_ffn_all = _L0_ffn_setup()
    _L0_ffn_in = {k: v for k, v in _L0_ffn_all.items() if k in ('W_qkv', 'b_qkv', 'W_gate', 'b_gate', 'W_experts', 'b_experts')}
    del _L0_ffn_all
    return {'x': x, 'ctx_1024': ctx_1024, 'mask_Bx1xS2_ik0': mask_Bx1xS2_ik0, 'L0_xattn_Wq': _L0_xattn_in['Wq'], 'L0_xattn_bq': _L0_xattn_in['bq'], 'L0_xattn_Wk': _L0_xattn_in['Wk'], 'L0_xattn_bk': _L0_xattn_in['bk'], 'L0_xattn_Wv': _L0_xattn_in['Wv'], 'L0_xattn_bv': _L0_xattn_in['bv'], 'L0_xattn_Wo': _L0_xattn_in['Wo'], 'L0_xattn_bo': _L0_xattn_in['bo'], 'L0_attn_Wq': _L0_attn_in['Wq'], 'L0_attn_bq': _L0_attn_in['bq'], 'L0_attn_Wk': _L0_attn_in['Wk'], 'L0_attn_bk': _L0_attn_in['bk'], 'L0_attn_Wv': _L0_attn_in['Wv'], 'L0_attn_bv': _L0_attn_in['bv'], 'L0_ffn_W_qkv': _L0_ffn_in['W_qkv'], 'L0_ffn_b_qkv': _L0_ffn_in['b_qkv'], 'L0_ffn_W_gate': _L0_ffn_in['W_gate'], 'L0_ffn_b_gate': _L0_ffn_in['b_gate'], 'L0_ffn_W_experts': _L0_ffn_in['W_experts'], 'L0_ffn_b_experts': _L0_ffn_in['b_experts']}

def reference(x, ctx_1024, mask_Bx1xS2_ik0, L0_xattn_Wq, L0_xattn_bq, L0_xattn_Wk, L0_xattn_bk, L0_xattn_Wv, L0_xattn_bv, L0_xattn_Wo, L0_xattn_bo, L0_attn_Wq, L0_attn_bq, L0_attn_Wk, L0_attn_bk, L0_attn_Wv, L0_attn_bv, L0_ffn_W_qkv, L0_ffn_b_qkv, L0_ffn_W_gate, L0_ffn_b_gate, L0_ffn_W_experts, L0_ffn_b_experts):
    import jax
    import jax.numpy as jnp

    def _L0_xattn_ref(Q, K, V, mask, Wq, bq, Wk, bk, Wv, bv, Wo, bo):
        import jax, jax.numpy as jnp
        import numpy as np
        B, SQ, SK = (2, 1024, 1024)
        DQ = DK = DV = DM = 512
        H = 16
        DHEAD = DM // H
        b, sq, _ = Q.shape
        q = Q @ Wq.T + bq
        k = K @ Wk.T + bk
        v = V @ Wv.T + bv
        q = q.reshape(b, sq, H, DHEAD).transpose(0, 2, 1, 3)
        k = k.reshape(b, -1, H, DHEAD).transpose(0, 2, 1, 3)
        v = v.reshape(b, -1, H, DHEAD).transpose(0, 2, 1, 3)
        scores = jnp.einsum('bhqd,bhkd->bhqk', q, k) / np.sqrt(DHEAD).astype(np.float32)
        m = mask[:, None, :, :]
        scores = jnp.where(m == 0, -jnp.inf, scores)
        attn = jax.nn.softmax(scores, axis=-1)
        out = jnp.einsum('bhqk,bhkd->bhqd', attn, v)
        out = out.transpose(0, 2, 1, 3).reshape(b, sq, DM)
        return out @ Wo.T + bo

    def _L0_attn_ref(x, Wq, bq, Wk, bk, Wv, bv):
        import jax, jax.numpy as jnp
        import numpy as np
        D = 512
        B, S = (4, 1024)
        Q = jnp.einsum('bsd,ed->bse', x, Wq) + bq
        K = jnp.einsum('bsd,ed->bse', x, Wk) + bk
        V = jnp.einsum('bsd,ed->bse', x, Wv) + bv
        dk = K.shape[1]
        logits = jnp.einsum('bqd,bkd->bqk', Q, K) / jnp.sqrt(jnp.asarray(dk, Q.dtype))
        att = jax.nn.softmax(logits, axis=-1)
        return jnp.einsum('bqk,bkd->bqd', att, V)

    def _L0_ffn_ref(x, W_qkv, b_qkv, W_gate, b_gate, W_experts, b_experts):
        import jax, jax.numpy as jnp
        import numpy as np
        NUM_HEADS = 16
        TOP_K = 2
        B, S, D = x.shape
        H = NUM_HEADS
        hd = D // H
        E = W_gate.shape[-1]
        qkv = (x @ W_qkv + b_qkv).reshape(B, S, 3, H, hd)
        q, k, v = (qkv[:, :, 0], qkv[:, :, 1], qkv[:, :, 2])
        attn = jnp.einsum('bqhd,bkhd->bhqk', q, k) / jnp.sqrt(jnp.asarray(hd, x.dtype))
        attn = jax.nn.softmax(attn, axis=-1)
        attn_out = jnp.einsum('bhqk,bkhd->bqhd', attn, v).reshape(B, S, D)
        gate = jax.nn.softmax(x @ W_gate + b_gate, axis=-1)
        top_g, top_i = jax.lax.top_k(gate, TOP_K)
        combine = jnp.sum(jax.nn.one_hot(top_i, E, dtype=x.dtype) * top_g[..., None], axis=2)
        expert_out = jnp.einsum('bsd,edf->bsef', x, W_experts) + b_experts
        moe_out = jnp.einsum('bsef,bse->bsf', expert_out, combine)
        return attn_out + moe_out
    x = x + _L0_xattn_ref(_layernorm(x, axis=-1), ctx_1024, ctx_1024, mask_Bx1xS2_ik0, L0_xattn_Wq, L0_xattn_bq, L0_xattn_Wk, L0_xattn_bk, L0_xattn_Wv, L0_xattn_bv, L0_xattn_Wo, L0_xattn_bo)
    x = x + _L0_attn_ref(_layernorm(x, axis=-1), L0_attn_Wq, L0_attn_bq, L0_attn_Wk, L0_attn_bk, L0_attn_Wv, L0_attn_bv)
    x = x + _L0_ffn_ref(_layernorm(x, axis=-1), L0_ffn_W_qkv, L0_ffn_b_qkv, L0_ffn_W_gate, L0_ffn_b_gate, L0_ffn_W_experts, L0_ffn_b_experts)
    return x

_drawn_inputs = setup_inputs


def setup_inputs(seed=0):
    import zlib

    import numpy as np

    out = dict(_drawn_inputs(seed))
    spreads = {'L0_xattn_bq': (0.0, 0.8),
     'L0_xattn_bk': (0.0, 0.8),
     'L0_xattn_bv': (0.0, 0.1),
     'L0_xattn_bo': (0.0, 0.1),
     'L0_attn_bq': (0.0, 0.1),
     'L0_attn_bk': (0.0, 0.8),
     'L0_attn_bv': (0.0, 0.1),
     'L0_ffn_b_qkv': (0.0, 0.1),
     'L0_ffn_b_gate': (0.0, 0.1),
     'L0_ffn_b_experts': (0.0, 0.363)}
    factors = {'L0_xattn_Wq': 2.844, 'L0_xattn_Wk': 2.744}
    for name, (base, spread) in spreads.items():
        noise = np.random.default_rng([zlib.crc32(name.encode()), seed]).standard_normal(out[name].shape)
        drawn = base * np.exp(spread * noise) if base else spread * noise
        out[name] = jnp.asarray(drawn.astype(out[name].dtype))
    for name, factor in factors.items():
        out[name] = (out[name] * factor).astype(out[name].dtype)
    return out
```

```python
from contextlib import ExitStack

import numpy as np

import concourse.bass as bass
from concourse import mybir

F32 = mybir.dt.float32
F32R = mybir.dt.float32r
BF16 = mybir.dt.bfloat16
I32 = mybir.dt.int32
ALU = mybir.AluOpType
ACT = mybir.ActivationFunctionType
AX = mybir.AxisListType

B, S, SK, D, H, E = 32, 32, 257, 512, 16, 8
P = 128
TOK = B * S
NT = TOK // P
KC = D // P
DH = D // H
HG = P // DH
CK = 64
NCH = -(-SK // CK)
PAD = NCH * CK - SK
TAIL = SK - CK
NPAIR = B // 2
NQ = 4
SCALE = float(DH) ** -0.5
ATTN_SCALE = float(S) ** -0.5
EPS = 1e-5
MASKED = -1.0e30

KB = 1024
NW = 18
NSLOT = 3


def perceiver_kernel(nc, x_d, ctx_tail_d, ctx_all_d, mask_d, mask_tail_d, mask_all_d, w_d, bias_col_d,
                     bias_row_d, w_gate_d, b_gate_d, b_exp_d, ident_d, head_on_d, out_d):
    ctx = ExitStack()
    with ctx:
        base = -(-nc.sbuf_base // 64) * 64
        arena = ctx.enter_context(nc.sbuf_tensor("arena", [P, 208 * KB - 256], mybir.dt.uint8))
        del arena

        def sb(name, kb, shape, dt=F32):
            return nc.alloc_sbuf_tensor_at(name, shape, dt, offset=base + int(kb * KB))

        w_stage = sb("w_stage", 0, [P, KC, D])
        w_hi = sb("w_hi", 8, [P, NSLOT, KC, D], F32R)
        w_lo = sb("w_lo", 32, [P, NSLOT, KC, D], F32R)
        x = sb("x", 56, [P, NT, D])
        xt_hi = sb("xt_hi", 72, [P, KC, TOK], F32R)
        xt_lo = sb("xt_lo", 88, [P, KC, TOK], F32R)
        o_t = sb("o_t", 88, [P, KC, TOK])
        q_t = sb("q_t", 104, [P, KC, TOK])
        k_t = sb("k_t", 120, [P, KC, TOK])
        kq_t = sb("kq_t", 120, [P, KC, 512])
        s_rows = sb("s_rows", 128, [P, 2, 512])
        p_rows = sb("p_rows", 132, [P, 2, 512])
        v_n = sb("v_n", 136, [P, NT, D])
        vq_n = sb("vq_n", 136, [P, 4, D])
        pt_x = sb("pt_x", 144, [P, 2, 512])
        bias_x = sb("bias_x", 148, [P, 2, D])
        c_hi = sb("c_hi", 152, [P, 2, KC, 512], F32R)
        c_lo = sb("c_lo", 168, [P, 2, KC, 512], F32R)
        c_stage = sb("c_stage", 184, [P, KC, 512])
        mask_i = sb("mask_i", 184, [P, B * CK], I32)
        q_bd = sb("q_bd", 192, [P, 2, 2, KC, P])
        m_bias = sb("m_bias", 200, [P, B * CK], BF16)
        bias_f = sb("bias_f", 200, [P, 2, D])
        ident = sb("ident", 204, [P, P])
        bias_col = sb("bias_col", 204.5, [P, 6, KC])
        stats = sb("stats", 204.625, [P, NT, 6])
        aggr = sb("aggr", 204.875, [P, NT, 2])
        rstd = sb("rstd", 205, [P, 2, NT])
        power = sb("power", 205.0625, [P, 1])
        row_max = sb("row_max", 205.125, [P, 2, 16])
        row_sum = sb("row_sum", 205.25, [P, 2, 16])
        row_inv = sb("row_inv", 205.375, [P, 2, 16])
        nan_b = sb("nan_b", 205.5, [P, 3, B])
        flag_i = sb("flag_i", 206, [1, 1], I32)
        ones = sb("ones", 206.0625, [P, 1])
        any_col = sb("any_col", 206.125, [P, 1])
        b_gate = sb("b_gate", 206.1875, [P, E])
        head_on = sb("head_on", 206.25, [P, HG])
        mask_nat = sb("mask_nat", 144, [B, SK], I32)
        mask_on = sb("mask_on", 146, [B, TAIL])
        g_ctx = sb("g_ctx", 184, [P, KC, P])
        g_mask = sb("g_mask", 186, [P, NCH, P], I32)
        g_bias = sb("g_bias", 189, [P, NCH, P])
        g_chi = sb("g_chi", 128, [P, KC, P], F32R)
        g_clo = sb("g_clo", 130, [P, KC, P], F32R)
        g_k = sb("g_k", 120, [P, KC, P])
        g_s = sb("g_s", 152, [P, NCH, 512])
        g_pt = sb("g_pt", 162, [P, NCH, 512])
        g_v = sb("g_v", 172, [P, NCH, D])
        xn_0 = sb("xn_0", 144, [P, 2, D])
        xn_1 = sb("xn_1", 152, [P, 2, D])
        a_s = sb("a_s", 156, [P, NT, S])
        a_p = sb("a_p", 157, [P, NT, S])
        a_pt = sb("a_pt", 158, [P, NT, P])
        f_s = sb("f_s", 162, [P, H, S])
        f_p = sb("f_p", 164, [P, H, S])
        f_pt = sb("f_pt", 166, [P, H, P])
        gate = sb("gate", 174, [P, NT, E])
        gate_x = sb("gate_x", 174.25, [P, NT, 16])
        gate_r = sb("gate_r", 174.75, [P, NT, 16])
        top = sb("top", 175.25, [P, NT, 8])
        top2 = sb("top2", 175.5, [P, NT, 8])
        comb = sb("comb", 175.75, [P, NT, E])
        comb_t = sb("comb_t", 176, [E, TOK])
        b_exp = sb("b_exp", 180, [E, D])
        g_stage = sb("g_stage", 182, [P, KC, E])
        wg_hi = sb("wg_hi", 182.125, [P, KC, E], F32R)
        wg_lo = sb("wg_lo", 182.25, [P, KC, E], F32R)

        bank = [ctx.enter_context(nc.psum_tensor(f"bank{i}", [P, 512], F32)) for i in range(8)]

        names = """x_in ident_in bias_in biasx_in biasf_in mask_in masknat_in maskn_done gate_in bexp_in
            w_in w_hi_done w_lo_done c_in c_hi_done c_lo_done
            g_hi pow_set stats_done aggr_done eps_done rstd_done xn_done tr_done xt_hi_done xt_lo_done
            t_mm t_ev n_mm n_ev
            flag_sum flag_mm flag_done mbias_done ones_set xb_done pt_zeroed gx_set
            qbd_done s_mm s_add s_max s_sub exp_done s_sum s_inv p_done pt_mm pt_ev o_mm o_act o_dve
            o_hi o_lo
            a_mm a_ext a_max a_sub a_exp a_sum a_inv a_norm a_tr av_mm x_acc
            gate_mm gate_v gate_exp comb_done combt_mm combt_ev be_mm be_chain wg_split
            f_mm f_act f_dve f_max f_sub f_exp f_sum f_inv f_norm f_tr fv_mm
            g_c_in g_m_in g_pe g_act g_dve g_pool g_q g_b done_out""".split()
        sem = {n: ctx.enter_context(nc.semaphore(n)) for n in names}

        ACC = [("xo", t) for t in range(NT)] + [("av", t) for t in range(NT)] + [("be", t) for t in range(NT)]
        for e in range(E):
            ACC += [("ex", e, t) for t in range(NT)] + [("fv", e)]
        ACC_AT = {a: i + 1 for i, a in enumerate(ACC)}
        X_FINAL = [max(ACC_AT[("ex", E - 1, t)], ACC_AT[("fv", t)]) for t in range(NT)]

        def last_acc(i):
            t = ACC[i][-1]
            return max(j + 1 for j in range(i) if ACC[j][-1] == t)

        (W_XQ, W_XK, W_XV, W_XO, W_AQ, W_AK, W_AV, W_FQ, W_FK, W_FV, W_EX) = range(11)

        G_XQ, G_XKV, G_XO, G_AQ, G_AK, G_AV, G_FQ, G_FK, G_FV, G_EX = 0, 8, 40, 48, 56, 64, 72, 80, 88, 96
        XQ_T, XK_T, AQ_T, AK_T, FQ_T, FK_T = 0, 8, 24, 32, 40, 48
        XV_N, XO_N, AV_N, FV_N, EX_N = 0, 16, 24, 32, 40
        XV_EV, AV_EV, FV_EV = 0, 16, 24

        freed = [("t_ev", XQ_T + j + 1) for j in range(8)]
        for q in range(NQ):
            freed += [("t_ev", XK_T + 4 * q + j + 1) for j in range(4)] + [("n_ev", XV_EV + 4 * q + j + 1) for j in range(4)]
        freed += [("x_acc", ACC_AT["xo", t]) for t in range(NT)]
        freed += [("t_ev", AQ_T + j + 1) for j in range(16)] + [("n_ev", AV_EV + t + 1) for t in range(NT)]
        freed += [("t_ev", FQ_T + j + 1) for j in range(16)] + [("n_ev", FV_EV + t + 1) for t in range(NT)]
        freed += [("x_acc", ACC_AT["ex", e, t]) for e in range(E) for t in range(NT)]

        def evacuated(eng, g):
            if g >= 4:
                name, value = freed[g - 4]
                eng.wait_ge(sem[name], value)

        W_USED = [("t_mm", XQ_T + 8), ("t_mm", XK_T + 16), ("n_mm", XV_N + 16), ("n_mm", XO_N + 8),
                  ("t_mm", AQ_T + 8), ("t_mm", AK_T + 8), ("n_mm", AV_N + 8), ("t_mm", FQ_T + 8),
                  ("t_mm", FK_T + 8), ("n_mm", FV_N + 8)] + [("n_mm", EX_N + 8 * (e + 1)) for e in range(E)]

        def take_out(eng, n):
            b = 0 if eng.engine == nc.scalar.engine else 1
            src = bank[(6 if n % 2 == 0 else 2) + b]
            eng.wait_ge(sem["o_mm"], n + 1)
            for h in range(HG):
                rows = slice(h * DH, (h + 1) * DH)
                dst = o_t[rows, :, n * 2 * S + b * S:n * 2 * S + (b + 1) * S]
                blk = src[rows, :].rearrange("p (g n) -> p g n", g=KC)[:, :, h * S:(h + 1) * S]
                if b == 0:
                    ins = nc.scalar.activation(dst, blk, ACT.Copy)
                else:
                    ins = nc.vector.tensor_copy(dst, blk)
            ins.then_inc(sem["o_act" if b == 0 else "o_dve"], 1)

        block = ctx.enter_context(nc.Block())

        @block.sync
        def _(sp):
            for t in range(NT):
                sp.dma_start(x[:, t, :], x_d[t * P:(t + 1) * P, :]).then_inc(sem["x_in"], 16)
                if t == 0:
                    sp.dma_start(ident[:], ident_d).then_inc(sem["ident_in"], 16)
            sp.dma_start(mask_nat[:], mask_d).then_inc(sem["masknat_in"], 16)
            sp.dma_start(w_stage[:], w_d[0]).then_inc(sem["w_in"], 16)
            sp.dma_start(bias_col[:], bias_col_d).then_inc(sem["bias_in"], 16)
            sp.dma_start(head_on[:], head_on_d).then_inc(sem["bias_in"], 16)
            sp.dma_start(mask_i[:], mask_tail_d.broadcast_to([P, B * CK])).then_inc(sem["mask_in"], 16)
            sp.dma_start(bias_x[:], bias_row_d[0:1, 0:2, :].broadcast_to([P, 2, D])).then_inc(sem["biasx_in"], 16)
            sp.dma_start(b_gate[:], b_gate_d.broadcast_to([P, E])).then_inc(sem["gate_in"], 16)

            def load_w(n):
                sp.wait_ge(sem["w_lo_done"], n)
                sp.dma_start(w_stage[:], w_d[n]).then_inc(sem["w_in"], 16)

            def load_c(q):
                if q == 0:
                    sp.wait_ge(sem["mbias_done"], 1)
                sp.wait_ge(sem["c_lo_done"], q)
                sp.dma_start(c_stage[:], ctx_tail_d[q]).then_inc(sem["c_in"], 16)

            load_w(W_XK)
            load_c(0)
            load_w(W_XV)
            sp.wait_ge(sem["flag_done"], 1)
            general = sp.value_load(flag_i[0:1, 0:1], min_val=0, max_val=1)
            with sp.If(general == 0):
                for q in range(1, NQ):
                    load_c(q)
            with sp.Else():
                sp.wait_ge(sem["c_in"], 16)
                with sp.Fori(0, NPAIR) as i:
                    sp.wait_ge(sem["g_dve"], i * (NCH + 1))
                    sp.dma_start(g_mask[:], mask_all_d[bass.ds(i, 1), :].broadcast_to([P, NCH * P])).then_inc(sem["g_m_in"], 16)
                    for c in range(NCH):
                        sp.wait_ge(sem["g_b"], i * NCH + c)
                        sp.dma_start(g_ctx[:], ctx_all_d[bass.ds(i * NCH + c, 1)]).then_inc(sem["g_c_in"], 16)
            sp.end_ifs()
            load_w(W_XO)
            load_w(W_AQ)
            sp.wait_ge(sem["o_lo"], NQ)
            sp.dma_start(bias_f[:], bias_row_d[0:1, 2:4, :].broadcast_to([P, 2, D])).then_inc(sem["biasf_in"], 16)
            sp.dma_start(g_stage[:], w_gate_d).then_inc(sem["gate_in"], 16)
            sp.dma_start(b_exp[:], b_exp_d).then_inc(sem["bexp_in"], 16)
            for n in range(W_AQ + 1, NW):
                load_w(n)
            for t in range(NT):
                sp.wait_ge(sem["x_acc"], X_FINAL[t])
                sp.dma_start(out_d[t * P:(t + 1) * P, :], x[:, t, :]).then_inc(sem["done_out"], 16)
            sp.wait_ge(sem["done_out"], 16 * NT)

        @block.tensor
        def _(pe):
            def transposes(s):
                xn = xn_0 if s == 0 else xn_1
                for t in range(NT):
                    n = s * NT + t
                    pe.wait_ge(sem["xn_done"], n + 1)
                    if t >= 2:
                        pe.wait_ge(sem["xt_lo_done"], n - 1)
                    for c in range(KC):
                        mm = pe.transpose(bank[4 + t % 2][:, c * P:(c + 1) * P], xn[:, t % 2, c * P:(c + 1) * P], ident[:])
                    mm.then_inc(sem["tr_done"], 1)

            def three_passes(out, l_hi, l_lo, r_hi, r_lo):
                for c in range(KC):
                    pe.matmul(out, l_hi(c), r_hi(c), start=(c == 0), stop=False)
                    pe.matmul(out, l_hi(c), r_lo(c), start=False, stop=False)
                    mm = pe.matmul(out, l_lo(c), r_hi(c), start=False, stop=(c == KC - 1))
                return mm

            def weight_ready(n):
                pe.wait_ge(sem["w_lo_done"], n + 1)

            def product_t(w, g0):
                weight_ready(w)
                k = w % NSLOT
                for j in range(8):
                    m, half = j % 4, j // 4
                    evacuated(pe, g0 + j)
                    mm = three_passes(bank[(g0 + j) % 4][:],
                                      lambda c: w_hi[:, k, c, m * P:(m + 1) * P], lambda c: w_lo[:, k, c, m * P:(m + 1) * P],
                                      lambda c: xt_hi[:, c, half * 512:(half + 1) * 512], lambda c: xt_lo[:, c, half * 512:(half + 1) * 512])
                    mm.then_inc(sem["t_mm"], 1)

            def product_n(w, g0):
                weight_ready(w)
                k = w % NSLOT
                for t in range(NT):
                    evacuated(pe, g0 + t)
                    mm = three_passes(bank[(g0 + t) % 4][:],
                                      lambda c: xt_hi[:, c, t * P:(t + 1) * P], lambda c: xt_lo[:, c, t * P:(t + 1) * P],
                                      lambda c: w_hi[:, k, c, :], lambda c: w_lo[:, k, c, :])
                    mm.then_inc(sem["n_mm"], 1)

            pe.wait_ge(sem["ident_in"], 16)
            pe.wait_ge(sem["flag_sum"], 1)
            pe.matmul(bank[6][0:1, 0:1], any_col[0:B, :], ones[0:B, :], start=True, stop=True).then_inc(sem["flag_mm"], 1)
            transposes(0)
            pe.wait_ge(sem["xt_lo_done"], NT)
            product_t(W_XQ, G_XQ)
            weight_ready(W_XV)
            kx, vx = W_XK % NSLOT, W_XV % NSLOT

            pe.wait_ge(sem["flag_done"], 1)
            general = pe.value_load(flag_i[0:1, 0:1], min_val=0, max_val=1)
            with pe.If(general == 0):
                for q in range(NQ):
                    u, g0 = q % 2, G_XKV + 8 * q
                    pe.wait_ge(sem["c_lo_done"], q + 1)
                    for m in range(KC):
                        evacuated(pe, g0 + m)
                        if q >= 1 and m >= 2:
                            pe.wait_ge(sem["o_act"], 4 * q)
                            pe.wait_ge(sem["o_dve"], 4 * q)
                        mm = three_passes(bank[m][:],
                                          lambda c: w_hi[:, kx, c, m * P:(m + 1) * P], lambda c: w_lo[:, kx, c, m * P:(m + 1) * P],
                                          lambda c: c_hi[:, u, c, :], lambda c: c_lo[:, u, c, :])
                        mm.then_inc(sem["t_mm"], 1)

                    def value_rows(p):
                        evacuated(pe, g0 + 4 + p)
                        mm = three_passes(bank[p][:],
                                          lambda c: c_hi[:, u, c, p * P:(p + 1) * P], lambda c: c_lo[:, u, c, p * P:(p + 1) * P],
                                          lambda c: w_hi[:, vx, c, :], lambda c: w_lo[:, vx, c, :])
                        mm.then_inc(sem["n_mm"], 1)

                    value_rows(0)
                    for p in range(4):
                        n = 4 * q + p
                        pe.wait_ge(sem["t_ev"], XK_T + 4 * (q + 1))
                        pe.wait_ge(sem["qbd_done"], n + 1)
                        if p >= 2:
                            pe.wait_ge(sem["s_add"], n - 1)
                        elif q >= 1:
                            pe.wait_ge(sem["pt_ev"], 4 * q)
                        for b in range(2):
                            for g in range(KC):
                                mm = pe.matmul(bank[4 + p % 2][:, g * P + b * CK:g * P + (b + 1) * CK], q_bd[:, n % 2, b, g, :],
                                               kq_t[:, g, p * P + b * CK:p * P + (b + 1) * CK], start=True, stop=True)
                        mm.then_inc(sem["s_mm"], 1)
                        if p >= 1:
                            value_rows(p)
                    for p in range(4):
                        n = 4 * q + p
                        pe.wait_ge(sem["p_done"], n + 1)
                        pe.wait_ge(sem["s_add"], 4 * (q + 1))
                        if p >= 2:
                            pe.wait_ge(sem["pt_ev"], n - 1)
                        for g in range(KC):
                            mm = pe.transpose(bank[4 + p % 2][:, g * P:(g + 1) * P], p_rows[:, n % 2, g * P:(g + 1) * P], ident[:])
                        mm.then_inc(sem["pt_mm"], 1)
                        pe.wait_ge(sem["pt_ev"], n + 1)
                        pe.wait_ge(sem["n_ev"], XV_EV + 4 * (q + 1))
                        if p >= 2:
                            pe.wait_ge(sem["o_act"], n - 1)
                            pe.wait_ge(sem["o_dve"], n - 1)
                        elif q >= 1 and p == 0:
                            pe.wait_ge(sem["o_act"], 4 * q)
                            pe.wait_ge(sem["o_dve"], 4 * q)
                        for b in range(2):
                            dst = bank[(6 if p % 2 == 0 else 2) + b]
                            for g in range(KC):
                                mm = pe.matmul(dst[:, g * P:(g + 1) * P], vq_n[b * CK:(b + 1) * CK, p, g * P:(g + 1) * P],
                                               pt_x[b * CK:(b + 1) * CK, n % 2, g * P:(g + 1) * P], start=True, stop=True)
                        mm.then_inc(sem["o_mm"], 1)
            with pe.Else():
                with pe.Fori(0, NPAIR) as i:
                    for c in range(NCH):
                        pe.wait_ge(sem["g_b"], i * NCH + c + 1)
                        if c == 0:
                            pe.wait_ge(sem["g_act"], i * (3 * NCH + 1))
                            pe.wait_ge(sem["g_dve"], i * (NCH + 1))
                        else:
                            pe.wait_ge(sem["g_dve"], i * (NCH + 1) + c)
                        for m in range(KC):
                            mm = three_passes(bank[0][:, m * P:(m + 1) * P],
                                              lambda k: w_hi[:, kx, k, m * P:(m + 1) * P], lambda k: w_lo[:, kx, k, m * P:(m + 1) * P],
                                              lambda k: g_chi[:, k, :], lambda k: g_clo[:, k, :])
                        mm.then_inc(sem["g_pe"], 1)
                        mm = three_passes(bank[1][:], lambda k: g_chi[:, k, :], lambda k: g_clo[:, k, :],
                                          lambda k: w_hi[:, vx, k, :], lambda k: w_lo[:, vx, k, :])
                        mm.then_inc(sem["g_pe"], 1)
                        pe.wait_ge(sem["g_act"], i * (3 * NCH + 1) + c + 1)
                        pe.wait_ge(sem["g_q"], i + 1)
                        for b in range(2):
                            for g in range(KC):
                                mm = pe.matmul(bank[4][:, g * P + b * CK:g * P + (b + 1) * CK], q_bd[:, 0, b, g, :],
                                               g_k[:, g, b * CK:(b + 1) * CK], start=True, stop=True)
                        mm.then_inc(sem["g_pe"], 1)
                    pe.wait_ge(sem["g_pool"], i + 1)
                    for c in range(NCH):
                        pe.wait_ge(sem["g_act"], i * (3 * NCH + 1) + NCH + 1 + c)
                        for g in range(KC):
                            mm = pe.transpose(bank[5][:, g * P:(g + 1) * P], g_s[:, c, g * P:(g + 1) * P], ident[:])
                        mm.then_inc(sem["g_pe"], 1)
                    pe.wait_ge(sem["g_act"], i * (3 * NCH + 1) + 2 * NCH + 1)
                    for b in range(2):
                        for g in range(KC):
                            for c in range(NCH):
                                mm = pe.matmul(bank[6 + b][:, g * P:(g + 1) * P], g_v[b * CK:(b + 1) * CK, c, g * P:(g + 1) * P],
                                               g_pt[b * CK:(b + 1) * CK, c, g * P:(g + 1) * P], start=(c == 0), stop=(c == NCH - 1))
                    mm.then_inc(sem["g_pe"], 1)
                pe.drain().then_inc(sem["t_mm"], 4 * NQ)
                pe.drain().then_inc(sem["n_mm"], 4 * NQ)
            pe.end_ifs()
            pe.wait_ge(sem["o_lo"], NQ)
            product_n(W_XO, G_XO)

            transposes(1)
            pe.wait_ge(sem["xt_lo_done"], 2 * NT)
            product_t(W_AQ, G_AQ)
            product_t(W_AK, G_AK)
            pe.wait_ge(sem["t_ev"], AK_T + 8)
            for t in range(NT):
                for c in range(KC):
                    mm = pe.matmul(bank[4 + t // 4][:, t % 4 * P:(t % 4 + 1) * P], q_t[:, c, t * P:(t + 1) * P],
                                   k_t[:, c, t * P:(t + 1) * P], start=(c == 0), stop=(c == KC - 1))
                if t % 4 == 3:
                    mm.then_inc(sem["a_mm"], 1)
            product_n(W_AV, G_AV)
            pe.wait_ge(sem["a_tr"], 4)
            pe.wait_ge(sem["n_ev"], AV_EV + 8)
            for t in range(NT):
                if t >= 4:
                    pe.wait_ge(sem["x_acc"], ACC_AT[("av", t - 4)])
                pe.matmul(bank[4 + t % 4][:], a_pt[:, t, :], v_n[:, t, :], start=True, stop=True).then_inc(sem["av_mm"], 1)

            pe.wait_ge(sem["x_acc"], ACC_AT[("av", 5)])
            transposes(2)
            pe.wait_ge(sem["xt_lo_done"], 3 * NT)
            pe.wait_ge(sem["wg_split"], 2)
            for t in range(NT):
                out = bank[6][:, t * E:(t + 1) * E]
                for c in range(KC):
                    ts = slice(t * P, (t + 1) * P)
                    pe.matmul(out, xt_hi[:, c, ts], wg_hi[:, c, :], start=(c == 0), stop=False)
                    pe.matmul(out, xt_hi[:, c, ts], wg_lo[:, c, :], start=False, stop=False)
                    mm = pe.matmul(out, xt_lo[:, c, ts], wg_hi[:, c, :], start=False, stop=(c == KC - 1))
            mm.then_inc(sem["gate_mm"], 1)
            product_t(W_FQ, G_FQ)
            pe.wait_ge(sem["comb_done"], 1)
            for t in range(NT):
                mm = pe.transpose(bank[4 + t // 4][0:E, t % 4 * P:(t % 4 + 1) * P], comb[:, t, :], ident[:])
            mm.then_inc(sem["combt_mm"], 1)
            product_t(W_FK, G_FK)
            pe.wait_ge(sem["combt_ev"], 2)
            pe.wait_ge(sem["bexp_in"], 16)
            for t in range(NT):
                if t >= 4:
                    pe.wait_ge(sem["x_acc"], ACC_AT[("be", t - 4)])
                pe.matmul(bank[4 + t % 4][:], comb_t[:, t * P:(t + 1) * P], b_exp[:], start=True, stop=True).then_inc(sem["be_mm"], 1)
            product_n(W_FV, G_FV)
            pe.wait_ge(sem["t_ev"], FK_T + 8)
            pe.wait_ge(sem["x_acc"], ACC_AT[("be", NT - 1)])
            for e in range(E):
                if e >= 1:
                    pe.wait_ge(sem["x_acc"], ACC_AT[("fv", e - 1)])
                for g in range(KC):
                    for h in range(HG):
                        rows = slice(h * DH, (h + 1) * DH)
                        mm = pe.matmul(bank[4 + h][:, g * P:(g + 1) * P], q_t[rows, g, e * P:(e + 1) * P],
                                       k_t[rows, g, e * P:(e + 1) * P], start=True, stop=True)
                mm.then_inc(sem["f_mm"], 1)
                product_n(W_EX + e, G_EX + 8 * e)
                pe.wait_ge(sem["f_tr"], 4 * (e + 1))
                pe.wait_ge(sem["n_ev"], FV_EV + 8)
                for hd in range(H):
                    g, h = hd // HG, hd % HG
                    mm = pe.matmul(bank[4][:, hd * DH:(hd + 1) * DH], f_pt[:, hd, :],
                                   v_n[:, e, hd * DH:(hd + 1) * DH], start=True, stop=True)
                mm.then_inc(sem["fv_mm"], 1)

        @block.scalar
        def _(act):
            def split_w(n):
                act.wait_ge(sem["w_in"], 16 * (n + 1))
                if n >= NSLOT:
                    name, value = W_USED[n - NSLOT]
                    act.wait_ge(sem[name], value)
                act.activation(w_hi[:, n % NSLOT], w_stage[:], ACT.Copy).then_inc(sem["w_hi_done"], 1)

            def split_c(q):
                act.wait_ge(sem["c_in"], 16 * (q + 1))
                if q >= 2:
                    act.wait_ge(sem["n_mm"], XV_N + 4 * (q - 1))
                act.activation(c_hi[:, q % 2], c_stage[:], ACT.Copy).then_inc(sem["c_hi_done"], 1)

            def turned_hi(s):
                for t in range(NT):
                    act.wait_ge(sem["tr_done"], s * NT + t + 1)
                    if t == 0 and s >= 1:
                        act.wait_ge(sem["n_mm"], {1: XO_N, 2: AV_N}[s] + 8)
                    act.activation(xt_hi[:, :, t * P:(t + 1) * P], bank[4 + t % 2][:].rearrange("p (c n) -> p c n", c=KC),
                                   ACT.Copy).then_inc(sem["xt_hi_done"], 1)

            def out_t(dst, b, g0, t0):
                for j in range(8):
                    m, half = j % 4, j // 4
                    act.wait_ge(sem["t_mm"], t0 + j + 1)
                    act.activation(dst[:, m, half * 512:(half + 1) * 512], bank[(g0 + j) % 4][:], ACT.Identity,
                                   bias=bias_col[:, b, m:m + 1]).then_inc(sem["t_ev"], 1)

            def turned_probabilities(n):
                act.wait_ge(sem["pt_mm"], n + 1)
                if n >= 2:
                    act.wait_ge(sem["o_mm"], n - 1)
                act.activation(pt_x[:, n % 2, :], bank[4 + n % 2][:], ACT.Copy).then_inc(sem["pt_ev"], 1)

            split_w(W_XQ)
            turned_hi(0)
            split_w(W_XK)
            act.wait_ge(sem["bias_in"], 32)
            split_w(W_XV)
            out_t(q_t, 0, G_XQ, XQ_T)
            act.wait_ge(sem["flag_done"], 1)
            general = act.value_load(flag_i[0:1, 0:1], min_val=0, max_val=1)
            with act.If(general == 0):
                split_c(0)
                for q in range(NQ):
                    for m in range(KC):
                        n = XK_T + 4 * q + m
                        act.wait_ge(sem["t_mm"], n + 1)
                        if m == 0 and q >= 1:
                            act.wait_ge(sem["s_mm"], 4 * q)
                        act.activation(kq_t[:, m, :], bank[m][:], ACT.Identity, bias=bias_col[:, 1, m:m + 1]).then_inc(sem["t_ev"], 1)
                    if q + 1 < NQ:
                        split_c(q + 1)
                    for p in range(4):
                        n = 4 * q + p
                        if p >= 2:
                            turned_probabilities(n - 2)
                        act.wait_ge(sem["s_sub"], n + 1)
                        if n >= 2:
                            act.wait_ge(sem["pt_mm"], n - 1)
                        act.activation(p_rows[:, n % 2, :], s_rows[:, n % 2, :], ACT.Exp, scale=SCALE).then_inc(sem["exp_done"], 1)
                        if p >= 2:
                            take_out(act, n - 2)
                    for n in (4 * q + 2, 4 * q + 3):
                        turned_probabilities(n)
                        take_out(act, n)
                    ts = slice(q * 256, (q + 1) * 256)
                    act.wait_ge(sem["o_act"], 4 * (q + 1))
                    act.wait_ge(sem["o_dve"], 4 * (q + 1))
                    act.activation(xt_hi[:, :, ts], o_t[:, :, ts], ACT.Copy).then_inc(sem["o_hi"], 1)
            with act.Else():
                with act.Fori(0, NPAIR) as i:
                    a0 = i * (3 * NCH + 1)
                    for c in range(NCH):
                        act.wait_ge(sem["g_pe"], i * (4 * NCH + 1) + 3 * c + 1)
                        for m in range(KC):
                            ins = act.activation(g_k[:, m, :], bank[0][:, m * P:(m + 1) * P], ACT.Identity, bias=bias_col[:, 1, m:m + 1])
                        ins.then_inc(sem["g_act"], 1)
                    act.wait_ge(sem["g_dve"], i * (NCH + 1) + NCH + 1)
                    act.activation(g_s[:], g_s[:], ACT.Exp, scale=SCALE).then_inc(sem["g_act"], 1)
                    for c in range(NCH):
                        act.wait_ge(sem["g_pe"], i * (4 * NCH + 1) + 3 * NCH + c + 1)
                        act.activation(g_pt[:, c, :], bank[5][:], ACT.Copy).then_inc(sem["g_act"], 1)
                    act.wait_ge(sem["g_pe"], (i + 1) * (4 * NCH + 1))
                    for b in range(2):
                        for h in range(HG):
                            rows = slice(h * DH, (h + 1) * DH)
                            ins = act.activation(o_t[rows, :, bass.ds(i * 2 * S + b * S, S)],
                                                 bank[6 + b][rows, :].rearrange("p (g n) -> p g n", g=KC)[:, :, h * S:(h + 1) * S], ACT.Copy)
                    ins.then_inc(sem["g_act"], NCH)
                act.drain().then_inc(sem["t_ev"], 4 * NQ)
                act.wait_ge(sem["g_act"], NPAIR * (3 * NCH + 1))
                act.activation(xt_hi[:], o_t[:], ACT.Copy).then_inc(sem["o_hi"], NQ)
            act.end_ifs()
            split_w(W_XO)
            split_w(W_AQ)
            split_w(W_AK)

            turned_hi(1)
            split_w(W_AV)
            out_t(q_t, 2, G_AQ, AQ_T)
            out_t(k_t, 3, G_AK, AK_T)
            split_w(W_FQ)
            act.wait_ge(sem["a_sub"], 1)
            act.activation(a_p[:], a_s[:], ACT.Exp, scale=ATTN_SCALE).then_inc(sem["a_exp"], 1)
            split_w(W_FK)

            turned_hi(2)
            split_w(W_FV)
            act.wait_ge(sem["gate_v"], 1)
            act.activation(gate_x[:, :, 0:E], gate[:], ACT.Exp).then_inc(sem["gate_exp"], 1)
            out_t(q_t, 4, G_FQ, FQ_T)
            split_w(W_EX)
            out_t(k_t, 5, G_FK, FK_T)
            split_w(W_EX + 1)
            for e in range(E):
                act.wait_ge(sem["f_mm"], e + 1)
                if e >= 1:
                    act.wait_ge(sem["f_exp"], e)
                for h in range(2):
                    for b in range(4):
                        rows = slice(b * S, (b + 1) * S)
                        ins = act.activation(f_s[rows, h:H:HG, :], bank[4 + h][rows, :].rearrange("p (g n) -> p g n", g=KC)[:, :, b * S:(b + 1) * S],
                                             ACT.Copy)
                ins.then_inc(sem["f_act"], 1)
                act.wait_ge(sem["f_sub"], e + 1)
                if e >= 1:
                    act.wait_ge(sem["f_tr"], 4 * e)
                act.activation(f_p[:], f_s[:], ACT.Exp, scale=SCALE).then_inc(sem["f_exp"], 1)
                if e + 2 < E:
                    split_w(W_EX + e + 2)

        @block.gpsimd
        def _(pool):
            pool.memset(power[:], -0.5).then_inc(sem["pow_set"], 1)

            def inv_std(s):
                for t in range(NT):
                    n = s * NT + t
                    pool.wait_ge(sem["aggr_done"], n + 1)
                    pool.tensor_scalar(rstd[:, 0, t:t + 1], aggr[:, t, 1:2], EPS, None, ALU.add).then_inc(sem["eps_done"], 1)
                    pool.wait_ge(sem["eps_done"], n + 1)
                    pool.tensor_tensor(rstd[:, 1, t:t + 1], rstd[:, 0, t:t + 1], power[:], ALU.pow).then_inc(sem["rstd_done"], 1)

            def split_w(n):
                pool.wait_ge(sem["w_hi_done"], n + 1)
                k = n % NSLOT
                pool.tensor_tensor(w_lo[:, k], w_stage[:], w_hi[:, k].bitcast(F32), ALU.subtract).then_inc(sem["w_lo_done"], 1)

            def split_c(q):
                pool.wait_ge(sem["c_hi_done"], q + 1)
                pool.tensor_tensor(c_lo[:, q % 2], c_stage[:], c_hi[:, q % 2].bitcast(F32), ALU.subtract).then_inc(sem["c_lo_done"], 1)

            def block_queries(slot, col):
                for b in range(2):
                    ins = pool.tensor_tensor(q_bd[:, slot, b].rearrange("p g (h n) -> p g h n", h=HG),
                                             q_t[:, :, col(b)].unsqueeze(2).broadcast_to([P, KC, HG, S]),
                                             head_on[:].unsqueeze(1).unsqueeze(3).broadcast_to([P, KC, HG, S]), ALU.mult)
                return ins

            pool.wait_ge(sem["pow_set"], 1)
            split_w(W_XQ)
            inv_std(0)
            split_w(W_XK)
            split_w(W_XV)
            pool.wait_ge(sem["bias_in"], 32)
            pool.wait_ge(sem["t_ev"], XQ_T + 8)
            pool.wait_ge(sem["flag_done"], 1)
            general = pool.value_load(flag_i[0:1, 0:1], min_val=0, max_val=1)
            with pool.If(general == 0):
                split_c(0)
                for q in range(NQ):
                    for p in range(4):
                        n = 4 * q + p
                        if n >= 2:
                            pool.wait_ge(sem["s_mm"], n - 1)
                        block_queries(n % 2, lambda b: slice(n * 2 * S + b * S, n * 2 * S + (b + 1) * S)).then_inc(sem["qbd_done"], 1)
                    if q + 1 < NQ:
                        split_c(q + 1)
                    for p in range(4):
                        n = 4 * q + p
                        pool.wait_ge(sem["s_inv"], n + 1)
                        r = p_rows[:, n % 2, :].rearrange("p (e k) -> p e k", k=CK)
                        pool.tensor_tensor(r, r, row_inv[:, n % 2, 0:8].unsqueeze(2).broadcast_to([P, 8, CK]), ALU.mult).then_inc(sem["p_done"], 1)
                    ts = slice(q * 256, (q + 1) * 256)
                    pool.wait_ge(sem["o_hi"], q + 1)
                    pool.tensor_tensor(xt_lo[:, :, ts], o_t[:, :, ts], xt_hi[:, :, ts].bitcast(F32), ALU.subtract).then_inc(sem["o_lo"], 1)
            with pool.Else():
                with pool.Fori(0, NPAIR) as i:
                    pool.wait_ge(sem["g_pe"], i * (4 * NCH + 1))
                    block_queries(0, lambda b: bass.ds(i * 2 * S + b * S, S)).then_inc(sem["g_q"], 1)
                    for c in range(NCH):
                        pool.wait_ge(sem["g_c_in"], 16 * (i * NCH + c + 1))
                        if c >= 1:
                            pool.wait_ge(sem["g_pe"], i * (4 * NCH + 1) + 3 * c)
                        pool.tensor_tensor(g_chi[:], g_ctx[:], ones[:].unsqueeze(1).broadcast_to([P, KC, P]), ALU.mult).then_inc(sem["g_hi"], 1)
                        pool.wait_ge(sem["g_hi"], i * NCH + c + 1)
                        pool.tensor_tensor(g_clo[:], g_ctx[:], g_chi[:].bitcast(F32), ALU.subtract).then_inc(sem["g_b"], 1)
                    pool.wait_ge(sem["s_inv"], i + 1)
                    for c in range(NCH):
                        r = g_s[:, c, :].rearrange("p (e k) -> p e k", k=CK)
                        ins = pool.tensor_tensor(r, r, row_inv[:, 0, 0:8].unsqueeze(2).broadcast_to([P, 8, CK]), ALU.mult)
                    ins.then_inc(sem["g_pool"], 1)
                pool.wait_ge(sem["o_hi"], NQ)
                pool.tensor_tensor(xt_lo[:], o_t[:], xt_hi[:].bitcast(F32), ALU.subtract).then_inc(sem["o_lo"], NQ)
            pool.end_ifs()
            split_w(W_XO)
            split_w(W_AQ)
            pool.wait_ge(sem["o_lo"], NQ)
            pool.memset(a_pt[:], 0.0).then_inc(sem["pt_zeroed"], 1)
            pool.memset(f_pt[:], 0.0).then_inc(sem["pt_zeroed"], 1)
            split_w(W_AK)
            inv_std(1)
            split_w(W_AV)
            split_w(W_FQ)
            split_w(W_FK)
            inv_std(2)
            split_w(W_FV)
            split_w(W_EX)
            split_w(W_EX + 1)
            for e in range(E):
                if e + 2 < E:
                    split_w(W_EX + e + 2)

        @block.vector
        def _(dve):
            def normalise(s):
                xn = xn_0 if s == 0 else xn_1

                def start(t):
                    if s == 0:
                        dve.wait_ge(sem["x_in"], 16 * NT)
                    else:
                        dve.wait_ge(sem["x_acc"], ACC_AT[({1: "xo", 2: "av"}[s], t)])
                    n = s * NT + t
                    dve.bn_stats(stats[:, t, :], x[:, t, :]).then_inc(sem["stats_done"], 1)
                    dve.wait_ge(sem["stats_done"], n + 1)
                    dve.bn_aggr(aggr[:, t, :], stats[:, t, :]).then_inc(sem["aggr_done"], 1)

                def scale(t):
                    n = s * NT + t
                    dve.wait_ge(sem["rstd_done"], n + 1)
                    if t >= 2:
                        dve.wait_ge(sem["tr_done"], n - 1)
                    dve.tensor_scalar(xn[:, t % 2, :], x[:, t, :], aggr[:, t, 0:1], rstd[:, 1, t:t + 1],
                                      ALU.subtract, ALU.mult).then_inc(sem["xn_done"], 1)

                def low(t):
                    n = s * NT + t
                    dve.wait_ge(sem["xt_hi_done"], n + 1)
                    ts = slice(t * P, (t + 1) * P)
                    dve.tensor_tensor(xt_lo[:, :, ts], bank[4 + t % 2][:].rearrange("p (c n) -> p c n", c=KC),
                                      xt_hi[:, :, ts].bitcast(F32), ALU.subtract).then_inc(sem["xt_lo_done"], 1)

                for t in range(NT + 2):
                    if t < NT:
                        start(t)
                    if 1 <= t <= NT:
                        scale(t - 1)
                    if t >= 2:
                        low(t - 2)

            def out_n(dst, g0, n0, row):
                for t in range(NT):
                    dve.wait_ge(sem["n_mm"], n0 + t + 1)
                    dve.tensor_tensor(dst[:, t, :], bank[(g0 + t) % 4][:], row, ALU.add).then_inc(sem["n_ev"], 1)

            dve.memset(ones[:], 1.0).then_inc(sem["ones_set"], 1)
            dve.wait_ge(sem["masknat_in"], 16)
            dve.tensor_scalar(mask_on[:], mask_nat[:, 0:TAIL], 0.0, None, ALU.not_equal).then_inc(sem["maskn_done"], 1)
            dve.wait_ge(sem["maskn_done"], 1)
            dve.wait_ge(sem["ones_set"], 1)
            dve.tensor_reduce(any_col[0:B, :], mask_on[:], AX.X, ALU.max).then_inc(sem["flag_sum"], 1)
            dve.wait_ge(sem["flag_mm"], 1)
            dve.tensor_scalar(flag_i[:], bank[6][0:1, 0:1], 1.0, None, ALU.min).then_inc(sem["flag_done"], 1)
            normalise(0)
            dve.wait_ge(sem["mask_in"], 16)
            dve.tensor_scalar(m_bias[:], mask_i[:], 0.0, MASKED, ALU.is_equal, ALU.mult).then_inc(sem["mbias_done"], 1)
            dve.wait_ge(sem["mbias_done"], 1)

            def nan_where_all_masked(bias3, n, first):
                dve.tensor_reduce(nan_b[:, 0, 0:n], bias3, AX.X, ALU.max).then_inc(sem["maskn_done"], 1)
                dve.wait_ge(sem["maskn_done"], first + 1)
                dve.tensor_scalar(nan_b[:, 1, 0:n], nan_b[:, 0, 0:n], 0.0, None, ALU.is_equal).then_inc(sem["maskn_done"], 1)
                dve.wait_ge(sem["maskn_done"], first + 2)
                dve.reciprocal(nan_b[:, 2, 0:n], nan_b[:, 1, 0:n]).then_inc(sem["maskn_done"], 1)
                dve.wait_ge(sem["maskn_done"], first + 3)
                dve.tensor_tensor(nan_b[:, 0, 0:n], nan_b[:, 1, 0:n], nan_b[:, 2, 0:n], ALU.mult).then_inc(sem["maskn_done"], 1)
                dve.wait_ge(sem["maskn_done"], first + 4)
                dve.tensor_scalar(nan_b[:, 1, 0:n], nan_b[:, 0, 0:n], -1.0, None, ALU.add).then_inc(sem["maskn_done"], 1)
                dve.wait_ge(sem["maskn_done"], first + 5)

            m3 = m_bias[:].rearrange("p (b k) -> p b k", k=CK)
            nan_where_all_masked(m3, B, 1)
            dve.tensor_tensor(m3, m3, nan_b[:, 1, :].unsqueeze(2).broadcast_to([P, B, CK]), ALU.add).then_inc(sem["mbias_done"], 1)
            dve.wait_ge(sem["biasx_in"], 16)
            general = dve.value_load(flag_i[0:1, 0:1], min_val=0, max_val=1)
            with dve.If(general == 0):
                dve.wait_ge(sem["mbias_done"], 2)

                def softmax_head(n):
                    srow = s_rows[:, n % 2, :]
                    dve.wait_ge(sem["s_mm"], n + 1)
                    if n >= 2:
                        dve.wait_ge(sem["exp_done"], n - 1)
                    dve.tensor_tensor(srow.rearrange("p (g k) -> p g k", g=KC), bank[4 + n % 2][:].rearrange("p (g k) -> p g k", g=KC),
                                      m_bias[:, n * P:(n + 1) * P].unsqueeze(1).broadcast_to([P, KC, P]), ALU.add).then_inc(sem["s_add"], 1)
                    dve.wait_ge(sem["s_add"], n + 1)
                    r = srow.rearrange("p (e k) -> p e k", k=CK)
                    dve.tensor_reduce(row_max[:, n % 2, 0:8], r, AX.X, ALU.max).then_inc(sem["s_max"], 1)
                    dve.wait_ge(sem["s_max"], n + 1)
                    dve.tensor_tensor(r, r, row_max[:, n % 2, 0:8].unsqueeze(2).broadcast_to([P, 8, CK]), ALU.subtract).then_inc(sem["s_sub"], 1)

                def softmax_sum(n):
                    dve.wait_ge(sem["exp_done"], n + 1)
                    if n >= 2:
                        dve.wait_ge(sem["p_done"], n - 1)
                    r = p_rows[:, n % 2, :].rearrange("p (e k) -> p e k", k=CK)
                    dve.tensor_reduce(row_sum[:, n % 2, 0:8], r, AX.X, ALU.add).then_inc(sem["s_sum"], 1)
                    dve.wait_ge(sem["s_sum"], n + 1)
                    dve.reciprocal(row_inv[:, n % 2, 0:8], row_sum[:, n % 2, 0:8]).then_inc(sem["s_inv"], 1)

                def values(q, p):
                    n = XV_N + 4 * q + p
                    dve.wait_ge(sem["n_mm"], n + 1)
                    if p == 0 and q >= 1:
                        dve.wait_ge(sem["o_mm"], 4 * q)
                    dve.tensor_tensor(vq_n[:, p, :], bank[p][:], bias_x[:, 0, :], ALU.add).then_inc(sem["n_ev"], 1)

                for q in range(NQ):
                    n = 4 * q
                    values(q, 0)
                    softmax_head(n)
                    softmax_head(n + 1)
                    values(q, 1)
                    softmax_sum(n)
                    values(q, 2)
                    softmax_sum(n + 1)
                    softmax_head(n + 2)
                    softmax_head(n + 3)
                    values(q, 3)
                    take_out(dve, n)
                    softmax_sum(n + 2)
                    take_out(dve, n + 1)
                    softmax_sum(n + 3)
                    take_out(dve, n + 2)
                    take_out(dve, n + 3)
            with dve.Else():
                with dve.Fori(0, NPAIR) as i:
                    d0 = i * (NCH + 1)
                    dve.wait_ge(sem["g_m_in"], 16 * (i + 1))
                    dve.tensor_scalar(g_bias[:], g_mask[:], 0.0, MASKED, ALU.is_equal, ALU.mult).then_inc(sem["mbias_done"], 1)
                    dve.wait_ge(sem["mbias_done"], i * 2 + 3)
                    for b in range(2):
                        dve.tensor_reduce(nan_b[:, 0, b:b + 1], g_bias[:, :, b * CK:(b + 1) * CK], AX.XY, ALU.max).then_inc(sem["maskn_done"], 1)
                    dve.wait_ge(sem["maskn_done"], i * 6 + 8)
                    dve.tensor_scalar(nan_b[:, 1, 0:2], nan_b[:, 0, 0:2], 0.0, None, ALU.is_equal).then_inc(sem["maskn_done"], 1)
                    dve.wait_ge(sem["maskn_done"], i * 6 + 9)
                    dve.reciprocal(nan_b[:, 2, 0:2], nan_b[:, 1, 0:2]).then_inc(sem["maskn_done"], 1)
                    dve.wait_ge(sem["maskn_done"], i * 6 + 10)
                    dve.tensor_tensor(nan_b[:, 0, 0:2], nan_b[:, 1, 0:2], nan_b[:, 2, 0:2], ALU.mult).then_inc(sem["maskn_done"], 1)
                    dve.wait_ge(sem["maskn_done"], i * 6 + 11)
                    dve.tensor_scalar(nan_b[:, 1, 0:2], nan_b[:, 0, 0:2], -1.0, None, ALU.add).then_inc(sem["maskn_done"], 1)
                    dve.wait_ge(sem["maskn_done"], i * 6 + 12)
                    for b in range(2):
                        gb = g_bias[:, :, b * CK:(b + 1) * CK]
                        ins = dve.tensor_scalar(gb, gb, nan_b[:, 1, b:b + 1], None, ALU.add)
                    ins.then_inc(sem["mbias_done"], 1)
                    dve.wait_ge(sem["mbias_done"], i * 2 + 4)
                    dve.wait_ge(sem["g_act"], i * (3 * NCH + 1))
                    for c in range(NCH):
                        dve.wait_ge(sem["g_pe"], i * (4 * NCH + 1) + 3 * c + 2)
                        dve.tensor_tensor(g_v[:, c, :], bank[1][:], bias_x[:, 0, :], ALU.add).then_inc(sem["s_add"], 1)
                        dve.wait_ge(sem["g_pe"], i * (4 * NCH + 1) + 3 * c + 3)
                        dve.tensor_tensor(g_s[:, c, :].rearrange("p (g k) -> p g k", g=KC), bank[4][:].rearrange("p (g k) -> p g k", g=KC),
                                          g_bias[:, c, :].unsqueeze(1).broadcast_to([P, KC, P]), ALU.add).then_inc(sem["g_dve"], 1)
                    dve.wait_ge(sem["g_dve"], d0 + NCH)
                    r = g_s[:].rearrange("p c (e k) -> p e c k", k=CK)
                    dve.tensor_reduce(row_max[:, 0, 0:8], r, AX.XY, ALU.max).then_inc(sem["s_max"], 1)
                    dve.wait_ge(sem["s_max"], i + 1)
                    for c in range(NCH):
                        rc = g_s[:, c, :].rearrange("p (e k) -> p e k", k=CK)
                        ins = dve.tensor_tensor(rc, rc, row_max[:, 0, 0:8].unsqueeze(2).broadcast_to([P, 8, CK]), ALU.subtract)
                    ins.then_inc(sem["g_dve"], 1)
                    dve.wait_ge(sem["g_act"], i * (3 * NCH + 1) + NCH + 1)
                    dve.tensor_reduce(row_sum[:, 0, 0:8], r, AX.XY, ALU.add).then_inc(sem["s_sum"], 1)
                    dve.wait_ge(sem["s_sum"], i + 1)
                    dve.reciprocal(row_inv[:, 0, 0:8], row_sum[:, 0, 0:8]).then_inc(sem["s_inv"], 1)
                dve.drain().then_inc(sem["n_ev"], 4 * NQ)
            dve.end_ifs()

            xo_row = bias_x[:, 1, :]
            for t in range(NT):
                ins = dve.tensor_tensor(x[:, t, :], x[:, t, :], xo_row, ALU.add)
            ins.then_inc(sem["xb_done"], 1)
            dve.wait_ge(sem["xb_done"], 1)
            acc = [0]

            def add_to_x(what, src, scale=None):
                i = acc[0]
                assert ACC[i] == what
                t = what[-1]
                if i >= NT:
                    dve.wait_ge(sem["x_acc"], last_acc(i))
                if scale is None:
                    ins = dve.tensor_tensor(x[:, t, :], src, x[:, t, :], ALU.add)
                else:
                    ins = dve.scalar_tensor_tensor(x[:, t, :], src, scale, x[:, t, :], ALU.mult, ALU.add)
                ins.then_inc(sem["x_acc"], 1)
                acc[0] += 1

            for t in range(NT):
                dve.wait_ge(sem["n_mm"], XO_N + t + 1)
                add_to_x(("xo", t), bank[(G_XO + t) % 4][:])
            normalise(1)

            for k in range(2):
                dve.wait_ge(sem["a_mm"], k + 1)
                for b in range(4):
                    rows = slice(b * S, (b + 1) * S)
                    ins = dve.tensor_copy(a_s[rows, 4 * k:4 * k + 4, :], bank[4 + k][rows, :].rearrange("p (t n) -> p t n", t=4)[:, :, b * S:(b + 1) * S])
            ins.then_inc(sem["a_ext"], 1)
            dve.wait_ge(sem["a_ext"], 1)
            dve.tensor_reduce(row_max[:, 0, 0:NT], a_s[:], AX.X, ALU.max).then_inc(sem["a_max"], 1)
            dve.wait_ge(sem["a_max"], 1)
            dve.tensor_tensor(a_s[:], a_s[:], row_max[:, 0, 0:NT].unsqueeze(2).broadcast_to([P, NT, S]), ALU.subtract).then_inc(sem["a_sub"], 1)
            dve.wait_ge(sem["a_exp"], 1)
            dve.tensor_reduce(row_sum[:, 0, 0:NT], a_p[:], AX.X, ALU.add).then_inc(sem["a_sum"], 1)
            dve.wait_ge(sem["a_sum"], 1)
            dve.reciprocal(row_inv[:, 0, 0:NT], row_sum[:, 0, 0:NT]).then_inc(sem["a_inv"], 1)
            dve.wait_ge(sem["a_inv"], 1)
            dve.tensor_tensor(a_p[:], a_p[:], row_inv[:, 0, 0:NT].unsqueeze(2).broadcast_to([P, NT, S]), ALU.mult).then_inc(sem["a_norm"], 1)
            dve.wait_ge(sem["a_norm"], 1)
            dve.wait_ge(sem["pt_zeroed"], 2)
            for b in range(4):
                rows = slice(b * S, (b + 1) * S)
                dve.transpose(a_pt[rows, :, b * S:(b + 1) * S], a_p[rows, :, :]).then_inc(sem["a_tr"], 1)
            dve.wait_ge(sem["biasf_in"], 16)
            out_n(v_n, G_AV, AV_N, bias_f[:, 0, :])
            for t in range(NT):
                dve.wait_ge(sem["av_mm"], t + 1)
                add_to_x(("av", t), bank[4 + t % 4][:])

            dve.wait_ge(sem["gate_in"], 32)
            dve.tensor_copy(wg_hi[:], g_stage[:]).then_inc(sem["wg_split"], 1)
            dve.wait_ge(sem["wg_split"], 1)
            dve.tensor_tensor(wg_lo[:], g_stage[:], wg_hi[:].bitcast(F32), ALU.subtract).then_inc(sem["wg_split"], 1)
            dve.memset(gate_x[:], -1.0).then_inc(sem["gx_set"], 1)
            dve.memset(top2[:], -1.0).then_inc(sem["gx_set"], 1)
            normalise(2)
            step = [0]

            def then_wait(ins):
                step[0] += 1
                ins.then_inc(sem["be_chain"], 1)
                dve.wait_ge(sem["be_chain"], step[0])

            dve.wait_ge(sem["gate_mm"], 1)
            lg = bank[6][:, 0:NT * E].rearrange("p (t e) -> p t e", e=E)
            then_wait(dve.tensor_tensor(gate[:], lg, b_gate[:].unsqueeze(1).broadcast_to([P, NT, E]), ALU.add))
            then_wait(dve.tensor_reduce(row_max[:, 0, 0:NT], gate[:], AX.X, ALU.max))
            dve.wait_ge(sem["gx_set"], 2)
            dve.tensor_tensor(gate[:], gate[:], row_max[:, 0, 0:NT].unsqueeze(2).broadcast_to([P, NT, E]), ALU.subtract).then_inc(sem["gate_v"], 1)
            dve.wait_ge(sem["gate_exp"], 1)
            gx = gate_x[:, :, 0:E]
            then_wait(dve.tensor_reduce(row_sum[:, 0, 0:NT], gx, AX.X, ALU.add))
            then_wait(dve.reciprocal(row_inv[:, 0, 0:NT], row_sum[:, 0, 0:NT]))
            then_wait(dve.tensor_tensor(gx, gx, row_inv[:, 0, 0:NT].unsqueeze(2).broadcast_to([P, NT, E]), ALU.mult))
            for t in range(NT):
                ins = dve.max(top[:, t, :], gate_x[:, t, 0:E])
            then_wait(ins)
            then_wait(dve.tensor_copy(top2[:, :, 0:2], top[:, :, 0:2]))
            for t in range(NT):
                ins = dve.match_replace(gate_r[:, t, :], top2[:, t, :], gate_x[:, t, :], 0.0)
            then_wait(ins)
            dve.tensor_tensor(comb[:], gx, gate_r[:, :, 0:E], ALU.subtract).then_inc(sem["comb_done"], 1)
            dve.wait_ge(sem["combt_mm"], 1)
            for k in range(2):
                dve.tensor_copy(comb_t[:, k * 512:(k + 1) * 512], bank[4 + k][0:E, :]).then_inc(sem["combt_ev"], 1)
            for t in range(NT):
                dve.wait_ge(sem["be_mm"], t + 1)
                add_to_x(("be", t), bank[4 + t % 4][:])
            out_n(v_n, G_FV, FV_N, bias_f[:, 1, :])
            dve.wait_ge(sem["comb_done"], 1)

            def expert_out(e, t):
                dve.wait_ge(sem["n_mm"], EX_N + 8 * e + t + 1)
                add_to_x(("ex", e, t), bank[(G_EX + 8 * e + t) % 4][:], comb[:, t, e:e + 1])

            for e in range(E):
                dve.wait_ge(sem["f_mm"], e + 1)
                if e >= 1:
                    dve.wait_ge(sem["f_exp"], e)
                for h in range(2, 4):
                    for b in range(4):
                        rows = slice(b * S, (b + 1) * S)
                        ins = dve.tensor_copy(f_s[rows, h:H:HG, :], bank[4 + h][rows, :].rearrange("p (g n) -> p g n", g=KC)[:, :, b * S:(b + 1) * S])
                ins.then_inc(sem["f_dve"], 1)
                dve.wait_ge(sem["f_act"], e + 1)
                dve.wait_ge(sem["f_dve"], e + 1)
                dve.tensor_reduce(row_max[:, 0, :], f_s[:], AX.X, ALU.max).then_inc(sem["f_max"], 1)
                dve.wait_ge(sem["f_max"], e + 1)
                dve.tensor_tensor(f_s[:], f_s[:], row_max[:, 0, :].unsqueeze(2).broadcast_to([P, H, S]), ALU.subtract).then_inc(sem["f_sub"], 1)
                expert_out(e, 0)
                expert_out(e, 1)
                dve.wait_ge(sem["f_exp"], e + 1)
                dve.tensor_reduce(row_sum[:, 0, :], f_p[:], AX.X, ALU.add).then_inc(sem["f_sum"], 1)
                dve.wait_ge(sem["f_sum"], e + 1)
                dve.reciprocal(row_inv[:, 0, :], row_sum[:, 0, :]).then_inc(sem["f_inv"], 1)
                dve.wait_ge(sem["f_inv"], e + 1)
                dve.tensor_tensor(f_p[:], f_p[:], row_inv[:, 0, :].unsqueeze(2).broadcast_to([P, H, S]), ALU.mult).then_inc(sem["f_norm"], 1)
                dve.wait_ge(sem["f_norm"], e + 1)
                expert_out(e, 2)
                if e >= 1:
                    dve.wait_ge(sem["fv_mm"], e)
                for b in range(4):
                    rows = slice(b * S, (b + 1) * S)
                    dve.transpose(f_pt[rows, :, b * S:(b + 1) * S], f_p[rows, :, :]).then_inc(sem["f_tr"], 1)
                for t in range(3, NT):
                    expert_out(e, t)
                dve.wait_ge(sem["fv_mm"], e + 1)
                add_to_x(("fv", e), bank[4][:])


def _kernel_arrays(x, ctx_1024, mask, Wxq, bxq, Wxk, bxk, Wxv, bxv, Wxo, bxo, Waq, baq, Wak, bak, Wav, bav,
                   W_qkv, b_qkv, W_gate, b_gate, W_experts, b_experts):
    def rows(w):
        return w.reshape(KC, P, -1).transpose(1, 0, 2)

    ws = [w.T for w in (Wxq, Wxk, Wxv, Wxo, Waq, Wak, Wav)] + [W_qkv[:, i * D:(i + 1) * D] for i in range(3)] + list(W_experts)
    slots = np.concatenate([np.arange(1, PAD + 1), np.arange(SK)])
    chunks = ctx_1024[:, slots].reshape(NPAIR, 2, NCH, CK, KC, P).transpose(0, 2, 5, 4, 1, 3)
    m = np.concatenate([np.zeros((B, PAD), mask.dtype), mask.reshape(B, SK)], axis=1)
    cols = np.stack([bxq, bxk, baq, bak, b_qkv[0:D], b_qkv[D:2 * D]])
    c = np.ascontiguousarray
    return {
        "x_in_dram": c(x.reshape(TOK, D)),
        "ctx_tail_dram": c(ctx_1024[:, TAIL:].reshape(NQ, 8 * CK, KC, P).transpose(0, 3, 2, 1)),
        "ctx_all_dram": c(chunks).reshape(NPAIR * NCH, P, KC, P),
        "mask_dram": c(mask.reshape(B, SK)),
        "mask_tail_dram": c(mask.reshape(B, SK)[:, TAIL:]).reshape(1, B * CK),
        "mask_all_dram": c(m.reshape(NPAIR, 2, NCH, CK).transpose(0, 2, 1, 3)).reshape(NPAIR, NCH * P),
        "weights_dram": c(np.stack([rows(w) for w in ws])),
        "bias_col_dram": c(cols.reshape(6, KC, P).transpose(2, 0, 1)),
        "bias_row_dram": c(np.stack([bxv, bxo, bav, b_qkv[2 * D:]]))[None],
        "w_gate_dram": c(rows(W_gate)),
        "b_gate_dram": c(b_gate[None]),
        "b_experts_dram": c(b_experts),
        "ident_dram": np.eye(P, dtype=np.float32),
        "head_on_dram": np.repeat(np.eye(HG, dtype=np.float32), DH, axis=0),
    }


def kernel(**inputs):
    import concourse.bacc as bacc
    from concourse.bass_utils import run_bass_kernel_spmd

    nc = bacc.Bacc("TRN2", target_bir_lowering=False, num_devices=1)
    names = ["x", "ctx_1024", "mask_Bx1xS2_ik0"] + [f"L0_xattn_{n}" for n in "Wq bq Wk bk Wv bv Wo bo".split()] \
        + [f"L0_attn_{n}" for n in "Wq bq Wk bk Wv bv".split()] \
        + [f"L0_ffn_{n}" for n in "W_qkv b_qkv W_gate b_gate W_experts b_experts".split()]
    arrays = _kernel_arrays(*[np.asarray(inputs[n]) for n in names])
    args = [nc.dram_tensor(n, a.shape, mybir.dt.from_np(a.dtype), kind="ExternalInput").ap() for n, a in arrays.items()]
    out = nc.dram_tensor("out_dram", (TOK, D), F32, kind="ExternalOutput").ap()
    perceiver_kernel(nc, *args, out)
    r = run_bass_kernel_spmd(nc, [arrays], core_ids=[0])
    return r.results[0]["out_dram"].reshape(B, S, D)
```

```python
from contextlib import ExitStack

import numpy as np

import concourse.bass as bass
from concourse import mybir

F32 = mybir.dt.float32
F32R = mybir.dt.float32r
BF16 = mybir.dt.bfloat16
I32 = mybir.dt.int32
ALU = mybir.AluOpType
ACT = mybir.ActivationFunctionType
AX = mybir.AxisListType

B, S, SK, D, H, E = 32, 32, 257, 512, 16, 8
P = 128
TOK = B * S
NT = TOK // P
KC = D // P
DH = D // H
HG = P // DH
CK = 64
NCH = -(-SK // CK)
PAD = NCH * CK - SK
TAIL = SK - CK
NPAIR = B // 2
NQ = 4
SCALE = float(DH) ** -0.5
ATTN_SCALE = float(S) ** -0.5
EPS = 1e-5
MASKED = -1.0e30

KB = 1024
NW = 18
NSLOT = 3


def perceiver_kernel(nc, x_d, ctx_tail_d, ctx_all_d, mask_d, mask_tail_d, mask_all_d, w_d, bias_col_d,
                     bias_row_d, w_gate_d, b_gate_d, b_exp_d, ident_d, head_on_d, out_d):
    ctx = ExitStack()
    with ctx:
        base = -(-nc.sbuf_base // 64) * 64
        arena = ctx.enter_context(nc.sbuf_tensor("arena", [P, 208 * KB - 256], mybir.dt.uint8))
        del arena

        def sb(name, kb, shape, dt=F32):
            return nc.alloc_sbuf_tensor_at(name, shape, dt, offset=base + int(kb * KB))

        w_stage = sb("w_stage", 0, [P, KC, D])
        w1_stage = sb("w1_stage", 72, [P, KC, D])
        w_hi = sb("w_hi", 8, [P, NSLOT, KC, D], F32R)
        w_lo = sb("w_lo", 32, [P, NSLOT, KC, D], F32R)
        x = sb("x", 56, [P, NT, D])
        xt_hi = sb("xt_hi", 72, [P, KC, TOK], F32R)
        xt_lo = sb("xt_lo", 88, [P, KC, TOK], F32R)
        o_t = sb("o_t", 88, [P, KC, TOK])
        q_t = sb("q_t", 104, [P, KC, TOK])
        k_t = sb("k_t", 120, [P, KC, TOK])
        kq_t = sb("kq_t", 120, [P, KC, 512])
        s_rows = sb("s_rows", 128, [P, 2, 512])
        p_rows = sb("p_rows", 132, [P, 2, 512])
        v_n = sb("v_n", 136, [P, NT, D])
        vq_n = sb("vq_n", 136, [P, 4, D])
        pt_x = sb("pt_x", 144, [P, 2, 512])
        bias_x = sb("bias_x", 148, [P, 2, D])
        c_hi = sb("c_hi", 152, [P, 2, KC, 512], F32R)
        c_lo = sb("c_lo", 168, [P, 2, KC, 512], F32R)
        c_stage = sb("c_stage", 184, [P, KC, 512])
        mask_i = sb("mask_i", 128, [P, B * CK], I32)
        q_bd = sb("q_bd", 192, [P, 2, 2, KC, P])
        m_bias = sb("m_bias", 200, [P, B * CK], BF16)
        bias_f = sb("bias_f", 200, [P, 2, D])
        ident = sb("ident", 204, [P, P])
        bias_col = sb("bias_col", 204.5, [P, 6, KC])
        stats = sb("stats", 204.625, [P, NT, 6])
        aggr = sb("aggr", 204.875, [P, NT, 2])
        rstd = sb("rstd", 205, [P, 2, NT])
        power = sb("power", 205.0625, [P, 1])
        row_max = sb("row_max", 205.125, [P, 2, 16])
        row_sum = sb("row_sum", 205.25, [P, 2, 16])
        row_inv = sb("row_inv", 205.375, [P, 2, 16])
        nan_b = sb("nan_b", 205.5, [P, 3, B])
        flag_i = sb("flag_i", 206, [1, 1], I32)
        ones = sb("ones", 206.0625, [P, 1])
        any_col = sb("any_col", 206.125, [P, 1])
        b_gate = sb("b_gate", 206.1875, [E, 1])
        head_on = sb("head_on", 206.25, [P, HG])
        mask_nat = sb("mask_nat", 144, [B, SK], I32)
        mask_on = sb("mask_on", 146, [B, TAIL])
        g_ctx = sb("g_ctx", 184, [P, KC, P])
        g_mask = sb("g_mask", 186, [P, NCH, P], I32)
        g_bias = sb("g_bias", 189, [P, NCH, P])
        g_chi = sb("g_chi", 128, [P, KC, P], F32R)
        g_clo = sb("g_clo", 130, [P, KC, P], F32R)
        g_k = sb("g_k", 120, [P, KC, P])
        g_s = sb("g_s", 152, [P, NCH, 512])
        g_pt = sb("g_pt", 162, [P, NCH, 512])
        g_v = sb("g_v", 172, [P, NCH, D])
        xn_0 = sb("xn_0", 144, [P, 2, D])
        xn_1 = sb("xn_1", 152, [P, 2, D])
        a_s = sb("a_s", 160, [P, NT, S])
        a_p = sb("a_p", 161, [P, NT, S])
        a_pt = sb("a_pt", 162, [P, NT, P])
        f_s = sb("f_s", 152, [P, H, S])
        f_p = sb("f_p", 154, [P, H, S])
        f_pt = sb("f_pt", 166, [P, H, P])
        gate = sb("gate", 174, [P, NT, E])
        gate_x = sb("gate_x", 174.25, [P, NT, 16])
        gate_r = sb("gate_r", 174.75, [P, NT, 16])
        top = sb("top", 175.25, [P, NT, 8])
        top2 = sb("top2", 175.5, [P, NT, 8])
        comb = sb("comb", 175.75, [P, NT, E])
        gate_t = sb("gate_t", 176, [E, TOK])
        comb_t = sb("comb_t", 176, [E, TOK])
        b_exp = sb("b_exp", 180, [E, D])
        g_stage = sb("g_stage", 182, [P, KC, E])
        k_bd = sb("k_bd", 184, [P, 2, 4, KC, P])
        wg_hi = sb("wg_hi", 156, [P, KC, P], F32R)
        wg_lo = sb("wg_lo", 158, [P, KC, P], F32R)

        bank = [ctx.enter_context(nc.psum_tensor(f"bank{i}", [P, 512], F32)) for i in range(8)]

        names = """x_in ident_in bias_in biasx_in biasf_in mask_in masknat_in maskn_done gate_in bexp_in
            w0_in0 w0_in1 w0_in2 w0_in3 c0_in0 c0_in1 c0_in2 c0_in3 w0_hi_done w0_lo_done c0_hi_done c0_lo_done
            w1_in w_in w_hi_done w_lo_done c_in c_hi_done c_lo_done g_hi pow_set stats_done aggr_done eps_done
            rstd_done xn_done tr_done xt_hi_done xt_lo_done t_mm t_ev n_mm n_ev
            flag_sum flag_mm flag_done mbias_done ones_set xb_done pt_zeroed gx_set
            qbd_done s_mm s_add s_max s_sub exp_done s_sum s_inv p_done pt_mm pt_ev o_mm o_act o_dve
            o_hi o_lo
            a_mm a_ext a_max a_sub a_exp a_sum a_inv a_norm a_tr av_mm x_acc
            gate_mm gate_ev gatet_mm gate_v gate_exp comb_done combt_mm combt_ev be_mm gate_step wg_split
            kbd_done f_mm f_max f_sub f_exp f_sum f_inv f_norm f_tr fv_mm
            g_c_in g_m_in g_pe g_act g_dve g_pool g_q g_b done_out""".split()
        sem = {n: ctx.enter_context(nc.semaphore(n)) for n in names}

        WEIGHTS = ["xk", "xv", "xq", "xo", "aq", "ak", "av", "fq", "fk", "fv"] + [("ex", e) for e in range(E)]
        W_AT = {w: n for n, w in enumerate(WEIGHTS)}
        W_SLOT = [0, 1, 2, 2, 0, 1, 2, 0, 1, 2] + [e % NSLOT for e in range(E)]
        W_BEFORE = [max((m for m in range(n) if W_SLOT[m] == W_SLOT[n]), default=None) for n in range(NW)]

        GROUPS = [("xk", 0, m) for m in range(KC)] + [("xv", 0, p) for p in range(4)]
        GROUPS += [("xq", h, m) for h in range(2) for m in range(KC)]
        for q in range(1, NQ):
            GROUPS += [("xk", q, m) for m in range(KC)] + [("xv", q, p) for p in range(4)]
        GROUPS += [("xo", t) for t in range(6)] + [("aq", 0, m) for m in range(KC)] + [("xo", 6), ("xo", 7)]
        GROUPS += [("ak", 0, m) for m in range(KC)] + [(w, 1, m) for w in ("aq", "ak") for m in range(KC)]
        GROUPS += [("av", t) for t in range(NT)]
        GROUPS += [(w, h, m) for w in ("fq", "fk") for h in range(2) for m in range(KC)]
        GROUPS += [("fv", t) for t in range(NT)] + [("ex", e, t) for e in range(E) for t in range(NT)]
        BANK = {g: i % 4 for i, g in enumerate(GROUPS)}
        T_FORM = ("xk", "xq", "aq", "ak", "fq", "fk")
        T_GROUPS = [g for g in GROUPS if g[0] in T_FORM]
        N_GROUPS = [g for g in GROUPS if g[0] not in T_FORM]
        V_GROUPS = [g for g in N_GROUPS if g[0] in ("xv", "av", "fv")]
        MM_AT = {g: i + 1 for gs in (T_GROUPS, N_GROUPS) for i, g in enumerate(gs)}

        ACC = [("xo", t) for t in range(NT)] + [("at", t) for t in range(NT)] + [("be", t) for t in range(NT)]
        for e in range(E):
            ACC += [("ex", e, t) for t in range(6)] + [("fa", e)] + [("ex", e, t) for t in range(6, NT)]
        ACC_AT = {a: i + 1 for i, a in enumerate(ACC)}
        X_FINAL = [max(ACC_AT["ex", E - 1, t], ACC_AT["fa", t]) for t in range(NT)]

        FREED = {g: ("t_ev", i + 1) for i, g in enumerate(T_GROUPS)}
        FREED |= {g: ("n_ev", i + 1) for i, g in enumerate(V_GROUPS)}
        FREED |= {g: ("x_acc", ACC_AT[g]) for g in N_GROUPS if g[0] in ("xo", "ex")}

        def evacuated(eng, group):
            i = GROUPS.index(group)
            if i >= 4:
                name, value = FREED[GROUPS[i - 4]]
                eng.wait_ge(sem[name], value)

        def group_done(eng, group):
            eng.wait_ge(sem["t_mm" if group[0] in T_FORM else "n_mm"], MM_AT[group])

        def out_of_bank(eng, group):
            name, value = FREED[group]
            eng.wait_ge(sem[name], value)

        def last_group(w):
            return [g for g in GROUPS if g[0] == w or g[:2] == w][-1]

        PE_N, ACT_N, DVE_N = 4 * NCH + 1, 3 * NCH + 1, NCH + 1

        def take_out(eng, n, b):
            eng.wait_ge(sem["o_mm"], n + 1)
            for h in range(HG):
                rows = slice(h * DH, (h + 1) * DH)
                dst = o_t[rows, :, n * 2 * S + b * S:n * 2 * S + (b + 1) * S]
                blk = bank[6 + b][rows, :].rearrange("p (g n) -> p g n", g=KC)[:, :, h * S:(h + 1) * S]
                ins = eng.activation(dst, blk, ACT.Copy) if b == 0 else eng.tensor_copy(dst, blk)
            ins.then_inc(sem["o_act" if b == 0 else "o_dve"], 1)

        block = ctx.enter_context(nc.Block())

        @block.sync
        def _(sp):
            def load_w(n):
                if n == 2:
                    sp.wait_ge(sem["w0_lo_done"], KC)
                else:
                    sp.wait_ge(sem["w_lo_done"], n - 1)
                sp.dma_start(w_stage[:], w_d[n]).then_inc(sem["w_in"], 16)

            def load_c(q):
                if q == 1:
                    sp.wait_ge(sem["c0_lo_done"], KC)
                else:
                    sp.wait_ge(sem["c_lo_done"], q - 1)
                sp.dma_start(c_stage[:], ctx_tail_d[q]).then_inc(sem["c_in"], 16)

            sp.dma_start(mask_nat[:], mask_d).then_inc(sem["masknat_in"], 16)
            for c in range(KC):
                sp.dma_start(w_stage[:, c, :], w_d[0, :, c, :]).then_inc(sem[f"w0_in{c}"], 16)
                sp.dma_start(c_stage[:, c, :], ctx_tail_d[0, :, c, :]).then_inc(sem[f"c0_in{c}"], 16)
            sp.dma_start(w1_stage[:], w_d[1]).then_inc(sem["w1_in"], 16)
            for t in range(NT):
                sp.dma_start(x[:, t, :], x_d[t * P:(t + 1) * P, :]).then_inc(sem["x_in"], 16)
            sp.dma_start(ident[:], ident_d).then_inc(sem["ident_in"], 16)
            sp.dma_start(bias_col[:], bias_col_d).then_inc(sem["bias_in"], 16)
            sp.dma_start(head_on[:], head_on_d).then_inc(sem["bias_in"], 16)
            sp.dma_start(bias_x[:], bias_row_d[0:1, 0:2, :].broadcast_to([P, 2, D])).then_inc(sem["biasx_in"], 16)
            sp.dma_start(mask_i[:], mask_tail_d.broadcast_to([P, B * CK])).then_inc(sem["mask_in"], 16)
            sp.dma_start(b_gate[:], b_gate_d).then_inc(sem["gate_in"], 16)
            load_w(2)
            sp.wait_ge(sem["flag_done"], 1)
            general = sp.value_load(flag_i[0:1, 0:1], min_val=0, max_val=1)
            with sp.If(general == 0):
                load_c(1)
                load_c(2)
                load_c(3)
                load_w(3)
            with sp.Else():
                for c in range(KC):
                    sp.wait_ge(sem[f"c0_in{c}"], 16)
                with sp.Fori(0, NPAIR) as i:
                    sp.wait_ge(sem["g_dve"], i * DVE_N + 1)
                    sp.dma_start(g_mask[:], mask_all_d[bass.ds(i, 1), :].broadcast_to([P, NCH * P])).then_inc(sem["g_m_in"], 16)
                    for c in range(NCH):
                        sp.wait_ge(sem["g_b"], i * NCH + c + 1)
                        sp.dma_start(g_ctx[:], ctx_all_d[bass.ds(i * NCH + c, 1)]).then_inc(sem["g_c_in"], 16)
                load_w(3)
            sp.end_ifs()
            load_w(W_AT["aq"])
            load_w(W_AT["ak"])
            sp.wait_ge(sem["o_lo"], NQ)
            sp.dma_start(bias_f[:], bias_row_d[0:1, 2:4, :].broadcast_to([P, 2, D])).then_inc(sem["biasf_in"], 16)
            sp.dma_start(g_stage[:], w_gate_d).then_inc(sem["gate_in"], 16)
            sp.dma_start(b_exp[:], b_exp_d).then_inc(sem["bexp_in"], 16)
            for n in range(W_AT["ak"] + 1, NW):
                load_w(n)
            for t in range(NT):
                sp.wait_ge(sem["x_acc"], X_FINAL[t])
                sp.dma_start(out_d[t * P:(t + 1) * P, :], x[:, t, :]).then_inc(sem["done_out"], 16)
            sp.wait_ge(sem["done_out"], 16 * NT)

        @block.tensor
        def _(pe):
            def three_passes(out, l_hi, l_lo, r_hi, r_lo):
                for c in range(KC):
                    pe.matmul(out, l_hi(c), r_hi(c), start=(c == 0), stop=False)
                    pe.matmul(out, l_hi(c), r_lo(c), start=False, stop=False)
                    mm = pe.matmul(out, l_lo(c), r_hi(c), start=False, stop=(c == KC - 1))
                return mm

            def weight_ready(w):
                if W_AT[w] == 0:
                    pe.wait_ge(sem["w0_lo_done"], KC)
                else:
                    pe.wait_ge(sem["w_lo_done"], W_AT[w])
                return W_SLOT[W_AT[w]]

            def product_t(group, r_hi, r_lo):
                w, _, m = group
                k = weight_ready(w)
                evacuated(pe, group)
                ms = slice(m * P, (m + 1) * P)
                three_passes(bank[BANK[group]][:], lambda c: w_hi[:, k, c, ms], lambda c: w_lo[:, k, c, ms],
                             r_hi, r_lo).then_inc(sem["t_mm"], 1)

            def features(group):
                ts = slice(group[1] * 512, (group[1] + 1) * 512)
                pe.wait_ge(sem["xt_lo_done"], NT * {"xq": 0, "aq": 1, "ak": 1, "fq": 2, "fk": 2}[group[0]] + 4 * (group[1] + 1))
                product_t(group, lambda c: xt_hi[:, c, ts], lambda c: xt_lo[:, c, ts])

            def product_n(group):
                k = weight_ready(group[:2] if group[0] == "ex" else group[0])
                evacuated(pe, group)
                ts = slice(group[-1] * P, (group[-1] + 1) * P)
                three_passes(bank[BANK[group]][:], lambda c: xt_hi[:, c, ts], lambda c: xt_lo[:, c, ts],
                             lambda c: w_hi[:, k, c, :], lambda c: w_lo[:, k, c, :]).then_inc(sem["n_mm"], 1)

            def turn(s, t):
                n = s * NT + t
                pe.wait_ge(sem["xn_done"], n + 1)
                if t >= 2:
                    pe.wait_ge(sem["xt_lo_done"], n - 1)
                xn = xn_0 if s == 0 else xn_1
                for c in range(KC):
                    mm = pe.transpose(bank[4 + t % 2][:, c * P:(c + 1) * P], xn[:, t % 2, c * P:(c + 1) * P], ident[:])
                mm.then_inc(sem["tr_done"], 1)

            def first_keys():
                for c in range(KC):
                    pe.wait_ge(sem["w0_lo_done"], c + 1)
                    pe.wait_ge(sem["c0_lo_done"], c + 1)
                    for m in range(KC):
                        out, ms = bank[BANK["xk", 0, m]][:], slice(m * P, (m + 1) * P)
                        pe.matmul(out, w_hi[:, 0, c, ms], c_hi[:, 0, c, :], start=(c == 0), stop=False)
                        pe.matmul(out, w_hi[:, 0, c, ms], c_lo[:, 0, c, :], start=False, stop=False)
                        mm = pe.matmul(out, w_lo[:, 0, c, ms], c_hi[:, 0, c, :], start=False, stop=(c == KC - 1))
                        if c == KC - 1:
                            mm.then_inc(sem["t_mm"], 1)

            def keys(q, m):
                pe.wait_ge(sem["c_lo_done"], q)
                product_t(("xk", q, m), lambda c: c_hi[:, q % 2, c, :], lambda c: c_lo[:, q % 2, c, :])

            def values(q, p):
                group = ("xv", q, p)
                k = weight_ready("xv")
                evacuated(pe, group)
                ps = slice(p * P, (p + 1) * P)
                three_passes(bank[BANK[group]][:], lambda c: c_hi[:, q % 2, c, ps], lambda c: c_lo[:, q % 2, c, ps],
                             lambda c: w_hi[:, k, c, :], lambda c: w_lo[:, k, c, :]).then_inc(sem["n_mm"], 1)

            def scores(n):
                q, p = divmod(n, 4)
                out_of_bank(pe, ("xk", q, KC - 1))
                pe.wait_ge(sem["qbd_done"], n + 1)
                if p >= 2:
                    pe.wait_ge(sem["s_add"], n - 1)
                elif n >= 2:
                    pe.wait_ge(sem["pt_ev"], n - 1)
                else:
                    pe.wait_ge(sem["xt_lo_done"], NT)
                for b in range(2):
                    for g in range(KC):
                        mm = pe.matmul(bank[4 + n % 2][:, g * P + b * CK:g * P + (b + 1) * CK], q_bd[:, n % 2, b, g, :],
                                       kq_t[:, g, p * P + b * CK:p * P + (b + 1) * CK], start=True, stop=True)
                mm.then_inc(sem["s_mm"], 1)

            def probabilities(n):
                pe.wait_ge(sem["p_done"], n + 1)
                if n % 4 < 2:
                    pe.wait_ge(sem["s_add"], n + 3)
                else:
                    pe.wait_ge(sem["pt_ev"], n - 1)
                for g in range(KC):
                    mm = pe.transpose(bank[4 + n % 2][:, g * P:(g + 1) * P], p_rows[:, n % 2, g * P:(g + 1) * P], ident[:])
                mm.then_inc(sem["pt_mm"], 1)

            def outputs(n):
                q, p = divmod(n, 4)
                pe.wait_ge(sem["pt_ev"], n + 1)
                out_of_bank(pe, ("xv", q, p))
                if n >= 1:
                    pe.wait_ge(sem["o_act"], n)
                    pe.wait_ge(sem["o_dve"], n)
                for b in range(2):
                    for g in range(KC):
                        mm = pe.matmul(bank[6 + b][:, g * P:(g + 1) * P], vq_n[b * CK:(b + 1) * CK, p, g * P:(g + 1) * P],
                                       pt_x[b * CK:(b + 1) * CK, n % 2, g * P:(g + 1) * P], start=True, stop=True)
                mm.then_inc(sem["o_mm"], 1)

            def attend(q, between):
                n = 4 * q
                scores(n)
                scores(n + 1)
                between(0)
                scores(n + 2)
                scores(n + 3)
                between(1)
                between(2)
                probabilities(n)
                between(3)
                probabilities(n + 1)
                between(4)
                outputs(n)
                probabilities(n + 2)
                between(5)
                outputs(n + 1)
                probabilities(n + 3)
                between(6)
                outputs(n + 2)
                between(7)
                outputs(n + 3)

            pe.wait_ge(sem["flag_sum"], 1)
            pe.matmul(bank[6][0:1, 0:1], any_col[0:B, :], ones[0:B, :], start=True, stop=True).then_inc(sem["flag_mm"], 1)
            pe.wait_ge(sem["flag_done"], 1)
            general = pe.value_load(flag_i[0:1, 0:1], min_val=0, max_val=1)
            with pe.If(general == 0):
                first_keys()
                values(0, 0)
                values(0, 1)
                pe.wait_ge(sem["ident_in"], 16)
                turn(0, 0)
                values(0, 2)
                turn(0, 1)
                values(0, 3)
                turn(0, 2)
                turn(0, 3)
                for m in range(KC):
                    features(("xq", 0, m))
                    turn(0, 4 + m)
                for m in range(KC):
                    features(("xq", 1, m))
                for q in range(NQ - 1):
                    attend(q, lambda j: keys(q + 1, j) if j < KC else values(q + 1, j - KC))

                def between(j):
                    if j < 6:
                        pe.wait_ge(sem["o_lo"], j // 2 + 1)
                        product_n(("xo", j))
                    else:
                        pe.wait_ge(sem["pt_ev"], 4 * NQ - 7 + j)
                        turn(1, j - 6)
                attend(NQ - 1, between)
            with pe.Else():
                pe.sem_inc(sem["g_pe"], 1)
                pe.wait_ge(sem["ident_in"], 16)
                for t in range(NT):
                    turn(0, t)
                kx, vx, qx = (W_SLOT[W_AT[w]] for w in ("xk", "xv", "xq"))
                pe.wait_ge(sem["w_lo_done"], W_AT["xq"])
                pe.wait_ge(sem["w0_lo_done"], KC)
                pe.wait_ge(sem["xt_lo_done"], NT)
                for j in range(8):
                    ms, ts = slice(j % 4 * P, (j % 4 + 1) * P), slice(j // 4 * 512, (j // 4 + 1) * 512)
                    if j >= 4:
                        pe.wait_ge(sem["t_ev"], j - 3)
                    three_passes(bank[j % 4][:], lambda c: w_hi[:, qx, c, ms], lambda c: w_lo[:, qx, c, ms],
                                 lambda c: xt_hi[:, c, ts], lambda c: xt_lo[:, c, ts]).then_inc(sem["t_mm"], 1)
                pe.wait_ge(sem["t_ev"], 8)
                with pe.Fori(0, NPAIR) as i:
                    p0, a0, d0 = i * PE_N + 1, i * ACT_N + 1, i * DVE_N + 1
                    for c in range(NCH):
                        pe.wait_ge(sem["g_b"], i * NCH + c + 2)
                        pe.wait_ge(sem["g_dve"], d0 + c)
                        if c == 0:
                            pe.wait_ge(sem["g_act"], a0)
                        for m in range(KC):
                            ms = slice(m * P, (m + 1) * P)
                            mm = three_passes(bank[0][:, ms], lambda k: w_hi[:, kx, k, ms], lambda k: w_lo[:, kx, k, ms],
                                              lambda k: g_chi[:, k, :], lambda k: g_clo[:, k, :])
                        mm.then_inc(sem["g_pe"], 1)
                        three_passes(bank[1][:], lambda k: g_chi[:, k, :], lambda k: g_clo[:, k, :],
                                     lambda k: w_hi[:, vx, k, :], lambda k: w_lo[:, vx, k, :]).then_inc(sem["g_pe"], 1)
                        pe.wait_ge(sem["g_act"], a0 + c + 1)
                        pe.wait_ge(sem["g_q"], i + 1)
                        for b in range(2):
                            for g in range(KC):
                                mm = pe.matmul(bank[4][:, g * P + b * CK:g * P + (b + 1) * CK], q_bd[:, 0, b, g, :],
                                               g_k[:, g, b * CK:(b + 1) * CK], start=True, stop=True)
                        mm.then_inc(sem["g_pe"], 1)
                    pe.wait_ge(sem["g_pool"], i + 1)
                    for c in range(NCH):
                        pe.wait_ge(sem["g_act"], a0 + NCH + 1 + c)
                        for g in range(KC):
                            mm = pe.transpose(bank[5][:, g * P:(g + 1) * P], g_s[:, c, g * P:(g + 1) * P], ident[:])
                        mm.then_inc(sem["g_pe"], 1)
                    pe.wait_ge(sem["g_act"], a0 + 2 * NCH + 1)
                    for b in range(2):
                        for g in range(KC):
                            for c in range(NCH):
                                mm = pe.matmul(bank[6 + b][:, g * P:(g + 1) * P], g_v[b * CK:(b + 1) * CK, c, g * P:(g + 1) * P],
                                               g_pt[b * CK:(b + 1) * CK, c, g * P:(g + 1) * P], start=(c == 0), stop=(c == NCH - 1))
                    mm.then_inc(sem["g_pe"], 1)
                pe.drain().then_inc(sem["t_mm"], 4 * NQ)
                pe.drain().then_inc(sem["n_mm"], 4 * NQ)
                pe.wait_ge(sem["t_ev"], 8 + 4 * NQ)
                pe.wait_ge(sem["n_ev"], 4 * NQ)
                pe.wait_ge(sem["o_lo"], NQ)
                for t in range(6):
                    product_n(("xo", t))
                turn(1, 0)
                turn(1, 1)
            pe.end_ifs()
            turn(1, 2)
            turn(1, 3)
            for m in range(KC):
                features(("aq", 0, m))
            pe.wait_ge(sem["o_lo"], NQ)
            product_n(("xo", 6))
            product_n(("xo", 7))
            turn(1, 4)
            turn(1, 5)

            for m in range(KC):
                features(("ak", 0, m))

            def self_scores(k):
                out_of_bank(pe, ("ak", k, KC - 1))
                for j in range(4):
                    ts = slice((4 * k + j) * P, (4 * k + j + 1) * P)
                    for c in range(KC):
                        mm = pe.matmul(bank[6 + k][:, j * P:(j + 1) * P], q_t[:, c, ts], k_t[:, c, ts],
                                       start=(c == 0), stop=(c == KC - 1))
                mm.then_inc(sem["a_mm"], 1)

            def self_output(t):
                pe.wait_ge(sem["a_tr"], 4 * (t // 4 + 1))
                out_of_bank(pe, ("av", t))
                if t < 2:
                    pe.wait_ge(sem["a_ext"], 2)
                else:
                    pe.wait_ge(sem["x_acc"], ACC_AT["at", t - 2])
                pe.matmul(bank[6 + t % 2][:], a_pt[:, t, :], v_n[:, t, :], start=True, stop=True).then_inc(sem["av_mm"], 1)

            turn(1, 6)
            turn(1, 7)
            features(("aq", 1, 0))
            self_scores(0)
            for m in range(1, KC):
                features(("aq", 1, m))
            for m in range(KC):
                features(("ak", 1, m))
            product_n(("av", 0))
            self_scores(1)
            for t in range(1, NT):
                product_n(("av", t))
                if t >= 3:
                    self_output(t - 3)
                if t >= 6:
                    turn(2, t - 6)
            for t in range(5, NT):
                self_output(t)
                turn(2, t - 3)
            turn(2, 5)

            for m in range(KC):
                features(("fq", 0, m))
                if m < 2:
                    turn(2, 6 + m)
            for m in range(KC):
                features(("fq", 1, m))
            pe.wait_ge(sem["wg_split"], 2)
            pe.wait_ge(sem["x_acc"], ACC_AT["at", NT - 1])
            for k in range(2):
                ts = slice(k * 512, (k + 1) * 512)
                mm = three_passes(bank[6 + k][:], lambda c: wg_hi[:, c, :], lambda c: wg_lo[:, c, :],
                                  lambda c: xt_hi[:, c, ts], lambda c: xt_lo[:, c, ts])
            mm.then_inc(sem["gate_mm"], 1)
            features(("fk", 0, 0))
            features(("fk", 0, 1))
            pe.wait_ge(sem["gate_ev"], 1)
            for t in range(NT):
                mm = pe.transpose(bank[6][:, t * E:(t + 1) * E], gate_t[:, t * P:(t + 1) * P], ident[0:E, 0:E])
            mm.then_inc(sem["gatet_mm"], 1)
            features(("fk", 0, 2))
            features(("fk", 0, 3))
            for m in range(KC):
                features(("fk", 1, m))
            pe.wait_ge(sem["comb_done"], 1)
            for t in range(NT):
                mm = pe.transpose(bank[6 + t // 4][0:E, t % 4 * P:(t % 4 + 1) * P], comb[:, t, :], ident[:])
            mm.then_inc(sem["combt_mm"], 1)
            product_n(("fv", 0))

            def self_heads(t):
                pe.wait_ge(sem["kbd_done"], t + 1)
                if t >= 1:
                    pe.wait_ge(sem["f_sub"], t)
                else:
                    pe.wait_ge(sem["xt_lo_done"], 3 * NT)
                for b in range(4):
                    for g in range(KC):
                        mm = pe.matmul(bank[4][b * S:(b + 1) * S, g * P:(g + 1) * P], q_t[:, g, t * P + b * S:t * P + (b + 1) * S],
                                       k_bd[:, t % 2, b, g, :], start=True, stop=True)
                mm.then_inc(sem["f_mm"], 1)

            def head_outputs(t):
                pe.wait_ge(sem["f_tr"], 4 * (t + 1))
                out_of_bank(pe, ("fv", NT - 1))
                if t >= 1:
                    pe.wait_ge(sem["x_acc"], ACC_AT["fa", t - 1])
                for hd in range(H):
                    mm = pe.matmul(bank[5][:, hd * DH:(hd + 1) * DH], f_pt[:, hd, :],
                                   v_n[:, t, hd * DH:(hd + 1) * DH], start=True, stop=True)
                mm.then_inc(sem["fv_mm"], 1)

            self_heads(0)
            pe.wait_ge(sem["combt_ev"], 2)
            pe.wait_ge(sem["bexp_in"], 16)
            for t in range(NT):
                if t >= 1:
                    product_n(("fv", t))
                if t >= 2:
                    pe.wait_ge(sem["x_acc"], ACC_AT["be", t - 2])
                pe.matmul(bank[6 + t % 2][:], comb_t[:, t * P:(t + 1) * P], b_exp[:], start=True, stop=True).then_inc(sem["be_mm"], 1)
            for e in range(E):
                for t in range(NT):
                    product_n(("ex", e, t))
                    if t == 5:
                        head_outputs(e)
                    if t == 6 and e + 1 < E:
                        self_heads(e + 1)

        @block.scalar
        def _(act):
            def split_w(w):
                n = W_AT[w]
                if n == 1:
                    act.wait_ge(sem["w1_in"], 16)
                else:
                    act.wait_ge(sem["w_in"], 16 * (n - 1))
                if W_BEFORE[n] is not None:
                    group_done(act, last_group(WEIGHTS[W_BEFORE[n]]))
                stage = w1_stage if n == 1 else w_stage
                act.activation(w_hi[:, W_SLOT[n]], stage[:], ACT.Copy).then_inc(sem["w_hi_done"], 1)

            def first_weight(c):
                act.wait_ge(sem[f"w0_in{c}"], 16)
                act.activation(w_hi[:, 0, c, :], w_stage[:, c, :], ACT.Copy).then_inc(sem["w0_hi_done"], 1)

            def split_c(q):
                act.wait_ge(sem["c_in"], 16 * q)
                if q >= 2:
                    group_done(act, ("xv", q - 2, 3))
                act.activation(c_hi[:, q % 2], c_stage[:], ACT.Copy).then_inc(sem["c_hi_done"], 1)

            def split_next(q):
                split_c(q + 2) if q + 2 < NQ else split_w("xo" if q + 2 == NQ else "aq")

            def turned_hi(s, t):
                act.wait_ge(sem["tr_done"], s * NT + t + 1)
                if s >= 1:
                    group_done(act, ({1: "xo", 2: "av"}[s], t))
                act.activation(xt_hi[:, :, t * P:(t + 1) * P], bank[4 + t % 2][:].rearrange("p (c n) -> p c n", c=KC),
                               ACT.Copy).then_inc(sem["xt_hi_done"], 1)

            def out_t(group, b, dst):
                _, half, m = group
                group_done(act, group)
                act.activation(dst[:, m, half * 512:(half + 1) * 512], bank[BANK[group]][:], ACT.Identity,
                               bias=bias_col[:, b, m:m + 1]).then_inc(sem["t_ev"], 1)

            def out_keys(q, m):
                group_done(act, ("xk", q, m))
                if q >= 1:
                    act.wait_ge(sem["s_mm"], 4 * q)
                act.activation(kq_t[:, m, :], bank[BANK["xk", q, m]][:], ACT.Identity, bias=bias_col[:, 1, m:m + 1]).then_inc(sem["t_ev"], 1)

            def exponentials(n):
                act.wait_ge(sem["s_sub"], n + 1)
                if n >= 2:
                    act.wait_ge(sem["pt_mm"], n - 1)
                act.activation(p_rows[:, n % 2, :], s_rows[:, n % 2, :], ACT.Exp, scale=SCALE).then_inc(sem["exp_done"], 1)

            def turned_probabilities(n):
                act.wait_ge(sem["pt_mm"], n + 1)
                if n >= 2:
                    act.wait_ge(sem["o_mm"], n - 1)
                act.activation(pt_x[:, n % 2, :], bank[4 + n % 2][:], ACT.Copy).then_inc(sem["pt_ev"], 1)

            def attend(q, between):
                n = 4 * q
                exponentials(n)
                exponentials(n + 1)
                between(0)
                between(1)
                split_next(q)
                turned_probabilities(n)
                exponentials(n + 2)
                between(2)
                turned_probabilities(n + 1)
                exponentials(n + 3)
                between(3)
                take_out(act, n, 0)
                turned_probabilities(n + 2)
                take_out(act, n + 1, 0)
                turned_probabilities(n + 3)
                between(6)
                take_out(act, n + 2, 0)
                between(7)
                take_out(act, n + 3, 0)
                ts = slice(q * 256, (q + 1) * 256)
                act.wait_ge(sem["o_act"], 4 * (q + 1))
                act.wait_ge(sem["o_dve"], 4 * (q + 1))
                act.activation(xt_hi[:, :, ts], o_t[:, :, ts], ACT.Copy).then_inc(sem["o_hi"], 1)

            act.wait_ge(sem["flag_done"], 1)
            general = act.value_load(flag_i[0:1, 0:1], min_val=0, max_val=1)
            with act.If(general == 0):
                for c in range(KC):
                    first_weight(c)
                    act.wait_ge(sem[f"c0_in{c}"], 16)
                    act.activation(c_hi[:, 0, c, :], c_stage[:, c, :], ACT.Copy).then_inc(sem["c0_hi_done"], 1)
                split_w("xv")
                act.wait_ge(sem["bias_in"], 32)
                for m in range(KC):
                    out_keys(0, m)
                split_w("xq")
                split_c(1)
                for t in range(4):
                    turned_hi(0, t)
                for m in range(KC):
                    out_t(("xq", 0, m), 0, q_t)
                    turned_hi(0, 4 + m)
                for m in range(KC):
                    out_t(("xq", 1, m), 0, q_t)
                for q in range(NQ - 1):
                    attend(q, lambda j: out_keys(q + 1, j) if j < KC else None)

                def between(j):
                    if j >= 6:
                        turned_hi(1, j - 6)
                attend(NQ - 1, between)
            with act.Else():
                act.sem_inc(sem["g_act"], 1)
                for c in range(KC):
                    first_weight(c)
                split_w("xv")
                act.wait_ge(sem["bias_in"], 32)
                split_w("xq")
                for t in range(NT):
                    turned_hi(0, t)
                for j in range(8):
                    m, half = j % 4, j // 4
                    act.wait_ge(sem["t_mm"], j + 1)
                    act.activation(q_t[:, m, half * 512:(half + 1) * 512], bank[j % 4][:], ACT.Identity,
                                   bias=bias_col[:, 0, m:m + 1]).then_inc(sem["t_ev"], 1)
                with act.Fori(0, NPAIR) as i:
                    p0 = i * PE_N + 1
                    for c in range(NCH):
                        act.wait_ge(sem["g_pe"], p0 + 3 * c + 1)
                        for m in range(KC):
                            ins = act.activation(g_k[:, m, :], bank[0][:, m * P:(m + 1) * P], ACT.Identity, bias=bias_col[:, 1, m:m + 1])
                        ins.then_inc(sem["g_act"], 1)
                    act.wait_ge(sem["g_dve"], i * DVE_N + 1 + NCH + 1)
                    act.activation(g_s[:], g_s[:], ACT.Exp, scale=SCALE).then_inc(sem["g_act"], 1)
                    for c in range(NCH):
                        act.wait_ge(sem["g_pe"], p0 + 3 * NCH + c + 1)
                        act.activation(g_pt[:, c, :], bank[5][:], ACT.Copy).then_inc(sem["g_act"], 1)
                    act.wait_ge(sem["g_pe"], p0 + PE_N)
                    for b in range(2):
                        for h in range(HG):
                            rows = slice(h * DH, (h + 1) * DH)
                            ins = act.activation(o_t[rows, :, bass.ds(i * 2 * S + b * S, S)],
                                                 bank[6 + b][rows, :].rearrange("p (g n) -> p g n", g=KC)[:, :, h * S:(h + 1) * S], ACT.Copy)
                    ins.then_inc(sem["g_act"], NCH)
                act.drain().then_inc(sem["t_ev"], 4 * NQ)
                act.wait_ge(sem["g_act"], NPAIR * ACT_N + 1)
                act.activation(xt_hi[:], o_t[:], ACT.Copy).then_inc(sem["o_hi"], NQ)
                split_w("xo")
                split_w("aq")
                turned_hi(1, 0)
                turned_hi(1, 1)
            act.end_ifs()
            turned_hi(1, 2)
            turned_hi(1, 3)
            split_w("ak")
            for m in range(KC):
                out_t(("aq", 0, m), 2, q_t)
            turned_hi(1, 4)
            turned_hi(1, 5)
            split_w("av")

            for m in range(KC):
                out_t(("ak", 0, m), 3, k_t)
            turned_hi(1, 6)
            turned_hi(1, 7)
            out_t(("aq", 1, 0), 2, q_t)

            def self_exponentials(k):
                act.wait_ge(sem["a_sub"], k + 1)
                ts = slice(4 * k, 4 * k + 4)
                act.activation(a_p[:, ts, :], a_s[:, ts, :], ACT.Exp, scale=ATTN_SCALE).then_inc(sem["a_exp"], 1)

            out_t(("aq", 1, 1), 2, q_t)
            self_exponentials(0)
            out_t(("aq", 1, 2), 2, q_t)
            out_t(("aq", 1, 3), 2, q_t)
            split_w("fq")
            for m in range(KC):
                out_t(("ak", 1, m), 3, k_t)
            split_w("fk")
            self_exponentials(1)
            for t in range(6):
                turned_hi(2, t)
            split_w("fv")

            for m in range(KC):
                out_t(("fq", 0, m), 4, q_t)
                if m < 2:
                    turned_hi(2, 6 + m)
            for m in range(KC):
                out_t(("fq", 1, m), 4, q_t)
            split_w(("ex", 0))
            for m in range(KC):
                out_t(("fk", 0, m), 5, k_t)
            act.wait_ge(sem["gate_v"], 1)
            act.activation(gate_x[:, :, 0:E], gate[:], ACT.Exp).then_inc(sem["gate_exp"], 1)
            for m in range(KC):
                out_t(("fk", 1, m), 5, k_t)
            split_w(("ex", 1))
            for e in range(E):
                act.wait_ge(sem["f_sub"], e + 1)
                if e >= 1:
                    act.wait_ge(sem["f_tr"], 4 * e)
                act.activation(f_p[:], f_s[:], ACT.Exp, scale=SCALE).then_inc(sem["f_exp"], 1)
                if e + 2 < E:
                    split_w(("ex", e + 2))

        @block.gpsimd
        def _(pool):
            pool.memset(power[:], -0.5).then_inc(sem["pow_set"], 1)

            def inv_std(s, ts):
                n = s * NT + ts.stop
                pool.wait_ge(sem["aggr_done"], n)
                k = ts.stop - ts.start
                pool.tensor_scalar(rstd[:, 0, ts], aggr[:, ts, 1], EPS, None, ALU.add).then_inc(sem["eps_done"], k)
                pool.wait_ge(sem["eps_done"], n)
                pool.tensor_tensor(rstd[:, 1, ts], rstd[:, 0, ts], power[:].broadcast_to([P, k]), ALU.pow).then_inc(sem["rstd_done"], k)

            def tile_std(s, t):
                inv_std(s, slice(t, t + 1))

            def split_w(w):
                n = W_AT[w]
                pool.wait_ge(sem["w_hi_done"], n)
                k = W_SLOT[n]
                stage = w1_stage if n == 1 else w_stage
                pool.tensor_tensor(w_lo[:, k], stage[:], w_hi[:, k].bitcast(F32), ALU.subtract).then_inc(sem["w_lo_done"], 1)

            def split_c(q):
                pool.wait_ge(sem["c_hi_done"], q)
                pool.tensor_tensor(c_lo[:, q % 2], c_stage[:], c_hi[:, q % 2].bitcast(F32), ALU.subtract).then_inc(sem["c_lo_done"], 1)

            def split_next(q):
                split_c(q + 2) if q + 2 < NQ else split_w("xo" if q + 2 == NQ else "aq")

            def block_queries(slot, col):
                for b in range(2):
                    ins = pool.tensor_tensor(q_bd[:, slot, b].rearrange("p g (h n) -> p g h n", h=HG),
                                             q_t[:, :, col(b)].unsqueeze(2).broadcast_to([P, KC, HG, S]),
                                             head_on[:].unsqueeze(1).unsqueeze(3).broadcast_to([P, KC, HG, S]), ALU.mult)
                return ins

            def queries(n):
                if n >= 4 * NQ:
                    return
                if n >= 2:
                    pool.wait_ge(sem["s_mm"], n - 1)
                block_queries(n % 2, lambda b: slice(n * 2 * S + b * S, n * 2 * S + (b + 1) * S)).then_inc(sem["qbd_done"], 1)

            def normalised(n):
                pool.wait_ge(sem["s_inv"], n + 1)
                r = p_rows[:, n % 2, :].rearrange("p (e k) -> p e k", k=CK)
                pool.tensor_tensor(r, r, row_inv[:, n % 2, 0:8].unsqueeze(2).broadcast_to([P, 8, CK]), ALU.mult).then_inc(sem["p_done"], 1)

            def output_low(q):
                ts = slice(q * 256, (q + 1) * 256)
                pool.wait_ge(sem["o_hi"], q + 1)
                pool.tensor_tensor(xt_lo[:, :, ts], o_t[:, :, ts], xt_hi[:, :, ts].bitcast(F32), ALU.subtract).then_inc(sem["o_lo"], 1)

            pool.wait_ge(sem["pow_set"], 1)
            pool.wait_ge(sem["flag_done"], 1)
            general = pool.value_load(flag_i[0:1, 0:1], min_val=0, max_val=1)
            with pool.If(general == 0):
                for c in range(KC):
                    pool.wait_ge(sem["c0_hi_done"], c + 1)
                    pool.tensor_tensor(c_lo[:, 0, c, :], c_stage[:, c, :], c_hi[:, 0, c, :].bitcast(F32), ALU.subtract).then_inc(sem["c0_lo_done"], 1)
                split_w("xv")
                inv_std(0, slice(0, NT))
                split_w("xq")
                split_c(1)
                pool.wait_ge(sem["bias_in"], 32)
                out_of_bank(pool, ("xq", 0, KC - 1))
                queries(0)
                queries(1)
                for q in range(NQ):
                    n = 4 * q
                    if q == NQ // 2:
                        out_of_bank(pool, ("xq", 1, KC - 1))
                    queries(n + 2)
                    queries(n + 3)
                    normalised(n)
                    normalised(n + 1)
                    split_next(q)
                    normalised(n + 2)
                    if q == NQ - 1:
                        tile_std(1, 0)
                        tile_std(1, 1)
                    normalised(n + 3)
                    if q == NQ - 1:
                        for t in range(2, 6):
                            tile_std(1, t)
                    if q == 1:
                        out_of_bank(pool, ("xq", 1, KC - 1))
                    queries(n + 4)
                    queries(n + 5)
                    output_low(q)
            with pool.Else():
                pool.sem_inc(sem["g_b"], 1)
                split_w("xv")
                inv_std(0, slice(0, NT))
                split_w("xq")
                pool.wait_ge(sem["bias_in"], 32)
                pool.wait_ge(sem["t_ev"], 8)
                with pool.Fori(0, NPAIR) as i:
                    pool.wait_ge(sem["g_pe"], i * PE_N + 1)
                    block_queries(0, lambda b: bass.ds(i * 2 * S + b * S, S)).then_inc(sem["g_q"], 1)
                    for c in range(NCH):
                        pool.wait_ge(sem["g_c_in"], 16 * (i * NCH + c + 1))
                        if c >= 1:
                            pool.wait_ge(sem["g_pe"], i * PE_N + 1 + 3 * c)
                        pool.tensor_tensor(g_chi[:], g_ctx[:], ones[:].unsqueeze(1).broadcast_to([P, KC, P]), ALU.mult).then_inc(sem["g_hi"], 1)
                        pool.wait_ge(sem["g_hi"], i * NCH + c + 1)
                        pool.tensor_tensor(g_clo[:], g_ctx[:], g_chi[:].bitcast(F32), ALU.subtract).then_inc(sem["g_b"], 1)
                    pool.wait_ge(sem["s_inv"], i + 1)
                    for c in range(NCH):
                        r = g_s[:, c, :].rearrange("p (e k) -> p e k", k=CK)
                        ins = pool.tensor_tensor(r, r, row_inv[:, 0, 0:8].unsqueeze(2).broadcast_to([P, 8, CK]), ALU.mult)
                    ins.then_inc(sem["g_pool"], 1)
                pool.wait_ge(sem["o_hi"], NQ)
                pool.tensor_tensor(xt_lo[:], o_t[:], xt_hi[:].bitcast(F32), ALU.subtract).then_inc(sem["o_lo"], NQ)
                split_w("xo")
                split_w("aq")
                for t in range(6):
                    tile_std(1, t)
            pool.end_ifs()
            split_w("ak")
            pool.memset(a_pt[:], 0.0).then_inc(sem["pt_zeroed"], 1)
            split_w("av")
            tile_std(1, 6)
            tile_std(1, 7)
            pool.memset(f_pt[:], 0.0).then_inc(sem["pt_zeroed"], 1)
            pool.memset(wg_hi[:].bitcast(F32), 0.0).then_inc(sem["pt_zeroed"], 1)
            pool.memset(wg_lo[:].bitcast(F32), 0.0).then_inc(sem["pt_zeroed"], 1)
            split_w("fq")
            split_w("fk")
            for t in range(NT):
                tile_std(2, t)
            split_w("fv")
            split_w(("ex", 0))

            def block_keys(t):
                if t >= 2:
                    pool.wait_ge(sem["f_mm"], t - 1)
                for b in range(4):
                    ts = slice(t * P + b * S, t * P + (b + 1) * S)
                    ins = pool.tensor_tensor(k_bd[:, t % 2, b].rearrange("p g (h n) -> p g h n", h=HG),
                                             k_t[:, :, ts].unsqueeze(2).broadcast_to([P, KC, HG, S]),
                                             head_on[:].unsqueeze(1).unsqueeze(3).broadcast_to([P, KC, HG, S]), ALU.mult)
                ins.then_inc(sem["kbd_done"], 1)

            out_of_bank(pool, ("fk", 0, KC - 1))
            block_keys(0)
            block_keys(1)
            split_w(("ex", 1))
            out_of_bank(pool, ("fk", 1, KC - 1))
            for e in range(E):
                if e + 2 < E:
                    split_w(("ex", e + 2))
                    block_keys(e + 2)

        @block.vector
        def _(dve):
            def statistics(s, t):
                if s == 0:
                    dve.wait_ge(sem["x_in"], 16 * NT)
                else:
                    dve.wait_ge(sem["x_acc"], ACC_AT[{1: "xo", 2: "at"}[s], t])
                n = s * NT + t
                dve.bn_stats(stats[:, t, :], x[:, t, :]).then_inc(sem["stats_done"], 1)
                dve.wait_ge(sem["stats_done"], n + 1)
                dve.bn_aggr(aggr[:, t, :], stats[:, t, :]).then_inc(sem["aggr_done"], 1)

            def scale(s, t):
                n = s * NT + t
                dve.wait_ge(sem["rstd_done"], n + 1)
                if t >= 2:
                    dve.wait_ge(sem["tr_done"], n - 1)
                xn = xn_0 if s == 0 else xn_1
                dve.tensor_scalar(xn[:, t % 2, :], x[:, t, :], aggr[:, t, 0:1], rstd[:, 1, t:t + 1],
                                  ALU.subtract, ALU.mult).then_inc(sem["xn_done"], 1)

            def low(s, t):
                n = s * NT + t
                dve.wait_ge(sem["xt_hi_done"], n + 1)
                ts = slice(t * P, (t + 1) * P)
                dve.tensor_tensor(xt_lo[:, :, ts], bank[4 + t % 2][:].rearrange("p (c n) -> p c n", c=KC),
                                  xt_hi[:, :, ts].bitcast(F32), ALU.subtract).then_inc(sem["xt_lo_done"], 1)

            def out_n(group, dst, row):
                group_done(dve, group)
                dve.tensor_tensor(dst[:, group[-1], :], bank[BANK[group]][:], row, ALU.add).then_inc(sem["n_ev"], 1)

            acc = []

            def add_to_x(what, src, factor=None):
                i, t = len(acc), what[-1]
                assert ACC[i] == what
                before = [j + 1 for j in range(i) if ACC[j][-1] == t]
                if before:
                    dve.wait_ge(sem["x_acc"], before[-1])
                if factor is None:
                    ins = dve.tensor_tensor(x[:, t, :], src, x[:, t, :], ALU.add)
                else:
                    ins = dve.scalar_tensor_tensor(x[:, t, :], src, factor, x[:, t, :], ALU.mult, ALU.add)
                ins.then_inc(sem["x_acc"], 1)
                acc.append(what)

            def x_with_bias():
                for t in range(NT):
                    ins = dve.tensor_tensor(x[:, t, :], x[:, t, :], bias_x[:, 1, :], ALU.add)
                ins.then_inc(sem["xb_done"], 1)

            def projected(t):
                group_done(dve, ("xo", t))
                add_to_x(("xo", t), bank[BANK["xo", t]][:])

            dve.memset(ones[:], 1.0).then_inc(sem["ones_set"], 1)
            dve.wait_ge(sem["masknat_in"], 16)
            dve.tensor_scalar(mask_on[:], mask_nat[:, 0:TAIL], 0.0, None, ALU.not_equal).then_inc(sem["maskn_done"], 1)
            dve.wait_ge(sem["maskn_done"], 1)
            dve.wait_ge(sem["ones_set"], 1)
            dve.tensor_reduce(any_col[0:B, :], mask_on[:], AX.X, ALU.max).then_inc(sem["flag_sum"], 1)
            dve.wait_ge(sem["flag_mm"], 1)
            dve.tensor_scalar(flag_i[:], bank[6][0:1, 0:1], 1.0, None, ALU.min).then_inc(sem["flag_done"], 1)
            dve.wait_ge(sem["flag_done"], 1)
            general = dve.value_load(flag_i[0:1, 0:1], min_val=0, max_val=1)
            for c in range(KC):
                dve.wait_ge(sem["w0_hi_done"], c + 1)
                dve.tensor_tensor(w_lo[:, 0, c, :], w_stage[:, c, :], w_hi[:, 0, c, :].bitcast(F32), ALU.subtract).then_inc(sem["w0_lo_done"], 1)
            for t in range(NT):
                statistics(0, t)
            scale(0, 0)
            scale(0, 1)
            dve.wait_ge(sem["biasx_in"], 16)

            def nan_for_no_key(n, first):
                dve.wait_ge(sem["maskn_done"], first)
                dve.tensor_scalar(nan_b[:, 1, 0:n], nan_b[:, 0, 0:n], 0.0, None, ALU.is_equal).then_inc(sem["maskn_done"], 1)
                dve.wait_ge(sem["maskn_done"], first + 1)
                dve.reciprocal(nan_b[:, 2, 0:n], nan_b[:, 1, 0:n]).then_inc(sem["maskn_done"], 1)
                dve.wait_ge(sem["maskn_done"], first + 2)
                dve.tensor_tensor(nan_b[:, 0, 0:n], nan_b[:, 1, 0:n], nan_b[:, 2, 0:n], ALU.mult).then_inc(sem["maskn_done"], 1)
                dve.wait_ge(sem["maskn_done"], first + 3)
                dve.tensor_scalar(nan_b[:, 1, 0:n], nan_b[:, 0, 0:n], -1.0, None, ALU.add).then_inc(sem["maskn_done"], 1)
                dve.wait_ge(sem["maskn_done"], first + 4)

            with dve.If(general == 0):
                def softmax_head(n):
                    srow = s_rows[:, n % 2, :]
                    dve.wait_ge(sem["s_mm"], n + 1)
                    if n >= 2:
                        dve.wait_ge(sem["exp_done"], n - 1)
                    dve.tensor_tensor(srow.rearrange("p (g k) -> p g k", g=KC), bank[4 + n % 2][:].rearrange("p (g k) -> p g k", g=KC),
                                      m_bias[:, n * P:(n + 1) * P].unsqueeze(1).broadcast_to([P, KC, P]), ALU.add).then_inc(sem["s_add"], 1)
                    dve.wait_ge(sem["s_add"], n + 1)
                    r = srow.rearrange("p (e k) -> p e k", k=CK)
                    dve.tensor_reduce(row_max[:, n % 2, 0:8], r, AX.X, ALU.max).then_inc(sem["s_max"], 1)
                    dve.wait_ge(sem["s_max"], n + 1)
                    dve.tensor_tensor(r, r, row_max[:, n % 2, 0:8].unsqueeze(2).broadcast_to([P, 8, CK]), ALU.subtract).then_inc(sem["s_sub"], 1)

                def softmax_sum(n):
                    dve.wait_ge(sem["exp_done"], n + 1)
                    if n >= 2:
                        dve.wait_ge(sem["p_done"], n - 1)
                    r = p_rows[:, n % 2, :].rearrange("p (e k) -> p e k", k=CK)
                    dve.tensor_reduce(row_sum[:, n % 2, 0:8], r, AX.X, ALU.add).then_inc(sem["s_sum"], 1)
                    dve.wait_ge(sem["s_sum"], n + 1)
                    dve.reciprocal(row_inv[:, n % 2, 0:8], row_sum[:, n % 2, 0:8]).then_inc(sem["s_inv"], 1)

                def out_values(q, p):
                    if q >= 1:
                        dve.wait_ge(sem["o_mm"], 4 * (q - 1) + p + 1)
                    group_done(dve, ("xv", q, p))
                    dve.tensor_tensor(vq_n[:, p, :], bank[BANK["xv", q, p]][:], bias_x[:, 0, :], ALU.add).then_inc(sem["n_ev"], 1)

                def attend(q, between):
                    n = 4 * q
                    softmax_head(n)
                    softmax_head(n + 1)
                    between(0)
                    softmax_sum(n)
                    softmax_head(n + 2)
                    between(1)
                    softmax_sum(n + 1)
                    softmax_head(n + 3)
                    between(2)
                    softmax_sum(n + 2)
                    between(3)
                    softmax_sum(n + 3)
                    take_out(dve, n, 1)
                    between(4)
                    take_out(dve, n + 1, 1)
                    between(5)
                    take_out(dve, n + 2, 1)
                    between(6)
                    take_out(dve, n + 3, 1)
                    between(7)

                out_values(0, 0)
                out_values(0, 1)
                low(0, 0)
                scale(0, 2)
                out_values(0, 2)
                low(0, 1)
                scale(0, 3)
                out_values(0, 3)
                for t in range(2, NT):
                    low(0, t)
                    if t + 2 < NT:
                        scale(0, t + 2)
                dve.wait_ge(sem["mask_in"], 16)
                dve.tensor_scalar(m_bias[:], mask_i[:], 0.0, MASKED, ALU.is_equal, ALU.mult).then_inc(sem["mbias_done"], 1)
                dve.wait_ge(sem["mbias_done"], 1)
                m3 = m_bias[:].rearrange("p (b k) -> p b k", k=CK)
                dve.tensor_reduce(nan_b[:, 0, :], m3, AX.X, ALU.max).then_inc(sem["maskn_done"], 1)
                nan_for_no_key(B, 2)
                dve.tensor_tensor(m3, m3, nan_b[:, 1, :].unsqueeze(2).broadcast_to([P, B, CK]), ALU.add).then_inc(sem["mbias_done"], 1)
                dve.wait_ge(sem["mbias_done"], 2)
                for q in range(NQ - 1):
                    attend(q, lambda j: out_values(q + 1, j - KC) if j >= KC else None)
                    if q == 0:
                        x_with_bias()

                def between(j):
                    if j < 6:
                        if j == 0:
                            dve.wait_ge(sem["xb_done"], 1)
                        projected(j)
                        statistics(1, j)
                        if j == 4:
                            scale(1, 0)
                            scale(1, 1)
                    else:
                        low(1, j - 6)
                        scale(1, j - 4)
                attend(NQ - 1, between)
            with dve.Else():
                dve.sem_inc(sem["g_dve"], 1)
                for t in range(NT):
                    low(0, t)
                    if t + 2 < NT:
                        scale(0, t + 2)
                with dve.Fori(0, NPAIR) as i:
                    p0 = i * PE_N + 1
                    dve.wait_ge(sem["g_m_in"], 16 * (i + 1))
                    dve.tensor_scalar(g_bias[:], g_mask[:], 0.0, MASKED, ALU.is_equal, ALU.mult).then_inc(sem["mbias_done"], 1)
                    dve.wait_ge(sem["mbias_done"], i * 2 + 1)
                    for b in range(2):
                        dve.tensor_reduce(nan_b[:, 0, b:b + 1], g_bias[:, :, b * CK:(b + 1) * CK], AX.XY, ALU.max).then_inc(sem["maskn_done"], 1)
                    nan_for_no_key(2, i * 6 + 3)
                    for b in range(2):
                        gb = g_bias[:, :, b * CK:(b + 1) * CK]
                        ins = dve.tensor_scalar(gb, gb, nan_b[:, 1, b:b + 1], None, ALU.add)
                    ins.then_inc(sem["mbias_done"], 1)
                    dve.wait_ge(sem["mbias_done"], i * 2 + 2)
                    dve.wait_ge(sem["g_act"], i * ACT_N + 1)
                    for c in range(NCH):
                        dve.wait_ge(sem["g_pe"], p0 + 3 * c + 2)
                        dve.tensor_tensor(g_v[:, c, :], bank[1][:], bias_x[:, 0, :], ALU.add).then_inc(sem["s_add"], 1)
                        dve.wait_ge(sem["g_pe"], p0 + 3 * c + 3)
                        dve.tensor_tensor(g_s[:, c, :].rearrange("p (g k) -> p g k", g=KC), bank[4][:].rearrange("p (g k) -> p g k", g=KC),
                                          g_bias[:, c, :].unsqueeze(1).broadcast_to([P, KC, P]), ALU.add).then_inc(sem["g_dve"], 1)
                    dve.wait_ge(sem["g_dve"], i * DVE_N + 1 + NCH)
                    r = g_s[:].rearrange("p c (e k) -> p e c k", k=CK)
                    dve.tensor_reduce(row_max[:, 0, 0:8], r, AX.XY, ALU.max).then_inc(sem["s_max"], 1)
                    dve.wait_ge(sem["s_max"], i + 1)
                    for c in range(NCH):
                        rc = g_s[:, c, :].rearrange("p (e k) -> p e k", k=CK)
                        ins = dve.tensor_tensor(rc, rc, row_max[:, 0, 0:8].unsqueeze(2).broadcast_to([P, 8, CK]), ALU.subtract)
                    ins.then_inc(sem["g_dve"], 1)
                    dve.wait_ge(sem["g_act"], i * ACT_N + 1 + NCH + 1)
                    dve.tensor_reduce(row_sum[:, 0, 0:8], r, AX.XY, ALU.add).then_inc(sem["s_sum"], 1)
                    dve.wait_ge(sem["s_sum"], i + 1)
                    dve.reciprocal(row_inv[:, 0, 0:8], row_sum[:, 0, 0:8]).then_inc(sem["s_inv"], 1)
                dve.drain().then_inc(sem["n_ev"], 4 * NQ)
                x_with_bias()
                dve.wait_ge(sem["xb_done"], 1)
                del acc[:]
                for t in range(6):
                    projected(t)
                    statistics(1, t)
                scale(1, 0)
                scale(1, 1)
                low(1, 0)
                scale(1, 2)
                low(1, 1)
                scale(1, 3)
            dve.end_ifs()
            low(1, 2)
            scale(1, 4)
            low(1, 3)
            scale(1, 5)
            projected(6)
            statistics(1, 6)
            projected(7)
            statistics(1, 7)
            low(1, 4)
            scale(1, 6)
            low(1, 5)
            scale(1, 7)
            low(1, 6)
            low(1, 7)

            def self_softmax_head(k):
                ts = slice(4 * k, 4 * k + 4)
                dve.wait_ge(sem["a_mm"], k + 1)
                for b in range(4):
                    rows = slice(b * S, (b + 1) * S)
                    ins = dve.tensor_copy(a_s[rows, ts, :], bank[6 + k][rows, :].rearrange("p (t n) -> p t n", t=4)[:, :, b * S:(b + 1) * S])
                ins.then_inc(sem["a_ext"], 1)
                dve.wait_ge(sem["a_ext"], k + 1)
                dve.tensor_reduce(row_max[:, 0, ts], a_s[:, ts, :], AX.X, ALU.max).then_inc(sem["a_max"], 1)
                dve.wait_ge(sem["a_max"], k + 1)
                dve.tensor_tensor(a_s[:, ts, :], a_s[:, ts, :], row_max[:, 0, ts].unsqueeze(2).broadcast_to([P, 4, S]), ALU.subtract).then_inc(sem["a_sub"], 1)

            def self_softmax_sum(k):
                ts = slice(4 * k, 4 * k + 4)
                dve.wait_ge(sem["a_exp"], k + 1)
                dve.tensor_reduce(row_sum[:, 0, ts], a_p[:, ts, :], AX.X, ALU.add).then_inc(sem["a_sum"], 1)
                dve.wait_ge(sem["a_sum"], k + 1)
                dve.reciprocal(row_inv[:, 0, ts], row_sum[:, 0, ts]).then_inc(sem["a_inv"], 1)
                dve.wait_ge(sem["a_inv"], k + 1)
                dve.tensor_tensor(a_p[:, ts, :], a_p[:, ts, :], row_inv[:, 0, ts].unsqueeze(2).broadcast_to([P, 4, S]), ALU.mult).then_inc(sem["a_norm"], 1)
                dve.wait_ge(sem["a_norm"], k + 1)
                dve.wait_ge(sem["pt_zeroed"], 1)
                for b in range(4):
                    rows = slice(b * S, (b + 1) * S)
                    dve.transpose(a_pt[rows, ts, b * S:(b + 1) * S], a_p[rows, ts, :]).then_inc(sem["a_tr"], 1)

            self_softmax_head(0)
            self_softmax_sum(0)
            dve.wait_ge(sem["gate_in"], 32)
            dve.wait_ge(sem["pt_zeroed"], 4)
            dve.tensor_copy(wg_hi[:, :, 0:E], g_stage[:]).then_inc(sem["wg_split"], 1)
            dve.wait_ge(sem["wg_split"], 1)
            dve.tensor_tensor(wg_lo[:, :, 0:E], g_stage[:], wg_hi[:, :, 0:E].bitcast(F32), ALU.subtract).then_inc(sem["wg_split"], 1)
            dve.memset(gate_x[:], -1.0).then_inc(sem["gx_set"], 1)
            dve.memset(top2[:], -1.0).then_inc(sem["gx_set"], 1)
            dve.wait_ge(sem["biasf_in"], 16)
            out_n(("av", 0), v_n, bias_f[:, 0, :])
            self_softmax_head(1)
            out_n(("av", 1), v_n, bias_f[:, 0, :])
            self_softmax_sum(1)

            def self_added(t):
                dve.wait_ge(sem["av_mm"], t + 1)
                add_to_x(("at", t), bank[6 + t % 2][:])

            for t in range(2, NT + 4):
                if t < NT:
                    out_n(("av", t), v_n, bias_f[:, 0, :])
                if 3 <= t < NT + 3:
                    self_added(t - 3)
                    statistics(2, t - 3)
                if t >= 4:
                    scale(2, t - 4)
                if t >= 6:
                    low(2, t - 6)
            low(2, 6)
            low(2, 7)

            step = []

            def then_wait(ins):
                step.append(1)
                ins.then_inc(sem["gate_step"], 1)
                dve.wait_ge(sem["gate_step"], len(step))

            dve.wait_ge(sem["gate_mm"], 1)
            for k in range(2):
                ins = dve.tensor_scalar(gate_t[:, k * 512:(k + 1) * 512], bank[6 + k][0:E, :], b_gate[:, 0:1], None, ALU.add)
            ins.then_inc(sem["gate_ev"], 1)
            dve.wait_ge(sem["gatet_mm"], 1)
            lg = bank[6][:, 0:NT * E].rearrange("p (t e) -> p t e", e=E)
            then_wait(dve.tensor_reduce(row_max[:, 0, 0:NT], lg, AX.X, ALU.max))
            dve.wait_ge(sem["gx_set"], 2)
            dve.tensor_tensor(gate[:], lg, row_max[:, 0, 0:NT].unsqueeze(2).broadcast_to([P, NT, E]), ALU.subtract).then_inc(sem["gate_v"], 1)
            dve.wait_ge(sem["gate_exp"], 1)
            gx = gate_x[:, :, 0:E]
            then_wait(dve.tensor_reduce(row_sum[:, 0, 0:NT], gx, AX.X, ALU.add))
            then_wait(dve.reciprocal(row_inv[:, 0, 0:NT], row_sum[:, 0, 0:NT]))
            then_wait(dve.tensor_tensor(gx, gx, row_inv[:, 0, 0:NT].unsqueeze(2).broadcast_to([P, NT, E]), ALU.mult))
            for t in range(NT):
                ins = dve.max(top[:, t, :], gate_x[:, t, 0:E])
            then_wait(ins)
            then_wait(dve.tensor_copy(top2[:, :, 0:2], top[:, :, 0:2]))
            for t in range(NT):
                ins = dve.match_replace(gate_r[:, t, :], top2[:, t, :], gate_x[:, t, :], 0.0)
            then_wait(ins)
            dve.tensor_tensor(comb[:], gx, gate_r[:, :, 0:E], ALU.subtract).then_inc(sem["comb_done"], 1)
            dve.wait_ge(sem["combt_mm"], 1)
            for k in range(2):
                dve.tensor_copy(comb_t[:, k * 512:(k + 1) * 512], bank[6 + k][0:E, :]).then_inc(sem["combt_ev"], 1)

            def heads_softmax_head(t):
                dve.wait_ge(sem["f_mm"], t + 1)
                s3 = bank[4][:].rearrange("p (e k) -> p e k", k=S)
                dve.tensor_reduce(row_max[:, 0, :], s3, AX.X, ALU.max).then_inc(sem["f_max"], 1)
                dve.wait_ge(sem["f_max"], t + 1)
                if t >= 1:
                    dve.wait_ge(sem["f_exp"], t)
                dve.tensor_tensor(f_s[:], s3, row_max[:, 0, :].unsqueeze(2).broadcast_to([P, H, S]), ALU.subtract).then_inc(sem["f_sub"], 1)

            def heads_softmax_sum(t):
                dve.wait_ge(sem["f_exp"], t + 1)
                dve.tensor_reduce(row_sum[:, 0, :], f_p[:], AX.X, ALU.add).then_inc(sem["f_sum"], 1)
                dve.wait_ge(sem["f_sum"], t + 1)
                dve.reciprocal(row_inv[:, 0, :], row_sum[:, 0, :]).then_inc(sem["f_inv"], 1)
                dve.wait_ge(sem["f_inv"], t + 1)
                dve.tensor_tensor(f_p[:], f_p[:], row_inv[:, 0, :].unsqueeze(2).broadcast_to([P, H, S]), ALU.mult).then_inc(sem["f_norm"], 1)

            def heads_turned(t):
                dve.wait_ge(sem["f_norm"], t + 1)
                dve.wait_ge(sem["pt_zeroed"], 2)
                if t >= 1:
                    dve.wait_ge(sem["fv_mm"], t)
                for b in range(4):
                    rows = slice(b * S, (b + 1) * S)
                    dve.transpose(f_pt[rows, :, b * S:(b + 1) * S], f_p[rows, :, :]).then_inc(sem["f_tr"], 1)

            for t in range(NT):
                out_n(("fv", t), v_n, bias_f[:, 1, :])
                dve.wait_ge(sem["be_mm"], t + 1)
                add_to_x(("be", t), bank[6 + t % 2][:])
            dve.wait_ge(sem["comb_done"], 1)

            def expert_added(e, t):
                group_done(dve, ("ex", e, t))
                add_to_x(("ex", e, t), bank[BANK["ex", e, t]][:], comb[:, t, e:e + 1])

            for e in range(E):
                heads_softmax_head(e)
                expert_added(e, 0)
                heads_softmax_sum(e)
                expert_added(e, 1)
                heads_turned(e)
                for t in range(2, 6):
                    expert_added(e, t)
                dve.wait_ge(sem["fv_mm"], e + 1)
                add_to_x(("fa", e), bank[5][:])
                expert_added(e, 6)
                expert_added(e, 7)


def _kernel_arrays(x, ctx_1024, mask, Wxq, bxq, Wxk, bxk, Wxv, bxv, Wxo, bxo, Waq, baq, Wak, bak, Wav, bav,
                   W_qkv, b_qkv, W_gate, b_gate, W_experts, b_experts):
    def rows(w):
        return w.reshape(KC, P, -1).transpose(1, 0, 2)

    ws = [w.T for w in (Wxk, Wxv, Wxq, Wxo, Waq, Wak, Wav)] + [W_qkv[:, i * D:(i + 1) * D] for i in range(3)] + list(W_experts)
    slots = np.concatenate([np.arange(1, PAD + 1), np.arange(SK)])
    chunks = ctx_1024[:, slots].reshape(NPAIR, 2, NCH, CK, KC, P).transpose(0, 2, 5, 4, 1, 3)
    m = np.concatenate([np.zeros((B, PAD), mask.dtype), mask.reshape(B, SK)], axis=1)
    cols = np.stack([bxq, bxk, baq, bak, b_qkv[0:D], b_qkv[D:2 * D]])
    c = np.ascontiguousarray
    return {
        "x_in_dram": c(x.reshape(TOK, D)),
        "ctx_tail_dram": c(ctx_1024[:, TAIL:].reshape(NQ, 8 * CK, KC, P).transpose(0, 3, 2, 1)),
        "ctx_all_dram": c(chunks).reshape(NPAIR * NCH, P, KC, P),
        "mask_dram": c(mask.reshape(B, SK)),
        "mask_tail_dram": c(mask.reshape(B, SK)[:, TAIL:]).reshape(1, B * CK),
        "mask_all_dram": c(m.reshape(NPAIR, 2, NCH, CK).transpose(0, 2, 1, 3)).reshape(NPAIR, NCH * P),
        "weights_dram": c(np.stack([rows(w) for w in ws])),
        "bias_col_dram": c(cols.reshape(6, KC, P).transpose(2, 0, 1)),
        "bias_row_dram": c(np.stack([bxv, bxo, bav, b_qkv[2 * D:]]))[None],
        "w_gate_dram": c(rows(W_gate)),
        "b_gate_dram": c(b_gate[:, None]),
        "b_experts_dram": c(b_experts),
        "ident_dram": np.eye(P, dtype=np.float32),
        "head_on_dram": np.repeat(np.eye(HG, dtype=np.float32), DH, axis=0),
    }


def kernel(**inputs):
    import concourse.bacc as bacc
    from concourse.bass_utils import run_bass_kernel_spmd

    nc = bacc.Bacc("TRN2", target_bir_lowering=False, num_devices=1)
    names = ["x", "ctx_1024", "mask_Bx1xS2_ik0"] + [f"L0_xattn_{n}" for n in "Wq bq Wk bk Wv bv Wo bo".split()] \
        + [f"L0_attn_{n}" for n in "Wq bq Wk bk Wv bv".split()] \
        + [f"L0_ffn_{n}" for n in "W_qkv b_qkv W_gate b_gate W_experts b_experts".split()]
    arrays = _kernel_arrays(*[np.asarray(inputs[n]) for n in names])
    args = [nc.dram_tensor(n, a.shape, mybir.dt.from_np(a.dtype), kind="ExternalInput").ap() for n, a in arrays.items()]
    out = nc.dram_tensor("out_dram", (TOK, D), F32, kind="ExternalOutput").ap()
    perceiver_kernel(nc, *args, out)
    r = run_bass_kernel_spmd(nc, [arrays], core_ids=[0])
    return r.results[0]["out_dram"].reshape(B, S, D)
```

```python
from contextlib import ExitStack

import numpy as np

import concourse.bass as bass
from concourse import mybir

F32 = mybir.dt.float32
F32R = mybir.dt.float32r
BF16 = mybir.dt.bfloat16
I32 = mybir.dt.int32
ALU = mybir.AluOpType
ACT = mybir.ActivationFunctionType
AX = mybir.AxisListType

B, S, SK, D, H, E = 32, 32, 257, 512, 16, 8
P = 128
TOK = B * S
NT = TOK // P
KC = D // P
DH = D // H
HG = P // DH
CK = 64
NCH = -(-SK // CK)
PAD = NCH * CK - SK
TAIL = SK - CK
NPAIR = B // 2
NQ = 4
SCALE = float(DH) ** -0.5
ATTN_SCALE = float(S) ** -0.5
EPS = 1e-5
MASKED = -1.0e30

KB = 1024
NW = 18
NSLOT = 3
WARM = 2
EXPERT_TILES = 3
CAPACITY = EXPERT_TILES * P
NR = E * EXPERT_TILES
BACK_AT = [(0,), (1,), (2, 3), (4,), (5,), (6, 7), (), ()]
ADDED_AT = {5: (3,), 6: (4,), 7: (5, 6, 7)}
POOL_TILES = 3
FAR = 2 * NR * P


def perceiver_kernel(nc, x_d, ctx_tail_d, ctx_all_d, mask_d, mask_tail_d, mask_all_d, w_d, bias_col_d,
                     bias_row_d, w_gate_d, b_gate_d, b_exp_d, ident_d, head_on_d, before_d, count_d, first_row_d,
                     token_d, xn_rows_d, y_rows_d, out_d):
    ctx = ExitStack()
    with ctx:
        base = -(-nc.sbuf_base // 64) * 64
        arena = ctx.enter_context(nc.sbuf_tensor("arena", [P, 208 * KB - 256], mybir.dt.uint8))
        del arena

        def sb(name, kb, shape, dt=F32):
            return nc.alloc_sbuf_tensor_at(name, shape, dt, offset=base + int(kb * KB))

        w_stage = sb("w_stage", 0, [P, KC, D])
        w1_stage = sb("w1_stage", 72, [P, KC, D])
        w_hi = sb("w_hi", 8, [P, NSLOT, KC, D], F32R)
        w_lo = sb("w_lo", 32, [P, NSLOT, KC, D], F32R)
        x = sb("x", 56, [P, NT, D])
        xt_hi = sb("xt_hi", 72, [P, KC, TOK], F32R)
        xt_lo = sb("xt_lo", 88, [P, KC, TOK], F32R)
        warm = sb("warm", 88, [P, D])
        o_t = sb("o_t", 88, [P, KC, TOK])
        q_t = sb("q_t", 104, [P, KC, TOK])
        k_t = sb("k_t", 120, [P, KC, TOK])
        kq_t = sb("kq_t", 120, [P, KC, 512])
        s_rows = sb("s_rows", 128, [P, 2, 512])
        p_rows = sb("p_rows", 132, [P, 2, 512])
        v_n = sb("v_n", 136, [P, NT, D])
        vq_n = sb("vq_n", 136, [P, 4, D])
        pt_x = sb("pt_x", 144, [P, 2, 512])
        bias_x = sb("bias_x", 148, [P, 2, D])
        c_hi = sb("c_hi", 152, [P, 2, KC, 512], F32R)
        c_lo = sb("c_lo", 168, [P, 2, KC, 512], F32R)
        c_stage = sb("c_stage", 184, [P, KC, 512])
        mask_i = sb("mask_i", 128, [P, B * CK], I32)
        q_bd = sb("q_bd", 192, [P, 2, 2, KC, P])
        m_bias = sb("m_bias", 200, [P, B * CK], BF16)
        bias_f = sb("bias_f", 200, [P, 2, D])
        ident = sb("ident", 204, [P, P])
        bias_col = sb("bias_col", 204.5, [P, 6, KC])
        stats = sb("stats", 204.625, [P, NT, 6])
        aggr = sb("aggr", 204.875, [P, NT, 2])
        rstd = sb("rstd", 205, [P, 2, NT])
        power = sb("power", 205.0625, [P, 1])
        row_max = sb("row_max", 205.125, [P, 2, 16])
        row_sum = sb("row_sum", 205.25, [P, 2, 16])
        row_inv = sb("row_inv", 205.375, [P, 2, 16])
        table_on = sb("table_on", 206.5, [P, 1])
        nan_b = sb("nan_b", 205.5, [P, 3, B])
        flag_i = sb("flag_i", 206, [1, 1], I32)
        ones = sb("ones", 206.0625, [P, 1])
        any_col = sb("any_col", 206.125, [P, 1])
        b_gate = sb("b_gate", 206.1875, [E, 1])
        head_on = sb("head_on", 206.25, [P, HG])
        mask_nat = sb("mask_nat", 144, [B, SK], I32)
        mask_on = sb("mask_on", 146, [B, TAIL])
        g_ctx = sb("g_ctx", 184, [P, KC, P])
        g_mask = sb("g_mask", 186, [P, NCH, P], I32)
        g_bias = sb("g_bias", 189, [P, NCH, P])
        g_chi = sb("g_chi", 128, [P, KC, P], F32R)
        g_clo = sb("g_clo", 130, [P, KC, P], F32R)
        g_k = sb("g_k", 120, [P, KC, P])
        g_s = sb("g_s", 152, [P, NCH, 512])
        g_pt = sb("g_pt", 162, [P, NCH, 512])
        g_v = sb("g_v", 172, [P, NCH, D])
        xn_0 = sb("xn_0", 144, [P, 2, D])
        xn_1 = sb("xn_1", 152, [P, 2, D])
        xn_2 = sb("xn_2", 152, [P, 4, D])
        a_s = sb("a_s", 160, [P, NT, S])
        a_p = sb("a_p", 161, [P, NT, S])
        a_pt = sb("a_pt", 162, [P, NT, P])
        f_s = sb("f_s", 170, [P, H, S])
        f_p = sb("f_p", 172, [P, H, S])
        f_pt = [sb("f_pt0", 166, [P, H, S]), sb("f_pt1", 168, [P, H, S])]
        gate = sb("gate", 174, [P, NT, E])
        gate_x = sb("gate_x", 174.25, [P, NT, 16])
        gate_r = sb("gate_r", 174.75, [P, NT, 16])
        top = sb("top", 175.25, [P, NT, 8])
        top2 = sb("top2", 175.5, [P, NT, 8])
        comb = sb("comb", 175.75, [P, NT, E])
        gate_t = sb("gate_t", 176, [E, TOK])
        b_exp = sb("b_exp", 160, [P, 2, D])
        g_stage = sb("g_stage", 182, [P, KC, E])
        k_bd = sb("k_bd", 184, [P, 2, 4, KC, P])
        wg_hi = sb("wg_hi", 184, [P, KC, P], F32R)
        wg_lo = sb("wg_lo", 186, [P, KC, P], F32R)
        sel = sb("sel", 180, [P, NT, E])
        sums = [sb("sums0", 180.25, [P, NT, E]), sb("sums1", 180.5, [P, NT, E])]
        ahead = sb("ahead", 180.75, [P, NT + 1, E])
        row_e = sb("row_e", 181.25, [P, NT, E])
        from_far = sb("from_far", 181.5, [P, NT, E])
        or_zero = sb("or_zero", 181.75, [P, NT, E])
        part = sb("part", 182.25, [P, 2, NT, E])
        row_f = sb("row_f", 182.75, [P, NT, 2])
        row_i = sb("row_i", 182.8125, [P, NT, 2], I32)
        low_i = sb("low_i", 182.875, [P, NT, 2], I32)
        high_i = sb("high_i", 182.9375, [P, NT, 2], I32)
        low_f = sb("low_f", 183, [P, NT, 2])
        high_f = sb("high_f", 183.0625, [P, NT, 2])
        share = sb("share", 183.125, [P, 2, NT])
        token = sb("token", 183.25, [P, NT])
        row_token = sb("row_token", 183.375, [P, NR], I32)
        most = sb("most", 183.5, [1, 1])
        crowded_i = sb("crowded_i", 183.5625, [1, 1], I32)
        before = sb("before", 172, [P, P])
        all_on = sb("all_on", 172.5, [P, P])
        count = sb("count", 173, [P, P])
        first_row = sb("first_row", 173.5, [P, NT, E])
        at_low = sb("at_low", 192, [P, NT, 2, P])
        at_high = sb("at_high", 188, [P, NT, 2, NR])
        g_rows = sb("g_rows", 136, [P, 4, D])
        gt_hi = sb("gt_hi", 144, [P, 2, KC, P], F32R)
        gt_lo = sb("gt_lo", 148, [P, 2, KC, P], F32R)
        y_rows = sb("y_rows", 152, [P, 4, D])
        e_stage = sb("e_stage", 184, [P, KC, D])
        back = [sb(f"back{i}", kb, [P, 4, D]) for i, kb in enumerate((8, 24, 32, 48))]

        bank = [ctx.enter_context(nc.psum_tensor(f"bank{i}", [P, 512], F32)) for i in range(8)]

        names = """x_in0 x_in1 ident_in bias_in biasx_in biasf_in mask_in masknat_in maskn_done gate_in bexp_in
            w0_in0 w0_in1 w0_in2 w0_in3 c0_in0 c0_in1 c0_in2 c0_in3 w0_hi_done w0_lo_done c0_hi_done c0_lo_done
            w1_in e_in w_in w_hi_done w_lo_done c_in c_hi_done c_lo_done g_hi pow_set stats_done aggr_done eps_done
            rstd_done xn_done tr_done xt_hi_done xt_lo_done t_mm t_ev n_mm n_ev
            flag_sum flag_mm flag_done mbias_done ones_set xb_done pt_zeroed gx_set
            qbd_done s_mm s_add s_max s_sub exp_done s_sum s_inv p_done pt_mm pt_ev o_mm o_act o_dve
            o_hi o_lo
            a_mm a_ext a_max a_sub a_exp a_sum a_inv a_norm a_tr av_mm x_acc
            gate_mm gate_ev gatet_mm gate_v gate_exp comb_done gate_step wg_split
            route_in all_on_set sel_done row_mm crowded_set rows_done placed_done place_mm row_token_done share_done
            gt_mm gt_hi_done gt_lo_done y_ev y_added be_in0 be_in1 xn_out0 xn_out1 xn_out2 xn_out3
            g_in0 g_in1 g_in2 g_in3 y_out0 y_out1 y_out2 y_out3 x_final
            back_in0 back_in1 back_in2 back_in3 back_in4 back_in5 back_in6 back_in7 fa_added v_ev y_scaled y_first table_loaded warm_set warm_mm x_last
            kbd_done f_mm f_max f_sub f_exp f_sum f_inv f_norm f_tr fv_mm
            g_c_in g_m_in g_pe g_act g_dve g_pool g_q g_b done_out""".split()
        sem = {n: ctx.enter_context(nc.semaphore(n)) for n in names}

        WEIGHTS = ["xk", "xv", "xq", "xo", "aq", "ak", "av", "fq", "fk"] + [("ex", e) for e in range(E)] + ["fv"]
        W_AT = {w: n for n, w in enumerate(WEIGHTS)}
        W_SLOT = [0, 1, 2, 2, 0, 1, 2, 0, 1] + [(e + 2) % NSLOT for e in range(E)] + [1]
        W_BEFORE = [max((m for m in range(n) if W_SLOT[m] == W_SLOT[n]), default=None) for n in range(NW)]

        STAGE_2 = range(W_AT["ex", 3], NW, 2)

        def staged(n):
            if n == 1:
                return w1_stage, sem["w1_in"], 16
            if n in STAGE_2:
                return e_stage, sem["e_in"], 16 * (STAGE_2.index(n) + 1)
            return w_stage, sem["w_in"], 16 * sum(m not in STAGE_2 for m in range(2, n + 1))

        GROUPS = [("xk", 0, m) for m in range(KC)] + [("xv", 0, p) for p in range(4)]
        GROUPS += [("xq", h, m) for h in range(2) for m in range(KC)]
        for q in range(1, NQ):
            GROUPS += [("xk", q, m) for m in range(KC)] + [("xv", q, p) for p in range(4)]
        GROUPS += [("xo", t) for t in range(6)] + [("aq", 0, m) for m in range(KC)] + [("xo", 6), ("xo", 7)]
        GROUPS += [("ak", 0, m) for m in range(KC)] + [(w, 1, m) for w in ("aq", "ak") for m in range(KC)]
        GROUPS += [("av", t) for t in range(NT)]
        GROUPS += [("fq", 0, m) for m in range(KC)] + [("fk", 0, 0)] + [("fq", 1, m) for m in range(KC)]
        GROUPS += [("fk", 0, m) for m in range(1, KC)] + [("fk", 1, m) for m in range(KC)]
        BANK = {g: i % 4 for i, g in enumerate(GROUPS)}
        T_FORM = ("xk", "xq", "aq", "ak", "fq", "fk")
        T_GROUPS = [g for g in GROUPS if g[0] in T_FORM]
        N_GROUPS = [g for g in GROUPS if g[0] not in T_FORM]
        FFN_MM = len(N_GROUPS)
        V_GROUPS = [g for g in N_GROUPS if g[0] in ("xv", "av")]
        MM_AT = {g: i + 1 for gs in (T_GROUPS, N_GROUPS) for i, g in enumerate(gs)}

        ACC = [("xo", t) for t in range(NT)] + [("at", t) for t in range(NT)]
        ACC_AT = {a: i + 1 for i, a in enumerate(ACC)}

        FREED = {g: ("t_ev", i + 1) for i, g in enumerate(T_GROUPS)}
        FREED |= {g: ("n_ev", i + 1) for i, g in enumerate(V_GROUPS)}
        FREED |= {g: ("x_acc", ACC_AT[g]) for g in N_GROUPS if g[0] == "xo"}

        def evacuated(eng, group):
            i = GROUPS.index(group)
            if i >= 4:
                name, value = FREED[GROUPS[i - 4]]
                eng.wait_ge(sem[name], value)

        def group_done(eng, group):
            eng.wait_ge(sem["t_mm" if group[0] in T_FORM else "n_mm"], MM_AT[group])

        def out_of_bank(eng, group):
            name, value = FREED[group]
            eng.wait_ge(sem[name], value)

        def last_group(w):
            return [g for g in GROUPS if g[0] == w][-1]

        def slot_free(eng, n, tiles):
            m = W_BEFORE[n]
            if m is not None and WEIGHTS[m][0] == "ex":
                eng.wait_ge(sem["n_mm"], FFN_MM + tiles * (WEIGHTS[m][1] + 1))
            elif m is not None:
                group_done(eng, last_group(WEIGHTS[m]))

        PE_N, ACT_N, DVE_N = 4 * NCH + 1, 3 * NCH + 1, NCH + 1

        def xn_rows(s, t):
            return xn_2[:, t % 4, :] if s == 2 else (xn_0, xn_1)[s][:, t % 2, :]

        def take_out(eng, n, b):
            eng.wait_ge(sem["o_mm"], n + 1)
            dst = o_t[:, :, n * 2 * S + b * S:n * 2 * S + (b + 1) * S]
            src = bank[6 + b][:, 0:KC * S].rearrange("p (g n) -> p g n", g=KC)
            ins = eng.activation(dst, src, ACT.Copy) if b == 0 else eng.tensor_copy(dst, src)
            ins.then_inc(sem["o_act" if b == 0 else "o_dve"], 1)

        block = ctx.enter_context(nc.Block())

        @block.sync
        def _(sp):
            def load_w(n):
                if n == 2:
                    sp.wait_ge(sem["w0_lo_done"], KC)
                elif n == STAGE_2[0]:
                    sp.wait_ge(sem["place_mm"], 1)
                else:
                    sp.wait_ge(sem["w_lo_done"], n - 2 if n > STAGE_2[0] else n - 1)
                stage, loaded, _ = staged(n)
                sp.dma_start(stage[:], w_d[n]).then_inc(loaded, 16)

            def load_c(q):
                if q == 1:
                    sp.wait_ge(sem["c0_lo_done"], KC)
                else:
                    sp.wait_ge(sem["c_lo_done"], q - 1)
                sp.dma_start(c_stage[:], ctx_tail_d[q]).then_inc(sem["c_in"], 16)

            sp.dma_start(mask_nat[:], mask_d).then_inc(sem["masknat_in"], 16)
            for c in range(KC):
                sp.dma_start(w_stage[:, c, :], w_d[0, :, c, :]).then_inc(sem[f"w0_in{c}"], 16)
                sp.dma_start(c_stage[:, c, :], ctx_tail_d[0, :, c, :]).then_inc(sem[f"c0_in{c}"], 16)
            sp.dma_start(w1_stage[:], w_d[1]).then_inc(sem["w1_in"], 16)
            for t in range(NT):
                sp.dma_start(x[:, t, :], x_d[t * P:(t + 1) * P, :]).then_inc(sem[f"x_in{t // 4}"], 16)
            sp.dma_start(ident[:], ident_d).then_inc(sem["ident_in"], 16)
            sp.dma_start(bias_col[:], bias_col_d).then_inc(sem["bias_in"], 16)
            sp.dma_start(head_on[:], head_on_d).then_inc(sem["bias_in"], 16)
            load_w(2)
            sp.dma_start(bias_x[:], bias_row_d[0:1, 0:2, :].broadcast_to([P, 2, D])).then_inc(sem["biasx_in"], 16)
            sp.dma_start(mask_i[:], mask_tail_d.broadcast_to([P, B * CK])).then_inc(sem["mask_in"], 16)
            sp.dma_start(b_gate[:], b_gate_d).then_inc(sem["gate_in"], 16)
            sp.wait_ge(sem["flag_done"], 1)
            general = sp.value_load(flag_i[0:1, 0:1], min_val=0, max_val=1)
            with sp.If(general == 0):
                load_c(1)
                load_c(2)
                load_c(3)
                load_w(3)
            with sp.Else():
                for c in range(KC):
                    sp.wait_ge(sem[f"c0_in{c}"], 16)
                with sp.Fori(0, NPAIR) as i:
                    sp.wait_ge(sem["g_dve"], i * DVE_N + 1)
                    sp.dma_start(g_mask[:], mask_all_d[bass.ds(i, 1), :].broadcast_to([P, NCH * P])).then_inc(sem["g_m_in"], 16)
                    for c in range(NCH):
                        sp.wait_ge(sem["g_b"], i * NCH + c + 1)
                        sp.dma_start(g_ctx[:], ctx_all_d[bass.ds(i * NCH + c, 1)]).then_inc(sem["g_c_in"], 16)
                load_w(3)
            sp.end_ifs()
            load_w(W_AT["aq"])
            load_w(W_AT["ak"])
            sp.wait_ge(sem["o_lo"], NQ)
            sp.dma_start(bias_f[:], bias_row_d[0:1, 2:4, :].broadcast_to([P, 2, D])).then_inc(sem["biasf_in"], 16)
            sp.dma_start(g_stage[:], w_gate_d).then_inc(sem["gate_in"], 16)
            for dst, src in ((before, before_d), (count, count_d.broadcast_to([P, P])), (token, token_d),
                             (first_row, first_row_d.broadcast_to([P, NT, E]))):
                sp.dma_start(dst[:], src).then_inc(sem["route_in"], 16)
            for n in range(W_AT["ak"] + 1, W_AT["ex", 0] + 1):
                load_w(n)
            for t in range(NT):
                sp.wait_ge(sem["xn_done"], 2 * NT + t + 1)
                sp.dma_start(xn_rows_d[t * P:(t + 1) * P, :], xn_2[:, t % 4, :]).then_inc(sem[f"xn_out{t % 4}"], 16)
            load_w(W_AT["ex", 1])
            load_w(W_AT["ex", 2])

            def load_expert_bias(e, tiles):
                if e >= 2:
                    sp.wait_ge(sem["y_ev"], tiles * (e - 1))
                sp.dma_start(b_exp[:, e % 2, :], b_exp_d[e:e + 1, :].broadcast_to([P, D])).then_inc(sem[f"be_in{e % 2}"], 16)

            sp.wait_ge(sem["av_mm"], NT)
            load_expert_bias(0, 0)
            load_expert_bias(1, 0)
            sp.wait_ge(sem["crowded_set"], 1)
            crowded = sp.value_load(crowded_i[0:1, 0:1], min_val=0, max_val=1)
            load_w(W_AT["ex", 3])
            with sp.If(crowded == 0):
                for i in range(NR):
                    sp.wait_ge(sem["y_ev"], i + 1)
                    sp.dma_start(y_rows_d[i * P:(i + 1) * P, :], y_rows[:, i % 4, :]).then_inc(sem[f"y_out{i % 4}"], 16)
                    e, j = divmod(i, EXPERT_TILES)
                    if j == 0 and e + 4 <= E:
                        load_w(W_AT["ex", 4] + e)
                    if j == 0 and 1 <= e < E - 1:
                        load_expert_bias(e + 1, EXPERT_TILES)
            with sp.Else():
                for e in range(4, E + 1):
                    load_w(W_AT["ex", 0] + e)
                    load_expert_bias(e - 2, NT)
                load_expert_bias(E - 1, NT)
            sp.end_ifs()
            for t in range(NT):
                if t < POOL_TILES:
                    sp.wait_ge(sem["x_final"], t + 1)
                else:
                    sp.wait_ge(sem["x_last"], t + 1 - POOL_TILES)
                sp.dma_start(out_d[t * P:(t + 1) * P, :], x[:, t, :]).then_inc(sem["done_out"], 16)
            sp.wait_ge(sem["done_out"], 16 * NT)

        @block.tensor
        def _(pe):
            def three_passes(out, l_hi, l_lo, r_hi, r_lo):
                for c in range(KC):
                    pe.matmul(out, l_hi(c), r_hi(c), start=(c == 0), stop=False)
                    pe.matmul(out, l_hi(c), r_lo(c), start=False, stop=False)
                    mm = pe.matmul(out, l_lo(c), r_hi(c), start=False, stop=(c == KC - 1))
                return mm

            def weight_ready(w):
                if W_AT[w] == 0:
                    pe.wait_ge(sem["w0_lo_done"], KC)
                else:
                    pe.wait_ge(sem["w_lo_done"], W_AT[w])
                return W_SLOT[W_AT[w]]

            def product_t(group, r_hi, r_lo):
                w, _, m = group
                k = weight_ready(w)
                evacuated(pe, group)
                ms = slice(m * P, (m + 1) * P)
                three_passes(bank[BANK[group]][:], lambda c: w_hi[:, k, c, ms], lambda c: w_lo[:, k, c, ms],
                             r_hi, r_lo).then_inc(sem["t_mm"], 1)

            def features(group):
                ts = slice(group[1] * 512, (group[1] + 1) * 512)
                pe.wait_ge(sem["xt_lo_done"], NT * {"xq": 0, "aq": 1, "ak": 1, "fq": 2, "fk": 2}[group[0]] + 4 * (group[1] + 1))
                product_t(group, lambda c: xt_hi[:, c, ts], lambda c: xt_lo[:, c, ts])

            def product_n(group):
                k = weight_ready(group[0])
                evacuated(pe, group)
                ts = slice(group[-1] * P, (group[-1] + 1) * P)
                three_passes(bank[BANK[group]][:], lambda c: xt_hi[:, c, ts], lambda c: xt_lo[:, c, ts],
                             lambda c: w_hi[:, k, c, :], lambda c: w_lo[:, k, c, :]).then_inc(sem["n_mm"], 1)

            def turn(s, t):
                n = s * NT + t
                pe.wait_ge(sem["xn_done"], n + 1)
                if t >= 2:
                    pe.wait_ge(sem["xt_lo_done"], n - 1)
                rows = xn_rows(s, t)
                for c in range(KC):
                    mm = pe.transpose(bank[4 + t % 2][:, c * P:(c + 1) * P], rows[:, c * P:(c + 1) * P], ident[:])
                mm.then_inc(sem["tr_done"], 1)

            def first_keys():
                for c in range(KC):
                    pe.wait_ge(sem["w0_lo_done"], c + 1)
                    pe.wait_ge(sem["c0_lo_done"], c + 1)
                    for m in range(KC):
                        out, ms = bank[BANK["xk", 0, m]][:], slice(m * P, (m + 1) * P)
                        pe.matmul(out, w_hi[:, 0, c, ms], c_hi[:, 0, c, :], start=(c == 0), stop=False)
                        pe.matmul(out, w_hi[:, 0, c, ms], c_lo[:, 0, c, :], start=False, stop=False)
                        mm = pe.matmul(out, w_lo[:, 0, c, ms], c_hi[:, 0, c, :], start=False, stop=(c == KC - 1))
                        if c == KC - 1:
                            mm.then_inc(sem["t_mm"], 1)

            def keys(q, m):
                pe.wait_ge(sem["c_lo_done"], q)
                product_t(("xk", q, m), lambda c: c_hi[:, q % 2, c, :], lambda c: c_lo[:, q % 2, c, :])

            def values(q, p):
                group = ("xv", q, p)
                k = weight_ready("xv")
                evacuated(pe, group)
                ps = slice(p * P, (p + 1) * P)
                three_passes(bank[BANK[group]][:], lambda c: c_hi[:, q % 2, c, ps], lambda c: c_lo[:, q % 2, c, ps],
                             lambda c: w_hi[:, k, c, :], lambda c: w_lo[:, k, c, :]).then_inc(sem["n_mm"], 1)

            def scores(n):
                q, p = divmod(n, 4)
                out_of_bank(pe, ("xk", q, KC - 1))
                pe.wait_ge(sem["qbd_done"], n + 1)
                if p >= 2:
                    pe.wait_ge(sem["s_add"], n - 1)
                elif n >= 2:
                    pe.wait_ge(sem["pt_ev"], n - 1)
                else:
                    pe.wait_ge(sem["xt_lo_done"], NT)
                for b in range(2):
                    for g in range(KC):
                        mm = pe.matmul(bank[4 + n % 2][:, g * P + b * CK:g * P + (b + 1) * CK], q_bd[:, n % 2, b, g, :],
                                       kq_t[:, g, p * P + b * CK:p * P + (b + 1) * CK], start=True, stop=True)
                mm.then_inc(sem["s_mm"], 1)

            def probabilities(n):
                pe.wait_ge(sem["p_done"], n + 1)
                if n % 4 < 2:
                    pe.wait_ge(sem["s_add"], n + 3)
                else:
                    pe.wait_ge(sem["pt_ev"], n - 1)
                for g in range(KC):
                    mm = pe.transpose(bank[4 + n % 2][:, g * P:(g + 1) * P], p_rows[:, n % 2, g * P:(g + 1) * P], ident[:])
                mm.then_inc(sem["pt_mm"], 1)

            def outputs(n):
                q, p = divmod(n, 4)
                pe.wait_ge(sem["pt_ev"], n + 1)
                out_of_bank(pe, ("xv", q, p))
                if n >= 1:
                    pe.wait_ge(sem["o_act"], n)
                    pe.wait_ge(sem["o_dve"], n)
                for g in range(KC):
                    for h in range(HG):
                        for b in range(2):
                            rows, cols = slice(b * CK, (b + 1) * CK), slice(g * P + h * DH, g * P + (h + 1) * DH)
                            mm = pe.matmul(bank[6 + b][h * DH:(h + 1) * DH, g * S:(g + 1) * S], vq_n[rows, p, cols],
                                           pt_x[rows, n % 2, cols], start=True, stop=True)
                mm.then_inc(sem["o_mm"], 1)

            def attend(q, between):
                n = 4 * q
                scores(n)
                scores(n + 1)
                between(0)
                scores(n + 2)
                scores(n + 3)
                between(1)
                between(2)
                probabilities(n)
                between(3)
                probabilities(n + 1)
                between(4)
                outputs(n)
                probabilities(n + 2)
                between(5)
                outputs(n + 1)
                probabilities(n + 3)
                between(6)
                outputs(n + 2)
                between(7)
                outputs(n + 3)

            pe.wait_ge(sem["flag_sum"], 1)
            pe.matmul(bank[6][0:1, 0:1], any_col[0:B, :], ones[0:B, :], start=True, stop=True).then_inc(sem["flag_mm"], 1)
            pe.wait_ge(sem["flag_done"], 1)
            general = pe.value_load(flag_i[0:1, 0:1], min_val=0, max_val=1)
            with pe.If(general == 0):
                pe.wait_ge(sem["warm_set"], 1)
                for _ in range(WARM):
                    mm = pe.matmul(bank[7][:], warm[:, 0:P], warm[:], start=True, stop=True)
                mm.then_inc(sem["warm_mm"], 1)
                first_keys()
                pe.wait_ge(sem["ident_in"], 16)
                values(0, 0)
                turn(0, 0)
                turn(0, 1)
                values(0, 1)
                turn(0, 2)
                turn(0, 3)
                values(0, 2)
                turn(0, 4)
                values(0, 3)
                for m in range(KC):
                    features(("xq", 0, m))
                    if m < 3:
                        turn(0, 5 + m)
                for m in range(KC):
                    features(("xq", 1, m))
                for q in range(NQ - 1):
                    attend(q, lambda j: keys(q + 1, j) if j < KC else values(q + 1, j - KC))

                def between(j):
                    if j < 5:
                        pe.wait_ge(sem["o_lo"], j // 2 + 1)
                        product_n(("xo", j))
                    elif j >= 6:
                        pe.wait_ge(sem["pt_ev"], 4 * NQ - 7 + j)
                        turn(1, j - 6)
                attend(NQ - 1, between)
            with pe.Else():
                pe.sem_inc(sem["g_pe"], 1)
                pe.wait_ge(sem["ident_in"], 16)
                for t in range(NT):
                    turn(0, t)
                kx, vx, qx = (W_SLOT[W_AT[w]] for w in ("xk", "xv", "xq"))
                pe.wait_ge(sem["w_lo_done"], W_AT["xq"])
                pe.wait_ge(sem["w0_lo_done"], KC)
                pe.wait_ge(sem["xt_lo_done"], NT)
                for j in range(8):
                    ms, ts = slice(j % 4 * P, (j % 4 + 1) * P), slice(j // 4 * 512, (j // 4 + 1) * 512)
                    if j >= 4:
                        pe.wait_ge(sem["t_ev"], j - 3)
                    three_passes(bank[j % 4][:], lambda c: w_hi[:, qx, c, ms], lambda c: w_lo[:, qx, c, ms],
                                 lambda c: xt_hi[:, c, ts], lambda c: xt_lo[:, c, ts]).then_inc(sem["t_mm"], 1)
                pe.wait_ge(sem["t_ev"], 8)
                with pe.Fori(0, NPAIR) as i:
                    p0, a0, d0 = i * PE_N + 1, i * ACT_N + 1, i * DVE_N + 1
                    for c in range(NCH):
                        pe.wait_ge(sem["g_b"], i * NCH + c + 2)
                        pe.wait_ge(sem["g_dve"], d0 + c)
                        if c == 0:
                            pe.wait_ge(sem["g_act"], a0)
                        for m in range(KC):
                            ms = slice(m * P, (m + 1) * P)
                            mm = three_passes(bank[0][:, ms], lambda k: w_hi[:, kx, k, ms], lambda k: w_lo[:, kx, k, ms],
                                              lambda k: g_chi[:, k, :], lambda k: g_clo[:, k, :])
                        mm.then_inc(sem["g_pe"], 1)
                        three_passes(bank[1][:], lambda k: g_chi[:, k, :], lambda k: g_clo[:, k, :],
                                     lambda k: w_hi[:, vx, k, :], lambda k: w_lo[:, vx, k, :]).then_inc(sem["g_pe"], 1)
                        pe.wait_ge(sem["g_act"], a0 + c + 1)
                        pe.wait_ge(sem["g_q"], i + 1)
                        for b in range(2):
                            for g in range(KC):
                                mm = pe.matmul(bank[4][:, g * P + b * CK:g * P + (b + 1) * CK], q_bd[:, 0, b, g, :],
                                               g_k[:, g, b * CK:(b + 1) * CK], start=True, stop=True)
                        mm.then_inc(sem["g_pe"], 1)
                    pe.wait_ge(sem["g_pool"], i + 1)
                    for c in range(NCH):
                        pe.wait_ge(sem["g_act"], a0 + NCH + 1 + c)
                        for g in range(KC):
                            mm = pe.transpose(bank[5][:, g * P:(g + 1) * P], g_s[:, c, g * P:(g + 1) * P], ident[:])
                        mm.then_inc(sem["g_pe"], 1)
                    pe.wait_ge(sem["g_act"], a0 + 2 * NCH + 1)
                    for b in range(2):
                        for g in range(KC):
                            for c in range(NCH):
                                mm = pe.matmul(bank[6 + b][:, g * P:(g + 1) * P], g_v[b * CK:(b + 1) * CK, c, g * P:(g + 1) * P],
                                               g_pt[b * CK:(b + 1) * CK, c, g * P:(g + 1) * P], start=(c == 0), stop=(c == NCH - 1))
                    mm.then_inc(sem["g_pe"], 1)
                pe.drain().then_inc(sem["t_mm"], 4 * NQ)
                pe.drain().then_inc(sem["n_mm"], 4 * NQ)
                pe.wait_ge(sem["t_ev"], 8 + 4 * NQ)
                pe.wait_ge(sem["n_ev"], 4 * NQ)
                pe.wait_ge(sem["o_lo"], NQ)
                for t in range(5):
                    product_n(("xo", t))
                turn(1, 0)
                turn(1, 1)
            pe.end_ifs()
            turn(1, 2)
            turn(1, 3)
            product_n(("xo", 5))
            for m in range(KC):
                features(("aq", 0, m))
            pe.wait_ge(sem["o_lo"], NQ)
            product_n(("xo", 6))
            product_n(("xo", 7))
            turn(1, 4)
            turn(1, 5)

            for m in range(KC):
                features(("ak", 0, m))
                if m in (1, 2):
                    turn(1, 5 + m)

            def self_scores(k):
                out_of_bank(pe, ("ak", k, KC - 1))
                for j in range(4):
                    ts = slice((4 * k + j) * P, (4 * k + j + 1) * P)
                    for c in range(KC):
                        mm = pe.matmul(bank[6 + k][:, j * P:(j + 1) * P], q_t[:, c, ts], k_t[:, c, ts],
                                       start=(c == 0), stop=(c == KC - 1))
                mm.then_inc(sem["a_mm"], 1)

            def self_output(t):
                pe.wait_ge(sem["a_tr"], 4 * (t // 4 + 1))
                out_of_bank(pe, ("av", t))
                if t < 2:
                    pe.wait_ge(sem["a_ext"], 2)
                else:
                    pe.wait_ge(sem["x_acc"], ACC_AT["at", t - 2])
                pe.matmul(bank[6 + t % 2][:], a_pt[:, t, :], v_n[:, t, :], start=True, stop=True).then_inc(sem["av_mm"], 1)

            features(("aq", 1, 0))
            self_scores(0)
            for m in range(1, KC):
                features(("aq", 1, m))
            for m in range(KC):
                features(("ak", 1, m))
            product_n(("av", 0))
            self_scores(1)
            for t in range(1, NT):
                product_n(("av", t))
                if t >= 3:
                    self_output(t - 3)
                if t >= 6:
                    turn(2, t - 6)
            for t in range(5, NT):
                self_output(t)
                if t < NT - 1:
                    turn(2, t - 3)

            for m in range(KC):
                features(("fq", 0, m))
                turn(2, 4 + m)
            features(("fk", 0, 0))
            pe.wait_ge(sem["wg_split"], 2)
            pe.wait_ge(sem["xt_lo_done"], 3 * NT)
            pe.wait_ge(sem["x_acc"], ACC_AT["at", NT - 1])
            for k in range(2):
                ts = slice(k * 512, (k + 1) * 512)
                mm = three_passes(bank[6 + k][:], lambda c: wg_hi[:, c, :], lambda c: wg_lo[:, c, :],
                                  lambda c: xt_hi[:, c, ts], lambda c: xt_lo[:, c, ts])
            mm.then_inc(sem["gate_mm"], 1)
            features(("fq", 1, 0))
            pe.wait_ge(sem["gate_ev"], 1)
            for t in range(NT):
                mm = pe.transpose(bank[6][:, t * E:(t + 1) * E], gate_t[:, t * P:(t + 1) * P], ident[0:E, 0:E])
            mm.then_inc(sem["gatet_mm"], 1)
            for m in range(1, KC):
                features(("fq", 1, m))
            pe.wait_ge(sem["sel_done"], 1)
            pe.wait_ge(sem["route_in"], 64)
            pe.wait_ge(sem["all_on_set"], 1)
            rows = bank[6][:, NT * E:2 * NT * E]
            pe.matmul(rows, all_on[:], ahead[:, 0:NT, :], start=True, stop=False)
            pe.matmul(rows, before[:], sel[:], start=False, stop=True)
            pe.matmul(bank[6][:, 2 * NT * E:(2 * NT + 1) * E], all_on[:], ahead[:, NT, :], start=True, stop=True).then_inc(sem["row_mm"], 1)
            features(("fk", 0, 1))
            features(("fk", 0, 2))
            pe.wait_ge(sem["placed_done"], 2)
            for t in range(NT):
                for k in range(2):
                    mm = pe.matmul(bank[7][:, 0:NR], at_low[:, t, k, :], at_high[:, t, k, :],
                                   start=(t == 0 and k == 0), stop=(t == NT - 1 and k == 1))
            mm.then_inc(sem["place_mm"], 1)
            features(("fk", 0, 3))
            for m in range(KC):
                features(("fk", 1, m))

            def self_heads(t):
                pe.wait_ge(sem["kbd_done"], t + 1)
                if t >= 2:
                    pe.wait_ge(sem["f_sub"], t - 1)
                for g in range(KC):
                    for b in range(4):
                        mm = pe.matmul(bank[6 + t % 2][b * S:(b + 1) * S, g * P:(g + 1) * P], q_t[:, g, t * P + b * S:t * P + (b + 1) * S],
                                       k_bd[:, t % 2, b, g, :], start=True, stop=True)
                mm.then_inc(sem["f_mm"], 1)

            def head_outputs(t):
                pe.wait_ge(sem["f_tr"], t + 1)
                pe.wait_ge(sem["v_ev"], t + 1)
                if t >= 2:
                    pe.wait_ge(sem["fa_added"], t - 1)
                for hd in range(H):
                    for b in range(4):
                        rows, cols = slice(b * S, (b + 1) * S), slice(hd * DH, (hd + 1) * DH)
                        mm = pe.matmul(bank[4 + t % 2][rows, cols], f_pt[t % 2][rows, hd, :], v_n[rows, t, cols], start=True, stop=True)
                mm.then_inc(sem["fv_mm"], 1)

            def next_bank(i):
                if i < 4:
                    pe.wait_ge(sem["t_ev"], len(T_GROUPS))
                else:
                    pe.wait_ge(sem["y_ev"], i - 3)
                return bank[i % 4][:]

            def routed_turn(i):
                pe.wait_ge(sem[f"g_in{i % 4}"], 16 * (i // 4 + 1))
                if i >= 2:
                    pe.wait_ge(sem["gt_lo_done"], i - 1)
                for c in range(KC):
                    mm = pe.transpose(bank[4 + i % 2][:, c * P:(c + 1) * P], g_rows[:, i % 4, c * P:(c + 1) * P], ident[:])
                mm.then_inc(sem["gt_mm"], 1)

            def heads(n):
                for t in range(NT + 1):
                    if t < NT:
                        k = weight_ready("fv")
                        if t < 4:
                            pe.wait_ge(sem["y_ev"], n + t - 3)
                        else:
                            pe.wait_ge(sem["v_ev"], t - 3)
                        out = bank[t % 4][:]
                        ts = slice(t * P, (t + 1) * P)
                        three_passes(out, lambda c: xt_hi[:, c, ts], lambda c: xt_lo[:, c, ts],
                                     lambda c: w_hi[:, k, c, :], lambda c: w_lo[:, k, c, :]).then_inc(sem["n_mm"], 1)
                    if t + 2 < NT:
                        self_heads(t + 2)
                    if t >= 1:
                        head_outputs(t - 1)

            pe.wait_ge(sem["crowded_set"], 1)
            crowded = pe.value_load(crowded_i[0:1, 0:1], min_val=0, max_val=1)
            with pe.If(crowded == 0):
                routed_turn(0)
                routed_turn(1)
                for i in range(NR):
                    k = weight_ready(("ex", i // EXPERT_TILES))
                    out = next_bank(i)
                    pe.wait_ge(sem["gt_lo_done"], i + 1)
                    three_passes(out, lambda c: gt_hi[:, i % 2, c, :], lambda c: gt_lo[:, i % 2, c, :],
                                 lambda c: w_hi[:, k, c, :], lambda c: w_lo[:, k, c, :]).then_inc(sem["n_mm"], 1)
                    if i + 2 < NR:
                        routed_turn(i + 2)
                    if i in (NR - 4, NR - 2):
                        self_heads((i + 4 - NR) // 2)
                heads(NR)
            with pe.Else():
                for i in range(E * NT):
                    k = weight_ready(("ex", i // NT))
                    out = next_bank(i)
                    ts = slice(i % NT * P, (i % NT + 1) * P)
                    three_passes(out, lambda c: xt_hi[:, c, ts], lambda c: xt_lo[:, c, ts],
                                 lambda c: w_hi[:, k, c, :], lambda c: w_lo[:, k, c, :]).then_inc(sem["n_mm"], 1)
                self_heads(0)
                self_heads(1)
                heads(E * NT)
            pe.end_ifs()

        @block.scalar
        def _(act):
            def split_w(w, tiles=0):
                n = W_AT[w]
                stage, loaded, value = staged(n)
                act.wait_ge(loaded, value)
                slot_free(act, n, tiles)
                act.activation(w_hi[:, W_SLOT[n]], stage[:], ACT.Copy).then_inc(sem["w_hi_done"], 1)

            def first_weight(c):
                act.wait_ge(sem[f"w0_in{c}"], 16)
                act.activation(w_hi[:, 0, c, :], w_stage[:, c, :], ACT.Copy).then_inc(sem["w0_hi_done"], 1)

            def split_c(q):
                act.wait_ge(sem["c_in"], 16 * q)
                if q >= 2:
                    group_done(act, ("xv", q - 2, 3))
                act.activation(c_hi[:, q % 2], c_stage[:], ACT.Copy).then_inc(sem["c_hi_done"], 1)

            def split_next(q):
                split_c(q + 2) if q + 2 < NQ else split_w("xo" if q + 2 == NQ else "aq")

            def turned_hi(s, t):
                act.wait_ge(sem["tr_done"], s * NT + t + 1)
                if s >= 1:
                    group_done(act, ({1: "xo", 2: "av"}[s], t))
                act.activation(xt_hi[:, :, t * P:(t + 1) * P], bank[4 + t % 2][:].rearrange("p (c n) -> p c n", c=KC),
                               ACT.Copy).then_inc(sem["xt_hi_done"], 1)

            def out_t(group, b, dst):
                _, half, m = group
                group_done(act, group)
                act.activation(dst[:, m, half * 512:(half + 1) * 512], bank[BANK[group]][:], ACT.Identity,
                               bias=bias_col[:, b, m:m + 1]).then_inc(sem["t_ev"], 1)

            def out_keys(q, m):
                group_done(act, ("xk", q, m))
                if q >= 1:
                    act.wait_ge(sem["s_mm"], 4 * q)
                act.activation(kq_t[:, m, :], bank[BANK["xk", q, m]][:], ACT.Identity, bias=bias_col[:, 1, m:m + 1]).then_inc(sem["t_ev"], 1)

            def exponentials(n):
                act.wait_ge(sem["s_sub"], n + 1)
                if n >= 2:
                    act.wait_ge(sem["pt_mm"], n - 1)
                act.activation(p_rows[:, n % 2, :], s_rows[:, n % 2, :], ACT.Exp, scale=SCALE).then_inc(sem["exp_done"], 1)

            def turned_probabilities(n):
                act.wait_ge(sem["pt_mm"], n + 1)
                if n >= 2:
                    act.wait_ge(sem["o_mm"], n - 1)
                act.activation(pt_x[:, n % 2, :], bank[4 + n % 2][:], ACT.Copy).then_inc(sem["pt_ev"], 1)

            def attend(q, between):
                n = 4 * q
                exponentials(n)
                exponentials(n + 1)
                between(0)
                between(1)
                split_next(q)
                turned_probabilities(n)
                exponentials(n + 2)
                between(2)
                turned_probabilities(n + 1)
                exponentials(n + 3)
                between(3)
                take_out(act, n, 0)
                turned_probabilities(n + 2)
                take_out(act, n + 1, 0)
                turned_probabilities(n + 3)
                between(6)
                take_out(act, n + 2, 0)
                between(7)
                take_out(act, n + 3, 0)
                ts = slice(q * 256, (q + 1) * 256)
                act.wait_ge(sem["o_act"], 4 * (q + 1))
                act.wait_ge(sem["o_dve"], 4 * (q + 1))
                act.activation(xt_hi[:, :, ts], o_t[:, :, ts], ACT.Copy).then_inc(sem["o_hi"], 1)

            act.wait_ge(sem["ones_set"], 1)
            act.activation(table_on[:], ones[:], ACT.Exp).then_inc(sem["table_loaded"], 1)

            act.wait_ge(sem["flag_done"], 1)
            general = act.value_load(flag_i[0:1, 0:1], min_val=0, max_val=1)
            with act.If(general == 0):
                for c in range(KC):
                    first_weight(c)
                    act.wait_ge(sem[f"c0_in{c}"], 16)
                    act.activation(c_hi[:, 0, c, :], c_stage[:, c, :], ACT.Copy).then_inc(sem["c0_hi_done"], 1)
                split_w("xv")
                act.wait_ge(sem["bias_in"], 32)
                for m in range(KC):
                    out_keys(0, m)
                turned_hi(0, 0)
                turned_hi(0, 1)
                split_w("xq")
                turned_hi(0, 2)
                turned_hi(0, 3)
                turned_hi(0, 4)
                split_c(1)
                for m in range(KC):
                    out_t(("xq", 0, m), 0, q_t)
                    if m < 3:
                        turned_hi(0, 5 + m)
                for m in range(KC):
                    out_t(("xq", 1, m), 0, q_t)
                for q in range(NQ - 1):
                    attend(q, lambda j: out_keys(q + 1, j) if j < KC else None)

                def between(j):
                    if j >= 6:
                        turned_hi(1, j - 6)
                attend(NQ - 1, between)
            with act.Else():
                act.sem_inc(sem["g_act"], 1)
                for c in range(KC):
                    first_weight(c)
                split_w("xv")
                act.wait_ge(sem["bias_in"], 32)
                split_w("xq")
                for t in range(NT):
                    turned_hi(0, t)
                for j in range(8):
                    m, half = j % 4, j // 4
                    act.wait_ge(sem["t_mm"], j + 1)
                    act.activation(q_t[:, m, half * 512:(half + 1) * 512], bank[j % 4][:], ACT.Identity,
                                   bias=bias_col[:, 0, m:m + 1]).then_inc(sem["t_ev"], 1)
                with act.Fori(0, NPAIR) as i:
                    p0 = i * PE_N + 1
                    for c in range(NCH):
                        act.wait_ge(sem["g_pe"], p0 + 3 * c + 1)
                        for m in range(KC):
                            ins = act.activation(g_k[:, m, :], bank[0][:, m * P:(m + 1) * P], ACT.Identity, bias=bias_col[:, 1, m:m + 1])
                        ins.then_inc(sem["g_act"], 1)
                    act.wait_ge(sem["g_dve"], i * DVE_N + 1 + NCH + 1)
                    act.activation(g_s[:], g_s[:], ACT.Exp, scale=SCALE).then_inc(sem["g_act"], 1)
                    for c in range(NCH):
                        act.wait_ge(sem["g_pe"], p0 + 3 * NCH + c + 1)
                        act.activation(g_pt[:, c, :], bank[5][:], ACT.Copy).then_inc(sem["g_act"], 1)
                    act.wait_ge(sem["g_pe"], p0 + PE_N)
                    for b in range(2):
                        for h in range(HG):
                            rows = slice(h * DH, (h + 1) * DH)
                            ins = act.activation(o_t[rows, :, bass.ds(i * 2 * S + b * S, S)],
                                                 bank[6 + b][rows, :].rearrange("p (g n) -> p g n", g=KC)[:, :, h * S:(h + 1) * S], ACT.Copy)
                    ins.then_inc(sem["g_act"], NCH)
                act.drain().then_inc(sem["t_ev"], 4 * NQ)
                act.wait_ge(sem["g_act"], NPAIR * ACT_N + 1)
                act.activation(xt_hi[:], o_t[:], ACT.Copy).then_inc(sem["o_hi"], NQ)
                split_w("xo")
                split_w("aq")
                turned_hi(1, 0)
                turned_hi(1, 1)
            act.end_ifs()
            turned_hi(1, 2)
            turned_hi(1, 3)
            split_w("ak")
            for m in range(KC):
                out_t(("aq", 0, m), 2, q_t)
            turned_hi(1, 4)
            turned_hi(1, 5)
            split_w("av")

            for m in range(KC):
                out_t(("ak", 0, m), 3, k_t)
                if m in (1, 2):
                    turned_hi(1, 5 + m)
            out_t(("aq", 1, 0), 2, q_t)

            def self_exponentials(k):
                act.wait_ge(sem["a_sub"], k + 1)
                ts = slice(4 * k, 4 * k + 4)
                act.activation(a_p[:, ts, :], a_s[:, ts, :], ACT.Exp, scale=ATTN_SCALE).then_inc(sem["a_exp"], 1)

            out_t(("aq", 1, 1), 2, q_t)
            self_exponentials(0)
            out_t(("aq", 1, 2), 2, q_t)
            out_t(("aq", 1, 3), 2, q_t)
            split_w("fq")
            for m in range(KC):
                out_t(("ak", 1, m), 3, k_t)
            split_w("fk")
            self_exponentials(1)
            for t in range(4):
                turned_hi(2, t)

            for m in range(KC):
                out_t(("fq", 0, m), 4, q_t)
                turned_hi(2, 4 + m)
            out_t(("fk", 0, 0), 5, k_t)
            split_w(("ex", 0))
            out_t(("fq", 1, 0), 4, q_t)
            act.wait_ge(sem["gate_v"], 1)
            act.activation(gate_x[:, :, 0:E], gate[:], ACT.Exp).then_inc(sem["gate_exp"], 1)
            for m in range(1, KC):
                out_t(("fq", 1, m), 4, q_t)
            split_w(("ex", 1))
            for m in range(1, KC):
                out_t(("fk", 0, m), 5, k_t)
            for m in range(KC):
                out_t(("fk", 1, m), 5, k_t)

            def block_keys(t):
                if t >= 2:
                    act.wait_ge(sem["f_mm"], t - 1)
                for h in range(HG):
                    ins = act.activation(k_bd[:, t % 2, :, :, h * S:(h + 1) * S],
                                         k_t[:, :, t * P:(t + 1) * P].rearrange("p g (b n) -> p b g n", b=4),
                                         ACT.Copy, scale=head_on[:, h:h + 1])
                ins.then_inc(sem["kbd_done"], 1)

            def weighted(t):
                act.wait_ge(sem[f"back_in{t}"], 32)
                act.wait_ge(sem["share_done"], 1)
                for k in range(2):
                    y = back[t // 2][:, t % 2 * 2 + k, :]
                    ins = act.activation(y, y, ACT.Copy, scale=share[:, k, t:t + 1])
                ins.then_inc(sem["y_scaled"], 1)

            def heads(routed):
                for t in range(NT):
                    act.wait_ge(sem["f_sub"], t + 1)
                    if t >= 1:
                        act.wait_ge(sem["f_tr"], t)
                    act.activation(f_p[:], f_s[:], ACT.Exp, scale=SCALE).then_inc(sem["f_exp"], 1)
                    if t + 2 < NT:
                        block_keys(t + 2)
                    if routed and 0 <= t - 2 < POOL_TILES:
                        weighted(t - 2)

            act.wait_ge(sem["crowded_set"], 1)
            crowded = act.value_load(crowded_i[0:1, 0:1], min_val=0, max_val=1)
            with act.If(crowded == 0):
                for i in range(NR):
                    act.wait_ge(sem["gt_mm"], i + 1)
                    if i >= 2:
                        act.wait_ge(sem["n_mm"], FFN_MM + i - 1)
                    act.activation(gt_hi[:, i % 2], bank[4 + i % 2][:].rearrange("p (c n) -> p c n", c=KC), ACT.Copy).then_inc(sem["gt_hi_done"], 1)
                    e, j = divmod(i - 4, EXPERT_TILES)
                    if i == 1:
                        split_w(("ex", 2))
                    if j == 0 and 0 <= e <= E - 3:
                        split_w(WEIGHTS[W_AT["ex", 0] + e + 3], EXPERT_TILES)
                    if i in (NR - 4, NR - 2):
                        act.wait_ge(sem["w_lo_done"], W_AT["ex", E - 1])
                        act.wait_ge(sem["place_mm"], 1)
                        block_keys((i + 4 - NR) // 2)
                heads(True)
            with act.Else():
                for e in range(2, E + 1):
                    split_w(WEIGHTS[W_AT["ex", 0] + e], NT)
                act.wait_ge(sem["w_lo_done"], W_AT["ex", E - 1])
                act.wait_ge(sem["place_mm"], 1)
                block_keys(0)
                block_keys(1)
                heads(False)
            act.end_ifs()

        @block.gpsimd
        def _(pool):
            pool.memset(power[:], -0.5).then_inc(sem["pow_set"], 1)
            pool.memset(warm[:], 0.0).then_inc(sem["warm_set"], 1)

            def inv_std(s, ts):
                n = s * NT + ts.stop
                pool.wait_ge(sem["aggr_done"], n)
                k = ts.stop - ts.start
                pool.tensor_scalar(rstd[:, 0, ts], aggr[:, ts, 1], EPS, None, ALU.add).then_inc(sem["eps_done"], k)
                pool.wait_ge(sem["eps_done"], n)
                pool.tensor_tensor(rstd[:, 1, ts], rstd[:, 0, ts], power[:].broadcast_to([P, k]), ALU.pow).then_inc(sem["rstd_done"], k)

            def tile_std(s, t):
                inv_std(s, slice(t, t + 1))

            def split_w(w):
                n = W_AT[w]
                pool.wait_ge(sem["w_hi_done"], n)
                k = W_SLOT[n]
                stage, _, _ = staged(n)
                pool.tensor_tensor(w_lo[:, k], stage[:], w_hi[:, k].bitcast(F32), ALU.subtract).then_inc(sem["w_lo_done"], 1)

            def split_c(q):
                pool.wait_ge(sem["c_hi_done"], q)
                pool.tensor_tensor(c_lo[:, q % 2], c_stage[:], c_hi[:, q % 2].bitcast(F32), ALU.subtract).then_inc(sem["c_lo_done"], 1)

            def split_next(q):
                split_c(q + 2) if q + 2 < NQ else split_w("xo" if q + 2 == NQ else "aq")

            def block_queries(slot, col):
                for b in range(2):
                    ins = pool.tensor_tensor(q_bd[:, slot, b].rearrange("p g (h n) -> p g h n", h=HG),
                                             q_t[:, :, col(b)].unsqueeze(2).broadcast_to([P, KC, HG, S]),
                                             head_on[:].unsqueeze(1).unsqueeze(3).broadcast_to([P, KC, HG, S]), ALU.mult)
                return ins

            def queries(n):
                if n >= 4 * NQ:
                    return
                if n >= 2:
                    pool.wait_ge(sem["s_mm"], n - 1)
                block_queries(n % 2, lambda b: slice(n * 2 * S + b * S, n * 2 * S + (b + 1) * S)).then_inc(sem["qbd_done"], 1)

            def normalised(n):
                pool.wait_ge(sem["s_inv"], n + 1)
                r = p_rows[:, n % 2, :].rearrange("p (e k) -> p e k", k=CK)
                pool.tensor_tensor(r, r, row_inv[:, n % 2, 0:8].unsqueeze(2).broadcast_to([P, 8, CK]), ALU.mult).then_inc(sem["p_done"], 1)

            def output_low(q):
                ts = slice(q * 256, (q + 1) * 256)
                pool.wait_ge(sem["o_hi"], q + 1)
                pool.tensor_tensor(xt_lo[:, :, ts], o_t[:, :, ts], xt_hi[:, :, ts].bitcast(F32), ALU.subtract).then_inc(sem["o_lo"], 1)

            pool.wait_ge(sem["pow_set"], 1)
            pool.wait_ge(sem["flag_done"], 1)
            general = pool.value_load(flag_i[0:1, 0:1], min_val=0, max_val=1)
            with pool.If(general == 0):
                for c in range(KC):
                    pool.wait_ge(sem["c0_hi_done"], c + 1)
                    pool.tensor_tensor(c_lo[:, 0, c, :], c_stage[:, c, :], c_hi[:, 0, c, :].bitcast(F32), ALU.subtract).then_inc(sem["c0_lo_done"], 1)
                split_w("xv")
                inv_std(0, slice(0, 4))
                inv_std(0, slice(4, NT))
                split_w("xq")
                split_c(1)
                pool.wait_ge(sem["bias_in"], 32)
                out_of_bank(pool, ("xq", 0, KC - 1))
                queries(0)
                queries(1)
                for q in range(NQ):
                    n = 4 * q
                    if q == NQ // 2:
                        out_of_bank(pool, ("xq", 1, KC - 1))
                    queries(n + 2)
                    queries(n + 3)
                    normalised(n)
                    normalised(n + 1)
                    split_next(q)
                    normalised(n + 2)
                    if q == NQ - 1:
                        tile_std(1, 0)
                        tile_std(1, 1)
                    normalised(n + 3)
                    if q == NQ - 1:
                        for t in range(2, 5):
                            tile_std(1, t)
                    if q == 1:
                        out_of_bank(pool, ("xq", 1, KC - 1))
                    queries(n + 4)
                    queries(n + 5)
                    output_low(q)
            with pool.Else():
                pool.sem_inc(sem["g_b"], 1)
                split_w("xv")
                inv_std(0, slice(0, 4))
                inv_std(0, slice(4, NT))
                split_w("xq")
                pool.wait_ge(sem["bias_in"], 32)
                pool.wait_ge(sem["t_ev"], 8)
                with pool.Fori(0, NPAIR) as i:
                    pool.wait_ge(sem["g_pe"], i * PE_N + 1)
                    block_queries(0, lambda b: bass.ds(i * 2 * S + b * S, S)).then_inc(sem["g_q"], 1)
                    for c in range(NCH):
                        pool.wait_ge(sem["g_c_in"], 16 * (i * NCH + c + 1))
                        if c >= 1:
                            pool.wait_ge(sem["g_pe"], i * PE_N + 1 + 3 * c)
                        pool.tensor_tensor(g_chi[:], g_ctx[:], ones[:].unsqueeze(1).broadcast_to([P, KC, P]), ALU.mult).then_inc(sem["g_hi"], 1)
                        pool.wait_ge(sem["g_hi"], i * NCH + c + 1)
                        pool.tensor_tensor(g_clo[:], g_ctx[:], g_chi[:].bitcast(F32), ALU.subtract).then_inc(sem["g_b"], 1)
                    pool.wait_ge(sem["s_inv"], i + 1)
                    for c in range(NCH):
                        r = g_s[:, c, :].rearrange("p (e k) -> p e k", k=CK)
                        ins = pool.tensor_tensor(r, r, row_inv[:, 0, 0:8].unsqueeze(2).broadcast_to([P, 8, CK]), ALU.mult)
                    ins.then_inc(sem["g_pool"], 1)
                pool.wait_ge(sem["o_hi"], NQ)
                pool.tensor_tensor(xt_lo[:], o_t[:], xt_hi[:].bitcast(F32), ALU.subtract).then_inc(sem["o_lo"], NQ)
                split_w("xo")
                split_w("aq")
                for t in range(5):
                    tile_std(1, t)
            pool.end_ifs()
            split_w("ak")
            tile_std(1, 5)
            pool.memset(a_pt[:], 0.0).then_inc(sem["pt_zeroed"], 1)
            tile_std(1, 6)
            tile_std(1, 7)
            split_w("av")
            pool.memset(wg_hi[:].bitcast(F32), 0.0).then_inc(sem["pt_zeroed"], 1)
            pool.memset(wg_lo[:].bitcast(F32), 0.0).then_inc(sem["pt_zeroed"], 1)
            pool.memset(all_on[:], 1.0).then_inc(sem["all_on_set"], 1)
            split_w("fq")
            split_w("fk")
            for t in range(NT):
                tile_std(2, t)
            split_w(("ex", 0))
            split_w(("ex", 1))

            def normalised_heads(t):
                pool.wait_ge(sem["f_inv"], t + 1)
                pool.tensor_tensor(f_p[:], f_p[:], row_inv[:, 0, :].unsqueeze(2).broadcast_to([P, H, S]), ALU.mult).then_inc(sem["f_norm"], 1)

            def add_experts(t):
                pool.wait_ge(sem["y_scaled"], t + 1)
                pool.wait_ge(sem["fa_added"], t + 1)
                xt, y = x[:, t, :], back[t // 2]
                pool.tensor_tensor(xt, xt, y[:, t % 2 * 2, :], ALU.add).then_inc(sem["y_first"], 1)
                pool.wait_ge(sem["y_first"], t + 1)
                pool.tensor_tensor(xt, xt, y[:, t % 2 * 2 + 1, :], ALU.add).then_inc(sem["x_final"], 1)

            def heads(routed):
                normalised_heads(0)
                normalised_heads(1)
                if routed:
                    pool.wait_ge(sem["n_mm"], FFN_MM + NR)
                    for j in range(4):
                        pool.wait_ge(sem[f"y_out{j}"], 16 * (NR // 4))
                for t in range(NT):
                    for u in (BACK_AT[t] if routed else ()):
                        for k in range(2):
                            pool.indirect_dma_start(back[u // 2][:, u % 2 * 2 + k, :], None, y_rows_d,
                                                    bass.IndirectOffsetOnAxis(ap=row_i[:, u, k:k + 1], axis=0),
                                                    bounds_check=NR * P - 1, oob_is_err=False).then_inc(sem[f"back_in{u}"], 16)
                    if t + 2 < NT:
                        normalised_heads(t + 2)
                    if routed and 0 <= t - 1 < POOL_TILES:
                        add_experts(t - 1)

            pool.wait_ge(sem["crowded_set"], 1)
            crowded = pool.value_load(crowded_i[0:1, 0:1], min_val=0, max_val=1)
            with pool.If(crowded == 0):
                pool.wait_ge(sem["row_token_done"], 1)
                for j in range(4):
                    pool.wait_ge(sem[f"xn_out{j}"], 32)

                def gather(i):
                    if i >= 4:
                        pool.wait_ge(sem["gt_mm"], i - 3)
                    pool.indirect_dma_start(g_rows[:, i % 4, :], None, xn_rows_d,
                                            bass.IndirectOffsetOnAxis(ap=row_token[:, i:i + 1], axis=0),
                                            bounds_check=TOK - 1, oob_is_err=False).then_inc(sem[f"g_in{i % 4}"], 16)
                for i in range(4):
                    gather(i)
                for i in range(4, NR + 6):
                    if i < NR:
                        gather(i)
                    e, j = divmod(i - 8, EXPERT_TILES)
                    if i == 5:
                        split_w(("ex", 2))
                    elif j == 0 and 0 <= e <= E - 3:
                        split_w(WEIGHTS[W_AT["ex", 0] + e + 3])
                heads(True)
            with pool.Else():
                split_w(("ex", 2))
                for e in range(3, E + 1):
                    split_w(WEIGHTS[W_AT["ex", 0] + e])
                heads(False)
            pool.end_ifs()

        @block.vector
        def _(dve):
            def statistics(s, t):
                if s == 0:
                    dve.wait_ge(sem[f"x_in{t // 4}"], 16 * 4)
                else:
                    dve.wait_ge(sem["x_acc"], ACC_AT[{1: "xo", 2: "at"}[s], t])
                n = s * NT + t
                dve.bn_stats(stats[:, t, :], x[:, t, :]).then_inc(sem["stats_done"], 1)
                dve.wait_ge(sem["stats_done"], n + 1)
                dve.bn_aggr(aggr[:, t, :], stats[:, t, :]).then_inc(sem["aggr_done"], 1)

            def scale(s, t):
                n = s * NT + t
                dve.wait_ge(sem["rstd_done"], n + 1)
                k = 4 if s == 2 else 2
                if t >= k:
                    dve.wait_ge(sem["tr_done"], n - k + 1)
                if t >= k and s == 2:
                    dve.wait_ge(sem[f"xn_out{t % 4}"], 16)
                dve.tensor_scalar(xn_rows(s, t), x[:, t, :], aggr[:, t, 0:1], rstd[:, 1, t:t + 1],
                                  ALU.subtract, ALU.mult).then_inc(sem["xn_done"], 1)

            def low(s, t):
                n = s * NT + t
                dve.wait_ge(sem["xt_hi_done"], n + 1)
                ts = slice(t * P, (t + 1) * P)
                dve.tensor_tensor(xt_lo[:, :, ts], bank[4 + t % 2][:].rearrange("p (c n) -> p c n", c=KC),
                                  xt_hi[:, :, ts].bitcast(F32), ALU.subtract).then_inc(sem["xt_lo_done"], 1)

            def out_n(group, dst, row):
                group_done(dve, group)
                dve.tensor_tensor(dst[:, group[-1], :], bank[BANK[group]][:], row, ALU.add).then_inc(sem["n_ev"], 1)

            acc = []

            def add_to_x(what, src, factor=None):
                i, t = len(acc), what[-1]
                assert ACC[i] == what
                before = [j + 1 for j in range(i) if ACC[j][-1] == t]
                if before:
                    dve.wait_ge(sem["x_acc"], before[-1])
                if factor is None:
                    ins = dve.tensor_tensor(x[:, t, :], src, x[:, t, :], ALU.add)
                else:
                    ins = dve.scalar_tensor_tensor(x[:, t, :], src, factor, x[:, t, :], ALU.mult, ALU.add)
                ins.then_inc(sem["x_acc"], 1)
                acc.append(what)

            def x_with_bias():
                for t in range(NT):
                    ins = dve.tensor_tensor(x[:, t, :], x[:, t, :], bias_x[:, 1, :], ALU.add)
                ins.then_inc(sem["xb_done"], 1)

            def projected(t):
                group_done(dve, ("xo", t))
                add_to_x(("xo", t), bank[BANK["xo", t]][:])

            dve.memset(ones[:], 1.0).then_inc(sem["ones_set"], 1)
            dve.wait_ge(sem["masknat_in"], 16)
            dve.tensor_scalar(mask_on[:], mask_nat[:, 0:TAIL], 0.0, None, ALU.not_equal).then_inc(sem["maskn_done"], 1)
            dve.wait_ge(sem["maskn_done"], 1)
            dve.wait_ge(sem["ones_set"], 1)
            dve.tensor_reduce(any_col[0:B, :], mask_on[:], AX.X, ALU.max).then_inc(sem["flag_sum"], 1)
            dve.wait_ge(sem["flag_mm"], 1)
            dve.tensor_scalar(flag_i[:], bank[6][0:1, 0:1], 1.0, None, ALU.min).then_inc(sem["flag_done"], 1)
            dve.wait_ge(sem["flag_done"], 1)
            general = dve.value_load(flag_i[0:1, 0:1], min_val=0, max_val=1)
            for c in range(KC):
                dve.wait_ge(sem["w0_hi_done"], c + 1)
                dve.tensor_tensor(w_lo[:, 0, c, :], w_stage[:, c, :], w_hi[:, 0, c, :].bitcast(F32), ALU.subtract).then_inc(sem["w0_lo_done"], 1)
            for t in range(4):
                statistics(0, t)
            scale(0, 0)
            scale(0, 1)
            for t in range(4, NT):
                statistics(0, t)
            dve.wait_ge(sem["biasx_in"], 16)

            def nan_for_no_key(n, first):
                dve.wait_ge(sem["maskn_done"], first)
                dve.tensor_scalar(nan_b[:, 1, 0:n], nan_b[:, 0, 0:n], 0.0, None, ALU.is_equal).then_inc(sem["maskn_done"], 1)
                dve.wait_ge(sem["maskn_done"], first + 1)
                dve.reciprocal(nan_b[:, 2, 0:n], nan_b[:, 1, 0:n]).then_inc(sem["maskn_done"], 1)
                dve.wait_ge(sem["maskn_done"], first + 2)
                dve.tensor_tensor(nan_b[:, 0, 0:n], nan_b[:, 1, 0:n], nan_b[:, 2, 0:n], ALU.mult).then_inc(sem["maskn_done"], 1)
                dve.wait_ge(sem["maskn_done"], first + 3)
                dve.tensor_scalar(nan_b[:, 1, 0:n], nan_b[:, 0, 0:n], -1.0, None, ALU.add).then_inc(sem["maskn_done"], 1)
                dve.wait_ge(sem["maskn_done"], first + 4)

            with dve.If(general == 0):
                def softmax_head(n):
                    srow = s_rows[:, n % 2, :]
                    dve.wait_ge(sem["s_mm"], n + 1)
                    if n >= 2:
                        dve.wait_ge(sem["exp_done"], n - 1)
                    dve.tensor_tensor(srow.rearrange("p (g k) -> p g k", g=KC), bank[4 + n % 2][:].rearrange("p (g k) -> p g k", g=KC),
                                      m_bias[:, n * P:(n + 1) * P].unsqueeze(1).broadcast_to([P, KC, P]), ALU.add).then_inc(sem["s_add"], 1)
                    dve.wait_ge(sem["s_add"], n + 1)
                    r = srow.rearrange("p (e k) -> p e k", k=CK)
                    dve.tensor_reduce(row_max[:, n % 2, 0:8], r, AX.X, ALU.max).then_inc(sem["s_max"], 1)
                    dve.wait_ge(sem["s_max"], n + 1)
                    dve.tensor_tensor(r, r, row_max[:, n % 2, 0:8].unsqueeze(2).broadcast_to([P, 8, CK]), ALU.subtract).then_inc(sem["s_sub"], 1)

                def softmax_sum(n):
                    dve.wait_ge(sem["exp_done"], n + 1)
                    if n >= 2:
                        dve.wait_ge(sem["p_done"], n - 1)
                    r = p_rows[:, n % 2, :].rearrange("p (e k) -> p e k", k=CK)
                    dve.tensor_reduce(row_sum[:, n % 2, 0:8], r, AX.X, ALU.add).then_inc(sem["s_sum"], 1)
                    dve.wait_ge(sem["s_sum"], n + 1)
                    dve.reciprocal(row_inv[:, n % 2, 0:8], row_sum[:, n % 2, 0:8]).then_inc(sem["s_inv"], 1)

                def out_values(q, p):
                    if q >= 1:
                        dve.wait_ge(sem["o_mm"], 4 * (q - 1) + p + 1)
                    group_done(dve, ("xv", q, p))
                    dve.tensor_tensor(vq_n[:, p, :], bank[BANK["xv", q, p]][:], bias_x[:, 0, :], ALU.add).then_inc(sem["n_ev"], 1)

                def attend(q, between):
                    n = 4 * q
                    softmax_head(n)
                    softmax_head(n + 1)
                    between(0)
                    softmax_sum(n)
                    softmax_head(n + 2)
                    between(1)
                    softmax_sum(n + 1)
                    softmax_head(n + 3)
                    between(2)
                    softmax_sum(n + 2)
                    between(3)
                    softmax_sum(n + 3)
                    take_out(dve, n, 1)
                    between(4)
                    take_out(dve, n + 1, 1)
                    between(5)
                    take_out(dve, n + 2, 1)
                    between(6)
                    take_out(dve, n + 3, 1)
                    between(7)

                for t in range(4):
                    low(0, t)
                    scale(0, t + 2)
                    if t >= 2:
                        out_values(0, t - 2)
                out_values(0, 2)
                out_values(0, 3)
                for t in range(4, NT):
                    low(0, t)
                    if t + 2 < NT:
                        scale(0, t + 2)
                dve.wait_ge(sem["mask_in"], 16)
                dve.tensor_scalar(m_bias[:], mask_i[:], 0.0, MASKED, ALU.is_equal, ALU.mult).then_inc(sem["mbias_done"], 1)
                dve.wait_ge(sem["mbias_done"], 1)
                m3 = m_bias[:].rearrange("p (b k) -> p b k", k=CK)
                dve.tensor_reduce(nan_b[:, 0, :], m3, AX.X, ALU.max).then_inc(sem["maskn_done"], 1)
                nan_for_no_key(B, 2)
                dve.tensor_tensor(m3, m3, nan_b[:, 1, :].unsqueeze(2).broadcast_to([P, B, CK]), ALU.add).then_inc(sem["mbias_done"], 1)
                dve.wait_ge(sem["mbias_done"], 2)
                for q in range(NQ - 1):
                    attend(q, lambda j: out_values(q + 1, j - KC) if j >= KC else None)
                    if q == 0:
                        x_with_bias()

                def between(j):
                    if j < 5:
                        if j == 0:
                            dve.wait_ge(sem["xb_done"], 1)
                        projected(j)
                        statistics(1, j)
                        if j == 4:
                            scale(1, 0)
                            scale(1, 1)
                    elif j >= 6:
                        low(1, j - 6)
                        scale(1, j - 4)
                attend(NQ - 1, between)
            with dve.Else():
                dve.sem_inc(sem["g_dve"], 1)
                for t in range(NT):
                    low(0, t)
                    if t + 2 < NT:
                        scale(0, t + 2)
                with dve.Fori(0, NPAIR) as i:
                    p0 = i * PE_N + 1
                    dve.wait_ge(sem["g_m_in"], 16 * (i + 1))
                    dve.tensor_scalar(g_bias[:], g_mask[:], 0.0, MASKED, ALU.is_equal, ALU.mult).then_inc(sem["mbias_done"], 1)
                    dve.wait_ge(sem["mbias_done"], i * 2 + 1)
                    for b in range(2):
                        dve.tensor_reduce(nan_b[:, 0, b:b + 1], g_bias[:, :, b * CK:(b + 1) * CK], AX.XY, ALU.max).then_inc(sem["maskn_done"], 1)
                    nan_for_no_key(2, i * 6 + 3)
                    for b in range(2):
                        gb = g_bias[:, :, b * CK:(b + 1) * CK]
                        ins = dve.tensor_scalar(gb, gb, nan_b[:, 1, b:b + 1], None, ALU.add)
                    ins.then_inc(sem["mbias_done"], 1)
                    dve.wait_ge(sem["mbias_done"], i * 2 + 2)
                    dve.wait_ge(sem["g_act"], i * ACT_N + 1)
                    for c in range(NCH):
                        dve.wait_ge(sem["g_pe"], p0 + 3 * c + 2)
                        dve.tensor_tensor(g_v[:, c, :], bank[1][:], bias_x[:, 0, :], ALU.add).then_inc(sem["s_add"], 1)
                        dve.wait_ge(sem["g_pe"], p0 + 3 * c + 3)
                        dve.tensor_tensor(g_s[:, c, :].rearrange("p (g k) -> p g k", g=KC), bank[4][:].rearrange("p (g k) -> p g k", g=KC),
                                          g_bias[:, c, :].unsqueeze(1).broadcast_to([P, KC, P]), ALU.add).then_inc(sem["g_dve"], 1)
                    dve.wait_ge(sem["g_dve"], i * DVE_N + 1 + NCH)
                    r = g_s[:].rearrange("p c (e k) -> p e c k", k=CK)
                    dve.tensor_reduce(row_max[:, 0, 0:8], r, AX.XY, ALU.max).then_inc(sem["s_max"], 1)
                    dve.wait_ge(sem["s_max"], i + 1)
                    for c in range(NCH):
                        rc = g_s[:, c, :].rearrange("p (e k) -> p e k", k=CK)
                        ins = dve.tensor_tensor(rc, rc, row_max[:, 0, 0:8].unsqueeze(2).broadcast_to([P, 8, CK]), ALU.subtract)
                    ins.then_inc(sem["g_dve"], 1)
                    dve.wait_ge(sem["g_act"], i * ACT_N + 1 + NCH + 1)
                    dve.tensor_reduce(row_sum[:, 0, 0:8], r, AX.XY, ALU.add).then_inc(sem["s_sum"], 1)
                    dve.wait_ge(sem["s_sum"], i + 1)
                    dve.reciprocal(row_inv[:, 0, 0:8], row_sum[:, 0, 0:8]).then_inc(sem["s_inv"], 1)
                dve.drain().then_inc(sem["n_ev"], 4 * NQ)
                x_with_bias()
                dve.wait_ge(sem["xb_done"], 1)
                del acc[:]
                for t in range(5):
                    projected(t)
                    statistics(1, t)
                scale(1, 0)
                scale(1, 1)
                low(1, 0)
                scale(1, 2)
                low(1, 1)
                scale(1, 3)
            dve.end_ifs()
            low(1, 2)
            scale(1, 4)
            low(1, 3)
            projected(5)
            statistics(1, 5)
            scale(1, 5)
            projected(6)
            statistics(1, 6)
            projected(7)
            statistics(1, 7)
            low(1, 4)
            scale(1, 6)
            low(1, 5)
            scale(1, 7)
            low(1, 6)
            low(1, 7)

            def self_softmax_head(k):
                ts = slice(4 * k, 4 * k + 4)
                dve.wait_ge(sem["a_mm"], k + 1)
                for b in range(4):
                    rows = slice(b * S, (b + 1) * S)
                    ins = dve.tensor_copy(a_s[rows, ts, :], bank[6 + k][rows, :].rearrange("p (t n) -> p t n", t=4)[:, :, b * S:(b + 1) * S])
                ins.then_inc(sem["a_ext"], 1)
                dve.wait_ge(sem["a_ext"], k + 1)
                dve.tensor_reduce(row_max[:, 0, ts], a_s[:, ts, :], AX.X, ALU.max).then_inc(sem["a_max"], 1)
                dve.wait_ge(sem["a_max"], k + 1)
                dve.tensor_tensor(a_s[:, ts, :], a_s[:, ts, :], row_max[:, 0, ts].unsqueeze(2).broadcast_to([P, 4, S]), ALU.subtract).then_inc(sem["a_sub"], 1)

            def self_softmax_sum(k):
                ts = slice(4 * k, 4 * k + 4)
                dve.wait_ge(sem["a_exp"], k + 1)
                dve.tensor_reduce(row_sum[:, 0, ts], a_p[:, ts, :], AX.X, ALU.add).then_inc(sem["a_sum"], 1)
                dve.wait_ge(sem["a_sum"], k + 1)
                dve.reciprocal(row_inv[:, 0, ts], row_sum[:, 0, ts]).then_inc(sem["a_inv"], 1)
                dve.wait_ge(sem["a_inv"], k + 1)
                dve.tensor_tensor(a_p[:, ts, :], a_p[:, ts, :], row_inv[:, 0, ts].unsqueeze(2).broadcast_to([P, 4, S]), ALU.mult).then_inc(sem["a_norm"], 1)
                dve.wait_ge(sem["a_norm"], k + 1)
                dve.wait_ge(sem["pt_zeroed"], 1)
                for b in range(4):
                    rows = slice(b * S, (b + 1) * S)
                    dve.transpose(a_pt[rows, ts, b * S:(b + 1) * S], a_p[rows, ts, :]).then_inc(sem["a_tr"], 1)

            self_softmax_head(0)
            self_softmax_sum(0)
            dve.wait_ge(sem["gate_in"], 32)
            dve.wait_ge(sem["pt_zeroed"], 3)
            dve.tensor_copy(wg_hi[:, :, 0:E], g_stage[:]).then_inc(sem["wg_split"], 1)
            dve.wait_ge(sem["wg_split"], 1)
            dve.tensor_tensor(wg_lo[:, :, 0:E], g_stage[:], wg_hi[:, :, 0:E].bitcast(F32), ALU.subtract).then_inc(sem["wg_split"], 1)
            dve.memset(gate_x[:], -1.0).then_inc(sem["gx_set"], 1)
            dve.memset(top2[:], -1.0).then_inc(sem["gx_set"], 1)
            dve.wait_ge(sem["biasf_in"], 16)
            out_n(("av", 0), v_n, bias_f[:, 0, :])
            self_softmax_head(1)
            out_n(("av", 1), v_n, bias_f[:, 0, :])
            self_softmax_sum(1)

            def self_added(t):
                dve.wait_ge(sem["av_mm"], t + 1)
                add_to_x(("at", t), bank[6 + t % 2][:])

            for t in range(2, NT + 4):
                if t < NT:
                    out_n(("av", t), v_n, bias_f[:, 0, :])
                if 3 <= t < NT + 3:
                    self_added(t - 3)
                if 6 <= t < 10:
                    low(2, t - 6)
                if 3 <= t < NT + 3:
                    statistics(2, t - 3)
                if t >= 4:
                    scale(2, t - 4)
            for t in range(4, NT):
                low(2, t)

            step = []

            def then_wait(ins):
                step.append(1)
                ins.then_inc(sem["gate_step"], 1)
                dve.wait_ge(sem["gate_step"], len(step))

            dve.wait_ge(sem["gate_mm"], 1)
            for k in range(2):
                ins = dve.tensor_scalar(gate_t[:, k * 512:(k + 1) * 512], bank[6 + k][0:E, :], b_gate[:, 0:1], None, ALU.add)
            ins.then_inc(sem["gate_ev"], 1)
            dve.wait_ge(sem["gatet_mm"], 1)
            lg = bank[6][:, 0:NT * E].rearrange("p (t e) -> p t e", e=E)
            then_wait(dve.tensor_reduce(row_max[:, 0, 0:NT], lg, AX.X, ALU.max))
            dve.wait_ge(sem["gx_set"], 2)
            dve.tensor_tensor(gate[:], lg, row_max[:, 0, 0:NT].unsqueeze(2).broadcast_to([P, NT, E]), ALU.subtract).then_inc(sem["gate_v"], 1)
            dve.wait_ge(sem["gate_exp"], 1)
            gx = gate_x[:, :, 0:E]
            then_wait(dve.tensor_reduce(row_sum[:, 0, 0:NT], gx, AX.X, ALU.add))
            then_wait(dve.reciprocal(row_inv[:, 0, 0:NT], row_sum[:, 0, 0:NT]))
            then_wait(dve.tensor_tensor(gx, gx, row_inv[:, 0, 0:NT].unsqueeze(2).broadcast_to([P, NT, E]), ALU.mult))
            for t in range(NT):
                ins = dve.max(top[:, t, :], gate_x[:, t, 0:E])
            then_wait(ins)
            then_wait(dve.tensor_copy(top2[:, :, 0:2], top[:, :, 0:2]))
            for t in range(NT):
                ins = dve.match_replace(gate_r[:, t, :], top2[:, t, :], gate_x[:, t, :], -2.0)
            then_wait(ins)
            then_wait(dve.tensor_scalar(sel[:], gate_r[:, :, 0:E], -1.5, None, ALU.is_lt))
            dve.tensor_tensor(comb[:], gx, sel[:], ALU.mult).then_inc(sem["comb_done"], 1)

            last = sel
            for step_of, dst in ((1, sums[0]), (2, sums[1]), (4, None)):
                dst = ahead[:, 1:NT + 1, :] if dst is None else dst[:]
                dve.tensor_copy(dst[:, 0:step_of, :], last[:, 0:step_of, :])
                then_wait(dve.tensor_tensor(dst[:, step_of:NT, :], last[:, step_of:NT, :], last[:, 0:NT - step_of, :], ALU.add))
                last = dst
            dve.memset(ahead[:, 0:1, :], 0.0).then_inc(sem["sel_done"], 1)

            dve.wait_ge(sem["row_mm"], 1)
            then_wait(dve.tensor_reduce(most[:], bank[6][0:1, 2 * NT * E:(2 * NT + 1) * E], AX.X, ALU.max))
            dve.tensor_scalar(crowded_i[:], most[:], float(CAPACITY), None, ALU.is_gt).then_inc(sem["crowded_set"], 1)
            then_wait(dve.tensor_tensor(row_e[:], bank[6][:, NT * E:2 * NT * E].rearrange("p (t e) -> p t e", e=E), first_row[:], ALU.add))
            dve.scalar_tensor_tensor(from_far[:], row_e[:], -float(FAR), sel[:], ALU.add, ALU.mult)
            then_wait(dve.tensor_tensor(or_zero[:], row_e[:], sel[:], ALU.mult))
            dve.tensor_reduce(row_f[:, :, 0], from_far[:], AX.X, ALU.min)
            then_wait(dve.tensor_reduce(row_f[:, :, 1], or_zero[:], AX.X, ALU.max))
            dve.tensor_scalar(row_i[:, :, 0], row_f[:, :, 0], float(FAR), float(NR * P - 1), ALU.add, ALU.min)
            then_wait(dve.tensor_scalar(row_i[:, :, 1], row_f[:, :, 1], float(NR * P - 1), None, ALU.min))
            dve.tensor_scalar(low_i[:], row_i[:], P - 1, None, ALU.bitwise_and)
            then_wait(dve.tensor_scalar(high_i[:], row_i[:], P.bit_length() - 1, None, ALU.arith_shift_right))
            dve.tensor_copy(low_f[:], low_i[:])
            then_wait(dve.tensor_copy(high_f[:], high_i[:]))

            def over(values, n):
                return values.rearrange("p t k -> p (t k)").unsqueeze(2).broadcast_to([P, NT * 2, n])

            then_wait(dve.tensor_tensor(at_high[:].rearrange("p t k r -> p (t k) r"), count[:, 0:NR].unsqueeze(1).broadcast_to([P, NT * 2, NR]),
                                        over(high_f[:], NR), ALU.is_equal))
            dve.tensor_tensor(at_high[:].rearrange("p t k r -> p t (k r)"), at_high[:].rearrange("p t k r -> p t (k r)"),
                              token[:].unsqueeze(2).broadcast_to([P, NT, 2 * NR]), ALU.mult).then_inc(sem["placed_done"], 1)
            dve.tensor_tensor(at_low[:].rearrange("p t k r -> p (t k) r"), count[:].unsqueeze(1).broadcast_to([P, NT * 2, P]),
                              over(low_f[:], P), ALU.is_equal).then_inc(sem["placed_done"], 1)
            dve.wait_ge(sem["comb_done"], 1)
            for k, rows_k in enumerate((from_far, or_zero)):
                ins = dve.tensor_tensor(part[:, k], rows_k[:], row_f[:, :, k].unsqueeze(2).broadcast_to([P, NT, E]), ALU.is_equal)
            then_wait(ins)
            then_wait(dve.tensor_tensor(part[:], part[:], comb[:].unsqueeze(1).broadcast_to([P, 2, NT, E]), ALU.mult))
            dve.tensor_reduce(share[:], part[:], AX.X, ALU.add).then_inc(sem["share_done"], 1)
            dve.wait_ge(sem["place_mm"], 1)
            dve.tensor_copy(row_token[:], bank[7][:, 0:NR]).then_inc(sem["row_token_done"], 1)

            def heads_softmax_head(t):
                dve.wait_ge(sem["f_mm"], t + 1)
                s3 = bank[6 + t % 2][:].rearrange("p (e k) -> p e k", k=S)
                dve.tensor_reduce(row_max[:, 0, :], s3, AX.X, ALU.max).then_inc(sem["f_max"], 1)
                dve.wait_ge(sem["f_max"], t + 1)
                if t >= 1:
                    dve.wait_ge(sem["f_exp"], t)
                dve.tensor_tensor(f_s[:], s3, row_max[:, 0, :].unsqueeze(2).broadcast_to([P, H, S]), ALU.subtract).then_inc(sem["f_sub"], 1)

            def heads_softmax_sum(t):
                dve.wait_ge(sem["f_exp"], t + 1)
                dve.tensor_reduce(row_sum[:, 0, :], f_p[:], AX.X, ALU.add).then_inc(sem["f_sum"], 1)
                dve.wait_ge(sem["f_sum"], t + 1)
                if t >= 1:
                    dve.wait_ge(sem["f_norm"], t)
                dve.reciprocal(row_inv[:, 0, :], row_sum[:, 0, :]).then_inc(sem["f_inv"], 1)

            def heads_turned(t):
                dve.wait_ge(sem["f_norm"], t + 1)
                if t >= 2:
                    dve.wait_ge(sem["fv_mm"], t - 1)
                dve.transpose(f_pt[t % 2][:], f_p[:]).then_inc(sem["f_tr"], 1)

            def expert_bias(e, out, i):
                dve.wait_ge(sem["n_mm"], FFN_MM + i + 1)
                dve.wait_ge(sem[f"be_in{e % 2}"], 16 * (e // 2 + 1))
                dve.tensor_tensor(out, bank[i % 4][:], b_exp[:, e % 2, :], ALU.add).then_inc(sem["y_ev"], 1)

            def routed_out(i):
                if i >= 4:
                    dve.wait_ge(sem[f"y_out{i % 4}"], 16 * (i // 4))
                else:
                    dve.wait_ge(sem[f"xn_out{i}"], 32)
                expert_bias(i // EXPERT_TILES, y_rows[:, i % 4, :], i)

            def experts_added(t):
                if t < NT - 1:
                    dve.wait_ge(sem["fa_added"], t + 1)
                dve.wait_ge(sem[f"back_in{t}"], 32)
                xt, y = x[:, t, :], back[t // 2]
                dve.scalar_tensor_tensor(xt, y[:, t % 2 * 2, :], share[:, 0, t:t + 1], xt, ALU.mult, ALU.add).then_inc(sem["y_added"], 1)
                dve.wait_ge(sem["y_added"], t + 1 - POOL_TILES)
                dve.scalar_tensor_tensor(xt, y[:, t % 2 * 2 + 1, :], share[:, 1, t:t + 1], xt, ALU.mult,
                                         ALU.add).then_inc(sem["x_last" if t < NT - 1 else "y_added"], 1)

            def heads(n, routed):
                def values_out(t):
                    dve.wait_ge(sem["n_mm"], FFN_MM + n + t + 1)
                    dve.tensor_tensor(v_n[:, t, :], bank[t % 4][:], bias_f[:, 1, :], ALU.add).then_inc(sem["v_ev"], 1)

                values_out(0)
                heads_turned(1)
                for t in range(NT):
                    if t + 1 < NT:
                        values_out(t + 1)
                    if t + 2 < NT:
                        heads_softmax_head(t + 2)
                        heads_softmax_sum(t + 2)
                    for u in (ADDED_AT.get(t, ()) if routed else ()):
                        experts_added(u)
                    dve.wait_ge(sem["fv_mm"], t + 1)
                    last = routed and t == NT - 1
                    if last:
                        dve.wait_ge(sem["y_added"], NT - POOL_TILES + 1)
                    dve.tensor_tensor(x[:, t, :], bank[4 + t % 2][:], x[:, t, :], ALU.add).then_inc(sem["x_last" if last else "fa_added"], 1)
                    if t + 2 < NT:
                        heads_turned(t + 2)
                    if not routed:
                        dve.wait_ge(sem["fa_added"], t + 1)
                        dve.sem_inc(sem["x_final" if t < POOL_TILES else "x_last"], 1)

            dve.wait_ge(sem["crowded_set"], 1)
            crowded = dve.value_load(crowded_i[0:1, 0:1], min_val=0, max_val=1)
            dve.wait_ge(sem["share_done"], 1)
            with dve.If(crowded == 0):
                for i in range(NR):
                    dve.wait_ge(sem["gt_hi_done"], i + 1)
                    dve.tensor_tensor(gt_lo[:, i % 2], bank[4 + i % 2][:].rearrange("p (c n) -> p c n", c=KC),
                                      gt_hi[:, i % 2].bitcast(F32), ALU.subtract).then_inc(sem["gt_lo_done"], 1)
                    if i == NR - 1:
                        heads_softmax_sum(0)
                    if i >= 2:
                        routed_out(i - 2)
                    if i == NR - 2:
                        heads_softmax_head(0)
                heads_turned(0)
                routed_out(NR - 2)
                heads_softmax_head(1)
                routed_out(NR - 1)
                heads_softmax_sum(1)
                heads(NR, True)
            with dve.Else():
                for j in range(4):
                    dve.wait_ge(sem[f"xn_out{j}"], 32)
                for i in range(E * NT):
                    e, t = divmod(i, NT)
                    expert_bias(e, y_rows[:, i % 2, :], i)
                    dve.wait_ge(sem["y_ev"], i + 1)
                    if e >= 1:
                        dve.wait_ge(sem["y_added"], i - NT + 1)
                    dve.scalar_tensor_tensor(x[:, t, :], y_rows[:, i % 2, :], comb[:, t, e:e + 1], x[:, t, :], ALU.mult, ALU.add).then_inc(sem["y_added"], 1)
                dve.wait_ge(sem["y_added"], E * NT)
                heads_softmax_head(0)
                heads_softmax_sum(0)
                heads_turned(0)
                heads_softmax_head(1)
                heads_softmax_sum(1)
                heads(E * NT, False)
            dve.end_ifs()


def _kernel_arrays(x, ctx_1024, mask, Wxq, bxq, Wxk, bxk, Wxv, bxv, Wxo, bxo, Waq, baq, Wak, bak, Wav, bav,
                   W_qkv, b_qkv, W_gate, b_gate, W_experts, b_experts):
    def rows(w):
        return w.reshape(KC, P, -1).transpose(1, 0, 2)

    ws = [w.T for w in (Wxk, Wxv, Wxq, Wxo, Waq, Wak, Wav)] + [W_qkv[:, :D], W_qkv[:, D:2 * D]] + list(W_experts) + [W_qkv[:, 2 * D:]]
    slots = np.concatenate([np.arange(1, PAD + 1), np.arange(SK)])
    chunks = ctx_1024[:, slots].reshape(NPAIR, 2, NCH, CK, KC, P).transpose(0, 2, 5, 4, 1, 3)
    m = np.concatenate([np.zeros((B, PAD), mask.dtype), mask.reshape(B, SK)], axis=1)
    cols = np.stack([bxq, bxk, baq, bak, b_qkv[0:D], b_qkv[D:2 * D]])
    c = np.ascontiguousarray
    return {
        "x_in_dram": c(x.reshape(TOK, D)),
        "ctx_tail_dram": c(ctx_1024[:, TAIL:].reshape(NQ, 8 * CK, KC, P).transpose(0, 3, 2, 1)),
        "ctx_all_dram": c(chunks).reshape(NPAIR * NCH, P, KC, P),
        "mask_dram": c(mask.reshape(B, SK)),
        "mask_tail_dram": c(mask.reshape(B, SK)[:, TAIL:]).reshape(1, B * CK),
        "mask_all_dram": c(m.reshape(NPAIR, 2, NCH, CK).transpose(0, 2, 1, 3)).reshape(NPAIR, NCH * P),
        "weights_dram": c(np.stack([rows(w) for w in ws])),
        "bias_col_dram": c(cols.reshape(6, KC, P).transpose(2, 0, 1)),
        "bias_row_dram": c(np.stack([bxv, bxo, bav, b_qkv[2 * D:]]))[None],
        "w_gate_dram": c(rows(W_gate)),
        "b_gate_dram": c(b_gate[:, None]),
        "b_experts_dram": c(b_experts),
        "ident_dram": np.eye(P, dtype=np.float32),
        "head_on_dram": np.repeat(np.eye(HG, dtype=np.float32), DH, axis=0),
        "before_dram": np.triu(np.ones((P, P), np.float32), 1),
        "count_dram": np.arange(P, dtype=np.float32)[None],
        "first_row_dram": np.tile(np.arange(E, dtype=np.float32) * CAPACITY, (1, NT, 1)),
        "token_dram": c(np.arange(TOK, dtype=np.float32).reshape(NT, P).T),
    }


def kernel(**inputs):
    import concourse.bacc as bacc
    from concourse.bass_utils import run_bass_kernel_spmd

    nc = bacc.Bacc("TRN2", target_bir_lowering=False, num_devices=1)
    names = ["x", "ctx_1024", "mask_Bx1xS2_ik0"] + [f"L0_xattn_{n}" for n in "Wq bq Wk bk Wv bv Wo bo".split()] \
        + [f"L0_attn_{n}" for n in "Wq bq Wk bk Wv bv".split()] \
        + [f"L0_ffn_{n}" for n in "W_qkv b_qkv W_gate b_gate W_experts b_experts".split()]
    arrays = _kernel_arrays(*[np.asarray(inputs[n]) for n in names])
    args = [nc.dram_tensor(n, a.shape, mybir.dt.from_np(a.dtype), kind="ExternalInput").ap() for n, a in arrays.items()]
    out = nc.dram_tensor("out_dram", (TOK, D), F32, kind="ExternalOutput").ap()
    xn_rows = nc.dram_tensor("xn_rows_dram", (TOK, D), F32, kind="Internal").ap()
    y_rows = nc.dram_tensor("y_rows_dram", (NR * P, D), F32, kind="Internal").ap()
    perceiver_kernel(nc, *args, xn_rows, y_rows, out)
    r = run_bass_kernel_spmd(nc, [arrays], core_ids=[0])
    return r.results[0]["out_dram"].reshape(B, S, D)
```
